# Optimizing a Trainium2 kernel written in Bass

```python
import numpy as np
import jax
import jax.numpy as jnp

def _softmax(x, axis=-1):
    return jax.nn.softmax(x, axis=axis)

def _gelu(x):
    return jax.nn.gelu(x, approximate=True)

def _silu(x):
    return jax.nn.silu(x)

def _sigmoid(x):
    return jax.nn.sigmoid(x)

def _layernorm(x, axis=-1, eps=1e-05):
    m = jnp.mean(x, axis=axis, keepdims=True)
    v = jnp.var(x, axis=axis, keepdims=True)
    return (x - m) / jnp.sqrt(v + eps)

def _scatter_add(tgt, idx, src, axis=0):
    return tgt.at[idx].add(src)

def _segment_sum(src, seg, n):
    return jax.ops.segment_sum(src, seg, n)
kernel_name = 'mk_sandwich_d2_jaxref_r8_48b1c0'

def setup_inputs(seed: int=0):
    np.random.seed(seed)
    _w = jnp.asarray

    def _L0_attn_setup():
        import jax, jax.numpy as jnp
        import numpy as np
        DIM = 128
        HID = 512
        NUM_HEADS = 4
        WINDOW = 64
        NUM_PM = 64
        NEG = -1e+30

        def _swa(x_in, wq, wk, wv, wo):
            B, S, D = x_in.shape
            h, dh = (NUM_HEADS, D // NUM_HEADS)
            q = (x_in @ wq.T).reshape(B, S, h, dh).transpose(0, 2, 1, 3)
            k = (x_in @ wk.T).reshape(B, S, h, dh).transpose(0, 2, 1, 3)
            v = (x_in @ wv.T).reshape(B, S, h, dh).transpose(0, 2, 1, 3)
            i = jnp.arange(S)[:, None]
            j = jnp.arange(S)[None, :]
            mask = (j <= i) & (j > i - WINDOW)
            logits = jnp.einsum('bhqd,bhkd->bhqk', q, k) / np.sqrt(dh).astype(np.float32)
            logits = jnp.where(mask, logits, NEG)
            attn = jax.nn.softmax(logits, axis=-1)
            out = jnp.einsum('bhqk,bhkd->bhqd', attn, v)
            out = out.transpose(0, 2, 1, 3).reshape(B, S, D)
            return out @ wo.T

        def _mlp(w1, b1, w2, b2, x):
            return jax.nn.silu(x @ w1.T + b1) @ w2.T + b2
        key = jax.random.key(seed)
        ks = jax.random.split(key, 12)
        B, S = (2, 256)
        sc = 0.02
        n = lambda k, shape, s=sc: jax.random.normal(k, shape, jnp.float32) * s
        return {'x': n(ks[0], (B, S, DIM), 1.0), 'mem': n(ks[1], (NUM_PM, DIM), 1.0), 'wq': n(ks[2], (DIM, DIM)), 'wk': n(ks[3], (DIM, DIM)), 'wv': n(ks[4], (DIM, DIM)), 'wo': n(ks[5], (DIM, DIM)), 'w1': n(ks[6], (HID, DIM)), 'b1': jnp.zeros((HID,), jnp.float32), 'w2': n(ks[7], (DIM, HID)), 'b2': jnp.zeros((DIM,), jnp.float32), 'lin1': n(ks[8], (DIM, DIM)), 'lin2': n(ks[9], (DIM, DIM)), 'alpha': jnp.float32(0.0001), 'theta': jnp.float32(0.0001)}
    _L0_attn_in = _L0_attn_setup()

    def _L0_ffn_setup():
        import jax, jax.numpy as jnp
        import numpy as np
        TOP_K = 2
        key = jax.random.key(seed)
        ks = jax.random.split(key, 5)
        B, S, H, I, E = (2, 256, 128, 352, 8)
        x = jax.random.normal(ks[0], (B, S, H), dtype=jnp.float32)
        router_w = jax.random.normal(ks[1], (E, H), dtype=jnp.float32) * (1.0 / np.sqrt(H))
        Wg = jax.random.normal(ks[2], (E, I, H), dtype=jnp.float32) * (1.0 / np.sqrt(H))
        Wu = jax.random.normal(ks[3], (E, I, H), dtype=jnp.float32) * (1.0 / np.sqrt(H))
        Wd = jax.random.normal(ks[4], (E, H, I), dtype=jnp.float32) * (1.0 / np.sqrt(I))
        return {'x': x, 'router_w': router_w, 'Wg': Wg, 'Wu': Wu, 'Wd': Wd}
    _L0_ffn_in = _L0_ffn_setup()

    def _L1_attn_setup():
        import jax, jax.numpy as jnp
        import numpy as np
        NUM_HEAD = 16
        D_Q = 64
        D_KV = 64
        ROPE_BASE = 10000.0

        def _cos_sin(seq_len, dim):
            pos = jnp.arange(seq_len, dtype=jnp.float32)[:, None]
            ids = jnp.arange(dim // 2, dtype=jnp.float32)
            theta = ROPE_BASE ** (-2.0 * ids) / (dim // 2)
            r = pos * theta[None, :]
            return (jnp.cos(r), jnp.sin(r))

        def _rope(x, cos, sin):
            b, s, d = x.shape
            xv = x.reshape(b, s, d // 2, 2)
            x0, x1 = (xv[..., 0], xv[..., 1])
            out = jnp.stack([x0 * cos - x1 * sin, x1 * cos + x0 * sin], axis=-1)
            return out.reshape(b, s, d)
        key = jax.random.key(seed)
        ks = jax.random.split(key, 10)
        d_model, d_q, d_kv = (128, D_Q, D_KV)
        b, s = (2, 256)
        w = lambda k, i, o: jax.random.normal(k, (i, o), dtype=jnp.float32) * 0.02
        return {'x': jax.random.normal(ks[0], (b, s, d_model), dtype=jnp.float32), 'Wd_q_w': w(ks[1], d_model, d_q), 'Wd_q_b': jnp.zeros((d_q,), jnp.float32), 'Wu_q_w': w(ks[2], d_q, d_model), 'Wu_q_b': jnp.zeros((d_model,), jnp.float32), 'Wq_r_w': w(ks[3], d_q, d_model), 'Wq_r_b': jnp.zeros((d_model,), jnp.float32), 'Wk_r_w': w(ks[4], d_model, d_model), 'Wk_r_b': jnp.zeros((d_model,), jnp.float32), 'Wd_kv_w': w(ks[5], d_model, d_kv), 'Wd_kv_b': jnp.zeros((d_kv,), jnp.float32), 'Wu_k_w': w(ks[6], d_kv, d_model), 'Wu_k_b': jnp.zeros((d_model,), jnp.float32), 'Wu_v_w': w(ks[7], d_kv, d_model), 'Wu_v_b': jnp.zeros((d_model,), jnp.float32), 'Wo_w': w(ks[8], d_model, d_model), 'Wo_b': jnp.zeros((d_model,), jnp.float32)}
    _L1_attn_in = _L1_attn_setup()

    def _L1_ffn_setup():
        import jax, jax.numpy as jnp
        import numpy as np
        DIM = 128

        def _reference_tuple_inner(x, W_r, W_k, W_v, mu_r, mu_k):
            B, T, C = x.shape
            x_prev = jnp.concatenate([jnp.zeros((B, 1, C), x.dtype), x[:, :-1, :]], axis=1)
            xr = mu_r * x + (1.0 - mu_r) * x_prev
            xk = mu_k * x + (1.0 - mu_k) * x_prev
            r = jax.nn.sigmoid(jnp.einsum('btc,dc->btd', xr, W_r))
            k = jnp.einsum('btc,dc->btd', xk, W_k)
            k_act = jnp.square(jax.nn.relu(k))
            out = r * jnp.einsum('btc,dc->btd', k_act, W_v)
            new_state = x[:, -1, :]
            return (out, new_state)
        key = jax.random.key(seed)
        ks = jax.random.split(key, 6)
        B, T, C = (8, 256, DIM)
        x = jax.random.normal(ks[0], (B, T, C), dtype=jnp.float32)
        s = 1.0 / np.sqrt(C)
        W_r = jax.random.uniform(ks[1], (C, C), jnp.float32, -s, s)
        W_k = jax.random.uniform(ks[2], (C, C), jnp.float32, -s, s)
        W_v = jax.random.uniform(ks[3], (C, C), jnp.float32, -s, s)
        mu_r = jax.random.uniform(ks[4], (C,), jnp.float32)
        mu_k = jax.random.uniform(ks[5], (C,), jnp.float32)
        return {'x': x, 'W_r': W_r, 'W_k': W_k, 'W_v': W_v, 'mu_r': mu_r, 'mu_k': mu_k}
    _L1_ffn_in = _L1_ffn_setup()
    _d = {'L0_attn_x': _L0_attn_in['x'], 'L0_attn_mem': _L0_attn_in['mem'], 'L0_attn_wq': _L0_attn_in['wq'], 'L0_attn_wk': _L0_attn_in['wk'], 'L0_attn_wv': _L0_attn_in['wv'], 'L0_attn_wo': _L0_attn_in['wo'], 'L0_attn_w1': _L0_attn_in['w1'], 'L0_attn_b1': _L0_attn_in['b1'], 'L0_attn_w2': _L0_attn_in['w2'], 'L0_attn_b2': _L0_attn_in['b2'], 'L0_attn_lin1': _L0_attn_in['lin1'], 'L0_attn_lin2': _L0_attn_in['lin2'], 'L0_attn_alpha': _L0_attn_in['alpha'], 'L0_attn_theta': _L0_attn_in['theta'], 'L0_ffn_router_w': _L0_ffn_in['router_w'], 'L0_ffn_Wg': _L0_ffn_in['Wg'], 'L0_ffn_Wu': _L0_ffn_in['Wu'], 'L0_ffn_Wd': _L0_ffn_in['Wd'], 'L1_attn_Wd_q_w': _L1_attn_in['Wd_q_w'], 'L1_attn_Wd_q_b': _L1_attn_in['Wd_q_b'], 'L1_attn_Wu_q_w': _L1_attn_in['Wu_q_w'], 'L1_attn_Wu_q_b': _L1_attn_in['Wu_q_b'], 'L1_attn_Wq_r_w': _L1_attn_in['Wq_r_w'], 'L1_attn_Wq_r_b': _L1_attn_in['Wq_r_b'], 'L1_attn_Wk_r_w': _L1_attn_in['Wk_r_w'], 'L1_attn_Wk_r_b': _L1_attn_in['Wk_r_b'], 'L1_attn_Wd_kv_w': _L1_attn_in['Wd_kv_w'], 'L1_attn_Wd_kv_b': _L1_attn_in['Wd_kv_b'], 'L1_attn_Wu_k_w': _L1_attn_in['Wu_k_w'], 'L1_attn_Wu_k_b': _L1_attn_in['Wu_k_b'], 'L1_attn_Wu_v_w': _L1_attn_in['Wu_v_w'], 'L1_attn_Wu_v_b': _L1_attn_in['Wu_v_b'], 'L1_attn_Wo_w': _L1_attn_in['Wo_w'], 'L1_attn_Wo_b': _L1_attn_in['Wo_b'], 'L1_ffn_W_r': _L1_ffn_in['W_r'], 'L1_ffn_W_k': _L1_ffn_in['W_k'], 'L1_ffn_W_v': _L1_ffn_in['W_v'], 'L1_ffn_mu_r': _L1_ffn_in['mu_r'], 'L1_ffn_mu_k': _L1_ffn_in['mu_k']}
    _x0 = _d['L0_attn_x']
    _d['L0_attn_x'] = jax.random.normal(jax.random.fold_in(jax.random.key(seed), 1), (2, 1024, 128), dtype=_x0.dtype)
    del _x0
    return _d

def reference(L0_attn_x, L0_attn_mem, L0_attn_wq, L0_attn_wk, L0_attn_wv, L0_attn_wo, L0_attn_w1, L0_attn_b1, L0_attn_w2, L0_attn_b2, L0_attn_lin1, L0_attn_lin2, L0_attn_alpha, L0_attn_theta, L0_ffn_router_w, L0_ffn_Wg, L0_ffn_Wu, L0_ffn_Wd, L1_attn_Wd_q_w, L1_attn_Wd_q_b, L1_attn_Wu_q_w, L1_attn_Wu_q_b, L1_attn_Wq_r_w, L1_attn_Wq_r_b, L1_attn_Wk_r_w, L1_attn_Wk_r_b, L1_attn_Wd_kv_w, L1_attn_Wd_kv_b, L1_attn_Wu_k_w, L1_attn_Wu_k_b, L1_attn_Wu_v_w, L1_attn_Wu_v_b, L1_attn_Wo_w, L1_attn_Wo_b, L1_ffn_W_r, L1_ffn_W_k, L1_ffn_W_v, L1_ffn_mu_r, L1_ffn_mu_k):

    def _L0_attn_ref(x, mem, wq, wk, wv, wo, w1, b1, w2, b2, lin1, lin2, alpha, theta):
        import jax, jax.numpy as jnp
        import numpy as np
        DIM = 128
        HID = 512
        NUM_HEADS = 4
        WINDOW = 64
        NUM_PM = 64
        NEG = -1e+30

        def _swa(x_in, wq, wk, wv, wo):
            B, S, D = x_in.shape
            h, dh = (NUM_HEADS, D // NUM_HEADS)
            q = (x_in @ wq.T).reshape(B, S, h, dh).transpose(0, 2, 1, 3)
            k = (x_in @ wk.T).reshape(B, S, h, dh).transpose(0, 2, 1, 3)
            v = (x_in @ wv.T).reshape(B, S, h, dh).transpose(0, 2, 1, 3)
            i = jnp.arange(S)[:, None]
            j = jnp.arange(S)[None, :]
            mask = (j <= i) & (j > i - WINDOW)
            logits = jnp.einsum('bhqd,bhkd->bhqk', q, k) / np.sqrt(dh).astype(np.float32)
            logits = jnp.where(mask, logits, NEG)
            attn = jax.nn.softmax(logits, axis=-1)
            out = jnp.einsum('bhqk,bhkd->bhqd', attn, v)
            out = out.transpose(0, 2, 1, 3).reshape(B, S, D)
            return out @ wo.T

        def _mlp(w1, b1, w2, b2, x):
            return jax.nn.silu(x @ w1.T + b1) @ w2.T + b2
        B, S, D = x.shape
        pm = jnp.broadcast_to(mem[None], (B, NUM_PM, D))
        x_in = jnp.concatenate([pm, x], axis=1)
        out_swa = _swa(x_in, wq, wk, wv, wo)
        k_flat = x_in.reshape(-1, D)
        v_flat = out_swa.reshape(-1, D)

        def loss_fn(params):
            pred = _mlp(*params, k_flat)
            return 0.5 * jnp.sum((pred - v_flat) ** 2)
        grads = jax.grad(loss_fn)((w1, b1, w2, b2))
        upd = jax.tree_util.tree_map(lambda p, g: (1.0 - alpha) * p - theta * g, (w1, b1, w2, b2), grads)
        out_mem = _mlp(*upd, k_flat).reshape(x_in.shape)
        g1 = jax.nn.sigmoid(out_swa @ lin1.T)
        g2 = jax.nn.sigmoid(out_mem @ lin2.T)
        out_merged = g1 * out_swa + g2 * out_mem
        return out_merged[:, NUM_PM:, :]

    def _L0_ffn_ref(x, router_w, Wg, Wu, Wd):
        import jax, jax.numpy as jnp
        import numpy as np
        TOP_K = 2
        B, S, H = x.shape
        E = router_w.shape[0]
        xf = x.reshape(-1, H)
        logits = xf @ router_w.T
        top_vals, top_idx = jax.lax.top_k(logits, TOP_K)
        top_w = jax.nn.softmax(top_vals, axis=-1)
        combine = jnp.einsum('tke,tk->te', jax.nn.one_hot(top_idx, E, dtype=xf.dtype), top_w)
        g = jnp.einsum('th,eih->eti', xf, Wg)
        u = jnp.einsum('th,eih->eti', xf, Wu)
        h = jax.nn.silu(g) * u
        y = jnp.einsum('eti,ehi->eth', h, Wd)
        out = jnp.einsum('te,eth->th', combine, y)
        return out.reshape(B, S, H)

    def _L1_attn_ref(x, Wd_q_w, Wd_q_b, Wu_q_w, Wu_q_b, Wq_r_w, Wq_r_b, Wk_r_w, Wk_r_b, Wd_kv_w, Wd_kv_b, Wu_k_w, Wu_k_b, Wu_v_w, Wu_v_b, Wo_w, Wo_b):
        import jax, jax.numpy as jnp
        import numpy as np
        NUM_HEAD = 16
        D_Q = 64
        D_KV = 64
        ROPE_BASE = 10000.0

        def _cos_sin(seq_len, dim):
            pos = jnp.arange(seq_len, dtype=jnp.float32)[:, None]
            ids = jnp.arange(dim // 2, dtype=jnp.float32)
            theta = ROPE_BASE ** (-2.0 * ids) / (dim // 2)
            r = pos * theta[None, :]
            return (jnp.cos(r), jnp.sin(r))

        def _rope(x, cos, sin):
            b, s, d = x.shape
            xv = x.reshape(b, s, d // 2, 2)
            x0, x1 = (xv[..., 0], xv[..., 1])
            out = jnp.stack([x0 * cos - x1 * sin, x1 * cos + x0 * sin], axis=-1)
            return out.reshape(b, s, d)
        b, s, d_model = x.shape
        h = NUM_HEAD
        hd = d_model // h
        scale = jnp.sqrt(jnp.float32(h + D_KV + D_Q))

        def heads(t):
            return t.reshape(b, s, h, hd).transpose(0, 2, 1, 3)
        cos, sin = _cos_sin(s, d_model)
        ct_q = x @ Wd_q_w + Wd_q_b
        qt_c = heads(ct_q @ Wu_q_w + Wu_q_b)
        qt_r = heads(_rope(ct_q @ Wq_r_w + Wq_r_b, cos, sin))
        query = qt_c + qt_r
        ct_kv = x @ Wd_kv_w + Wd_kv_b
        kt_c = heads(ct_kv @ Wu_k_w + Wu_k_b)
        kt_r = heads(_rope(x @ Wk_r_w + Wk_r_b, cos, sin))
        key = kt_c + kt_r
        value = heads(ct_kv @ Wu_v_w + Wu_v_b)
        attn = jnp.einsum('bhqd,bhkd->bhqk', query, key) / scale
        attn = jax.nn.softmax(attn, axis=-1)
        out = jnp.einsum('bhqk,bhkd->bhqd', attn, value)
        out = out.transpose(0, 2, 1, 3).reshape(b, s, d_model)
        return out @ Wo_w + Wo_b

    def _L1_ffn_ref(x, W_r, W_k, W_v, mu_r, mu_k):
        import jax, jax.numpy as jnp
        import numpy as np
        DIM = 128

        def _reference_tuple_inner(x, W_r, W_k, W_v, mu_r, mu_k):
            B, T, C = x.shape
            x_prev = jnp.concatenate([jnp.zeros((B, 1, C), x.dtype), x[:, :-1, :]], axis=1)
            xr = mu_r * x + (1.0 - mu_r) * x_prev
            xk = mu_k * x + (1.0 - mu_k) * x_prev
            r = jax.nn.sigmoid(jnp.einsum('btc,dc->btd', xr, W_r))
            k = jnp.einsum('btc,dc->btd', xk, W_k)
            k_act = jnp.square(jax.nn.relu(k))
            out = r * jnp.einsum('btc,dc->btd', k_act, W_v)
            new_state = x[:, -1, :]
            return (out, new_state)
        return _reference_tuple_inner(x, W_r, W_k, W_v, mu_r, mu_k)[0]
    x = L0_attn_x
    x = x + _layernorm(_L0_attn_ref(_layernorm(x, axis=-1), L0_attn_mem, L0_attn_wq, L0_attn_wk, L0_attn_wv, L0_attn_wo, L0_attn_w1, L0_attn_b1, L0_attn_w2, L0_attn_b2, L0_attn_lin1, L0_attn_lin2, L0_attn_alpha, L0_attn_theta), axis=-1)
    x = x + _layernorm(_L0_ffn_ref(_layernorm(x, axis=-1), L0_ffn_router_w, L0_ffn_Wg, L0_ffn_Wu, L0_ffn_Wd), axis=-1)
    x = x + _layernorm(_L1_attn_ref(_layernorm(x, axis=-1), L1_attn_Wd_q_w, L1_attn_Wd_q_b, L1_attn_Wu_q_w, L1_attn_Wu_q_b, L1_attn_Wq_r_w, L1_attn_Wq_r_b, L1_attn_Wk_r_w, L1_attn_Wk_r_b, L1_attn_Wd_kv_w, L1_attn_Wd_kv_b, L1_attn_Wu_k_w, L1_attn_Wu_k_b, L1_attn_Wu_v_w, L1_attn_Wu_v_b, L1_attn_Wo_w, L1_attn_Wo_b), axis=-1)
    x = x + _layernorm(_L1_ffn_ref(_layernorm(x, axis=-1), L1_ffn_W_r, L1_ffn_W_k, L1_ffn_W_v, L1_ffn_mu_r, L1_ffn_mu_k), axis=-1)
    return x

_drawn_inputs = setup_inputs


def setup_inputs(seed=0):
    import zlib

    import numpy as np

    out = dict(_drawn_inputs(seed))
    spreads = {'L0_attn_b1': (0.0, 0.1),
     'L0_attn_b2': (0.0, 0.1),
     'L1_attn_Wd_q_b': (0.0, 2.0),
     'L1_attn_Wu_q_b': (0.0, 2.0),
     'L1_attn_Wq_r_b': (0.0, 2.0),
     'L1_attn_Wk_r_b': (0.0, 2.0),
     'L1_attn_Wd_kv_b': (0.0, 0.432),
     'L1_attn_Wu_k_b': (0.0, 2.0),
     'L1_attn_Wu_v_b': (0.0, 0.1),
     'L1_attn_Wo_b': (0.0, 0.1)}
    factors = {'L0_attn_wq': 3.299,
     'L0_attn_wk': 3.755,
     'L0_attn_lin1': 64.0,
     'L0_attn_lin2': 3.098,
     'L1_attn_Wd_q_w': 22.514,
     'L1_attn_Wu_q_w': 25.412,
     'L1_attn_Wq_r_w': 25.785,
     'L1_attn_Wk_r_w': 21.461,
     'L1_attn_Wd_kv_w': 3.129,
     'L1_attn_Wu_k_w': 31.421}
    for name, (base, spread) in spreads.items():
        noise = np.random.default_rng([zlib.crc32(name.encode()), seed]).standard_normal(out[name].shape)
        drawn = base * np.exp(spread * noise) if base else spread * noise
        out[name] = jnp.asarray(drawn.astype(out[name].dtype))
    for name, factor in factors.items():
        out[name] = (out[name] * factor).astype(out[name].dtype)
    return out
```

```python
from contextlib import ExitStack

import numpy as np

import concourse.bass as bass
from concourse import mybir

F32 = mybir.dt.float32
BF16 = mybir.dt.bfloat16
U32 = mybir.dt.uint32
ALU = mybir.AluOpType
ACT = mybir.ActivationFunctionType
AX = mybir.AxisListType

P = 128
B, S, D = 2, 1024, 128
NPM = 64
SM = S + NPM
ROWS = B * SM
T0 = ROWS // P
TOK = B * S
TT = TOK // P
HID = 512
HC = HID // P
NH0, DH0, WIN = 4, 32, 64
KW = P + WIN
PADC = P * (T0 + 1)
E, TOPK, I = 8, 2, 352
IC = [(0, 128), (128, 128), (256, 96)]
NH1, DH1 = 16, 8
DC = 64
NB = 512
EPS = 1e-5

PACK_A = [("woT", D), ("wqT", D), ("wkT", D), ("wvT", D), ("ident", P), ("headmask", NH0), ("b1row", HID),
          ("b2row", D), ("alpha", 1), ("theta", 1), ("b1col", HC), ("b2col", 1), ("ones", 1), ("masks", 3 * KW), ("ones3", P),
          ("w1T", HID), ("w2", HID), ("w2T", HID)]
PACK_B = [("lin1T", D), ("lin2T", D), ("routerT", E), ("expert_no", E),
          ("WgT", E * I), ("WuT", E * I), ("WdT", E * 3 * D)]
PACK_C = [("Wdown", D), ("Wuq", D), ("Wqr", D), ("Wqr_sw", D), ("Wuk", D), ("Wkr", D), ("Wkr_sw", D), ("Wuv", D),
          ("b_down", 1), ("b_uq", 1), ("b_qr", 1), ("b_qr_sw", 1), ("b_uk", 1), ("b_kr", 1), ("b_kr_sw", 1),
          ("b_uv_row", D), ("WoL1", D), ("b_o_row", D), ("cos", S), ("sin", S),
          ("W_rT", D), ("W_kT", D), ("W_vT", D), ("mu_r", 1), ("mu_k", 1)]


def offsets(pack):
    at, out = 0, {}
    for name, n in pack:
        out[name] = (at, n)
        at += n
    return out, at


class Count:

    def __init__(self, sem):
        self.sem, self.n = sem, 0

    def add(self, ins):
        self.n += 1
        ins.then_inc(self.sem, 1)
        return self.n


def build(nc, packA, packB, packC, x_in, mem, out):
    offA, nA = offsets(PACK_A)
    offB, nB = offsets(PACK_B)
    offC, nC = offsets(PACK_C)
    ctx = ExitStack()
    with ctx:
        def sb(name, shape, dt=F32, c=ctx):
            return c.enter_context(nc.sbuf_tensor(name, shape, dt))

        def sem(name):
            return ctx.enter_context(nc.semaphore(name))

        WA = sb("WA", [P, nA])
        WB = sb("WB", [P, nB])
        held = [(offA, WA), (offB, WB)]

        def w(name):
            for off, t in held:
                if name in off:
                    a, n = off[name]
                    return t[:, a:a + n]

        ident = w("ident")
        idb = sb("idb", [P, P], BF16)
        X = sb("X", [P, TT, D])
        Y = sb("Y", [P, TT, D])
        epsc = sb("epsc", [P, 1])
        ps = ctx.enter_context(nc.psum_tensor("ps", [P, 8, NB], F32))
        loaded_a, loaded_b, loaded_c, loaded_x = sem("loaded_a"), sem("loaded_b"), sem("loaded_c"), sem("loaded_x")

        first_layer(nc, sem, w, ident, idb, ps, X, Y, epsc, WA, WB, packA, packB, x_in, mem,
                    loaded_a, loaded_b, loaded_x)
        WC = sb("WC", [P, nC])
        held.append((offC, WC))
        XNT = sb("XNT", [P, TOK])
        residual_norm(nc, sem, ident, ps, X, Y, XNT, epsc, "r0")
        experts(nc, sem, w, ident, ps, XNT, Y, loaded_b, WC, packC, loaded_c)
        residual_norm(nc, sem, ident, ps, X, Y, XNT, epsc, "r1")
        second_attention(nc, sem, w, ident, idb, ps, XNT, Y, loaded_c)
        residual_norm(nc, sem, ident, ps, X, Y, XNT, epsc, "r2")
        channel_mix(nc, sem, w, ident, ps, XNT, Y)
        residual_norm(nc, sem, ident, ps, X, Y, None, epsc, "r3", out)


def norm_statistics(dve, chain, src, tiles, stats, mv):
    for t in range(tiles):
        last = chain.add(dve.bn_stats(stats[:, t, :], src[:, t, :]))
    for t in range(tiles):
        dve.wait_ge(chain.sem, last - tiles + 1 + t)
        n = chain.add(dve.bn_aggr(mv[:, t, :], stats[:, t, :]))
    return n


def residual_norm(nc, sem, ident, ps, X, Y, XNT, epsc, tag, out=None):
    with ExitStack() as c:
        def sb(name, shape, dt=F32):
            return c.enter_context(nc.sbuf_tensor(tag + name, shape, dt))

        stats, mv = sb("stats", [P, TT, 6]), sb("mv", [P, TT, 2])
        stats2, mv2 = sb("stats2", [P, TT, 6]), sb("mv2", [P, TT, 2])
        std, rstd = sb("std", [P, TT, 1]), sb("rstd", [P, TT, 1])
        std2, rstd2 = sb("std2", [P, TT, 1]), sb("rstd2", [P, TT, 1])
        XN = sb("XN", [P, TT, D])
        dve_done, var_ready, std_ready = sem(tag + "dve_done"), sem(tag + "var_ready"), sem(tag + "std_ready")
        xn_ready, turned, stored = sem(tag + "xn_ready"), sem(tag + "turned"), sem(tag + "stored")
        evac = sem(tag + "evac")
        x_ready = sem(tag + "x_ready")
        block = c.enter_context(nc.Block())

        @block.vector
        def _(dve):
            chain = Count(dve_done)

            def rstd_of(src, stats, mv, std, rstd, k):
                n = norm_statistics(dve, chain, src, TT, stats, mv)
                dve.wait_ge(dve_done, n)
                dve.nop().then_inc(var_ready, 1)
                dve.wait_ge(std_ready, k)
                dve.wait_ge(dve_done, chain.add(dve.reciprocal(rstd[:, :, :], std[:, :, :])))

            rstd_of(Y, stats, mv, std, rstd, 1)
            for t in range(TT):
                chain.add(dve.tensor_scalar(Y[:, t, :], Y[:, t, :], mv[:, t, 0:1], rstd[:, t, :],
                                            ALU.subtract, ALU.mult))
            for j in range(TT // 4):
                dve.wait_ge(dve_done, chain.n - (TT - 4 * (j + 1)) - j)
                n = chain.add(dve.tensor_tensor(X[:, 4 * j:4 * j + 4, :], X[:, 4 * j:4 * j + 4, :],
                                                Y[:, 4 * j:4 * j + 4, :], ALU.add))
            dve.wait_ge(dve_done, n)
            if out is not None:
                dve.nop().then_inc(x_ready, 1)
            else:
                rstd_of(X, stats2, mv2, std2, rstd2, 2)
                for t in range(TT):
                    dve.tensor_scalar(XN[:, t, :], X[:, t, :], mv2[:, t, 0:1], rstd2[:, t, :],
                                      ALU.subtract, ALU.mult).then_inc(xn_ready, 1)

        @block.scalar
        def _(act):
            act.wait_ge(var_ready, 1)
            act.activation(std[:, :, :], mv[:, :, 1:2], ACT.Sqrt, bias=epsc[:, :]).then_inc(std_ready, 1)
            if out is None:
                act.wait_ge(var_ready, 2)
                act.activation(std2[:, :, :], mv2[:, :, 1:2], ACT.Sqrt, bias=epsc[:, :]).then_inc(std_ready, 1)
                for j in range(TT // 4):
                    act.wait_ge(turned, j + 1)
                    act.activation(XNT[:, NB * j:NB * (j + 1)], ps[:, j, :], ACT.Copy).then_inc(evac, 1)
                act.wait_ge(evac, TT // 4)

        @block.tensor
        def _(pe):
            if out is None:
                for t in range(TT):
                    pe.wait_ge(xn_ready, t + 1)
                    ins = pe.transpose(ps[:, t // 4, P * (t % 4):P * (t % 4 + 1)], XN[:, t, :], ident)
                    if t % 4 == 3:
                        ins.then_inc(turned, 1)

        @block.sync
        def _(sp):
            if out is not None:
                sp.wait_ge(x_ready, 1)
                sp.dma_start(out.rearrange("(t p) d -> p t d", p=P), X[:, :, :]).then_inc(stored, 16)
                sp.wait_ge(stored, 16)


def first_layer(nc, sem, w, ident, idb, ps, X, Y, epsc, WA, WB, packA, packB, x_in, mem,
                loaded_a, loaded_b, loaded_x):
    SCALE = 1.0 / float(np.sqrt(DH0).astype(np.float32))
    with ExitStack() as c0:
        def sb(name, shape, dt=F32):
            return c0.enter_context(nc.sbuf_tensor(name, shape, dt))

        XT = sb("XT", [P, PADC])
        OT = sb("OT", [P, ROWS])
        dzsum = sb("dzsum", [P, HID])
        errsum = sb("errsum", [P, D])
        G1, G2 = ps[:, 6, :], ps[:, 7, :]
        with ExitStack() as c:
            def sbi(name, shape, dt=F32):
                return c.enter_context(nc.sbuf_tensor(name, shape, dt))

            XR = sbi("XR", [P, T0, D])
            XN = sbi("XN", [P, T0, D])
            KM = sbi("KM", [P, NH0, PADC])
            QT = sbi("QT", [P, PADC])
            V = sbi("V", [P, T0 + 1, D])
            masks = sbi("masks", [P, 3, 2, KW], BF16)
            ones_b = sbi("ones_b", [P, P], BF16)
            stats, mv = sbi("stats", [P, T0, 6]), sbi("mv", [P, T0, 2])
            std, rstd = sbi("std", [P, T0, 1]), sbi("rstd", [P, T0, 1])
            b1s = sbi("b1s", [P, HID], BF16)
            b1t = sbi("b1t", [P, 2, HID])
            b1h = sbi("b1h", [P, 2, HID], BF16)
            nwoT = sbi("nwoT", [P, D])
            mem_in, dve_done, var_ready, std_ready = (sem("mem_in"), sem("l0_dve_done"), sem("l0_var_ready"),
                                                      sem("l0_std_ready"))
            x_padded = sem("x_padded")
            xn_ready, turned, xt_ready = sem("l0_xn_ready"), sem("l0_turned"), sem("l0_xt_ready")
            qk_ready, q_out, k_out, v_ready, v_out = (sem("qk_ready"), sem("q_out"), sem("k_out"), sem("v_ready"),
                                                      sem("v_out"))
            x_in_ready, cast = sem("x_in_ready"), sem("l0_cast")
            pool_init = sem("pool_init")
            OWN = [(0, 0, NPM), (8, NPM, P)]

            with nc.Block() as block:
                @block.sync
                def _(sp):
                    sp.dma_start(XR[NPM:P, 0, :], x_in[0:NPM, :]).then_inc(loaded_x, 16)
                    sp.dma_start(XR[:, 1:8, :], x_in[NPM:NPM + 7 * P, :].rearrange("(t p) d -> p t d", p=P)).then_inc(loaded_x, 16)
                    sp.dma_start(XR[0:NPM, 8, :], x_in[S - NPM:S, :]).then_inc(loaded_x, 16)
                    sp.dma_start(XR[:, 9:T0, :], x_in[S:TOK, :].rearrange("(t p) d -> p t d", p=P)).then_inc(loaded_x, 16)
                    for t, a, b in OWN:
                        sp.dma_start(XR[a:b, t, :], mem).then_inc(loaded_x, 16)
                        sp.dma_start(XN[a:b, t, :], mem).then_inc(mem_in, 16)
                    sp.dma_start(X[:, :, :], x_in.rearrange("(t p) d -> p t d", p=P)).then_inc(x_in_ready, 16)
                    sp.dma_start(WB[:, :], packB).then_inc(loaded_b, 16)

                @block.gpsimd
                def _(pool):
                    pool.memset(epsc[:, :], EPS).then_inc(pool_init, 1)
                    pool.memset(XT[:, 0:NPM], 0.0).then_inc(x_padded, 1)
                    pool.memset(XT[:, PADC - NPM:PADC], 0.0).then_inc(x_padded, 1)
                    pool.memset(b1s[:, :], 0.0).then_inc(pool_init, 1)
                    pool.memset(dzsum[:, :], 0.0).then_inc(pool_init, 1)
                    pool.memset(errsum[:, :], 0.0).then_inc(pool_init, 1)
                    pool.wait_ge(loaded_a, 16)
                    pool.tensor_copy(idb[:, :], ident).then_inc(cast, 1)
                    pool.tensor_copy(ones_b[:, :], w("ones3")).then_inc(cast, 1)
                    for n in range(2):
                        pool.tensor_copy(masks[:, :, n, :], w("masks").rearrange("p (m k) -> p m k", m=3)).then_inc(cast, 1)
                    pool.wait_ge(cast, 4)

                @block.vector
                def _(dve):
                    chain = Count(dve_done)
                    dve.wait_ge(loaded_x, 16 * 6)
                    dve.wait_ge(dve_done, norm_statistics(dve, chain, XR, T0, stats, mv))
                    dve.nop().then_inc(var_ready, 1)
                    dve.wait_ge(std_ready, 1)
                    dve.wait_ge(dve_done, chain.add(dve.reciprocal(rstd[:, :, :], std[:, :, :])))
                    for t in range(T0):
                        a, b = {0: (NPM, P), 8: (0, NPM)}.get(t, (0, P))
                        dve.tensor_scalar(XN[a:b, t, :], XR[a:b, t, :], mv[a:b, t, 0:1], rstd[a:b, t, :],
                                          ALU.subtract, ALU.mult).then_inc(xn_ready, 1)
                    dve.wait_ge(loaded_a, 16)
                    for j in range(5):
                        dve.wait_ge(qk_ready, 2 * j + 2)
                        n = NB if j < 4 else PADC - 4 * NB
                        dve.wait_ge(k_out, 4 * j + 2)
                        for h in (2, 3):
                            dve.tensor_scalar(KM[:, h, NB * j:NB * j + n], ps[:, 4 + j % 2, 0:n],
                                              w("headmask")[:, h:h + 1], None, ALU.mult).then_inc(k_out, 1)
                    dve.wait_ge(pool_init, 2)
                    b1 = w("b1row")
                    dve.wait_ge(dve_done, chain.add(dve.tensor_copy(b1h[:, 0, :], b1)))
                    chain.add(dve.tensor_copy(b1s[0:1, :], b1h[0:1, 0, :]))
                    dve.wait_ge(dve_done, chain.add(dve.tensor_tensor(b1t[:, 0, :], b1, b1h[:, 0, :], ALU.subtract)))
                    dve.wait_ge(dve_done, chain.add(dve.tensor_copy(b1h[:, 1, :], b1t[:, 0, :])))
                    chain.add(dve.tensor_copy(b1s[32:33, :], b1h[32:33, 1, :]))
                    dve.wait_ge(dve_done, chain.add(dve.tensor_tensor(b1t[:, 1, :], b1t[:, 0, :], b1h[:, 1, :], ALU.subtract)))
                    dve.wait_ge(dve_done, chain.add(dve.tensor_copy(b1s[64:65, :], b1t[64:65, 1, :])))
                    dve.wait_ge(dve_done, chain.add(dve.tensor_scalar(nwoT[:, :], w("woT"), -1.0, None, ALU.mult)))

                @block.scalar
                def _(act):
                    act.dma_start(WA[:, :], packA).then_inc(loaded_a, 16)
                    act.wait_ge(pool_init, 1)
                    act.wait_ge(var_ready, 1)
                    act.activation(std[:, :, :], mv[:, :, 1:2], ACT.Sqrt, bias=epsc[:, :]).then_inc(std_ready, 1)
                    for j in range(5):
                        act.wait_ge(turned, j + 1)
                        n = NB if j < 4 else P
                        act.activation(XT[:, NPM + NB * j:NPM + NB * j + n], ps[:, j % 2, 0:n], ACT.Copy).then_inc(xt_ready, 1)
                    act.wait_ge(loaded_a, 16)
                    for j in range(5):
                        n = NB if j < 4 else PADC - 4 * NB
                        act.wait_ge(qk_ready, 2 * j + 1)
                        act.activation(QT[:, NB * j:NB * j + n], ps[:, 2 + j % 2, 0:n], ACT.Copy).then_inc(q_out, 1)
                        act.wait_ge(qk_ready, 2 * j + 2)
                        if j:
                            act.wait_ge(k_out, 4 * j)
                        for h in (0, 1):
                            act.activation(KM[:, h, NB * j:NB * j + n], ps[:, 4 + j % 2, 0:n], ACT.Copy,
                                           scale=w("headmask")[:, h:h + 1]).then_inc(k_out, 1)
                    for j in range(5):
                        act.wait_ge(v_ready, j + 1)
                        m = min(4, T0 + 1 - 4 * j)
                        act.activation(V[:, 4 * j:4 * j + m, :],
                                       ps[:, 6 + j % 2, 0:m * P].rearrange("p (t d) -> p t d", d=P),
                                       ACT.Copy).then_inc(v_out, 1)
                    act.wait_ge(v_out, 5)

                @block.tensor
                def _(pe):
                    pe.wait_ge(loaded_a, 16)
                    pe.wait_ge(mem_in, 32)
                    for t in range(T0):
                        pe.wait_ge(xn_ready, t + 1)
                        if t % 4 == 0 and t >= 8:
                            pe.wait_ge(xt_ready, t // 4 - 1)
                        ins = pe.transpose(ps[:, (t // 4) % 2, P * (t % 4):P * (t % 4 + 1)], XN[:, t, :], ident)
                        if t % 4 == 3 or t == T0 - 1:
                            ins.then_inc(turned, 1)
                    pe.wait_ge(x_padded, 2)
                    for j in range(5):
                        n = NB if j < 4 else PADC - 4 * NB
                        pe.wait_ge(xt_ready, min(j + 1, 5))
                        if j >= 2:
                            pe.wait_ge(q_out, j - 1)
                            pe.wait_ge(k_out, 4 * (j - 1))
                        pe.matmul(ps[:, 2 + j % 2, 0:n], w("wqT"), XT[:, NB * j:NB * j + n], start=True, stop=True).then_inc(qk_ready, 1)
                        pe.matmul(ps[:, 4 + j % 2, 0:n], w("wkT"), XT[:, NB * j:NB * j + n], start=True, stop=True).then_inc(qk_ready, 1)
                    for t in range(T0 + 1):
                        j = t // 4
                        if t % 4 == 0 and j >= 2:
                            pe.wait_ge(v_out, j - 1)
                        ins = pe.matmul(ps[:, 6 + j % 2, P * (t % 4):P * (t % 4 + 1)], XT[:, P * t:P * (t + 1)], w("wvT"),
                                        start=True, stop=True)
                        if t % 4 == 3 or t == T0:
                            ins.then_inc(v_ready, 1)

            Pm = sbi("Pm", [P, NH0, KW])
            PTA, PTB = sbi("PTA", [P, NH0, P]), sbi("PTB", [WIN, NH0, P])
            nmax, rowsum, rinv = sbi("nmax", [P, 2, NH0]), sbi("rowsum", [P, NH0]), sbi("rinv", [P, NH0])
            nbias = sbi("nbias", [P, NH0])
            rwide = sbi("rwide", [P, NH0, DH0])
            Osb = sbi("Osb", [P, P])
            Th, H2, U, W2 = sbi("Th", [P, HID]), sbi("H2", [P, HID]), sbi("U", [P, HID]), sbi("W2", [P, HID])
            dz = sbi("dz", [P, HID])
            hT, err, errT = sbi("hT", [P, HC, P]), sbi("err", [P, D]), sbi("errT", [P, P])
            names = ("s_ready nmax_ready nbias_ready p_ready rwide_ready pt_ready pta_out ptb_out o_ready osb_ready ot_ready "
                     "z_ready th_ready h_ready ht_ready ht_out err_psum err_ready errt_psum errt_ready dh_ready "
                     "dz_ready g1_done g2_done sums_done u_done w_done sum_e").split()
            q = {n: sem("l0_" + n) for n in names}
            SB = (0, 1)
            OB, ZB, HB, EB = 2, 3, 4, 5

            with nc.Block() as block:
                @block.tensor
                def _(pe):
                    pe.wait_ge(cast, 4)
                    for s in range(T0 + 2):
                        t, g, l = s, s - 1, s - 2
                        if t < T0:
                            m = 1 if t == 0 else 2 if t == 8 else 0
                            if t:
                                pe.wait_ge(q["pta_out"], t)
                                pe.wait_ge(q["ptb_out"], t)
                            for k in range(2):
                                dst = ps[:, SB[k], 0:2 * KW]
                                pe.matmul(dst, QT[:, NPM + P * t:NPM + P * (t + 1)],
                                          KM[:, 2 * k:2 * k + 2, P * t:P * t + KW], start=True, stop=False)
                                ins = pe.matmul(dst, idb[:, :], masks[:, m, :, :], start=False, stop=True)
                            ins.then_inc(q["s_ready"], 1)
                        if 0 <= g < T0:
                            if g:
                                pe.wait_ge(q["dz_ready"], g)
                            xt = XT[:, NPM + P * g:NPM + P * (g + 1)]
                            pe.matmul(ps[:, ZB, :], xt, w("w1T"), start=True, stop=False)
                            pe.matmul(ps[:, ZB, :], ones_b[:, :], b1s[:, :], start=False, stop=True).then_inc(q["z_ready"], 1)
                        if 0 <= l < T0:
                            pe.wait_ge(q["dz_ready"], l + 1)
                            pe.matmul(G1, XN[:, l, :], dz[:, :], start=(l == 0), stop=(l == T0 - 1)).then_inc(q["g1_done"], 1)
                        if 0 <= g < T0:
                            pe.wait_ge(q["h_ready"], g + 1)
                            if g:
                                pe.wait_ge(q["ht_out"], g)
                            for k in range(HC):
                                ins = pe.transpose(ps[:, HB, P * k:P * (k + 1)], H2[:, P * k:P * (k + 1)], ident)
                            ins.then_inc(q["ht_ready"], 1)
                        if t < T0:
                            pe.wait_ge(q["p_ready"], NH0 * (t + 1))
                            for h in range(NH0):
                                pe.transpose(ps[:, SB[0], P * h:P * (h + 1)], Pm[:, h, 0:P], ident)
                            for h in range(NH0):
                                pe.transpose(ps[0:WIN, SB[1], P * h:P * (h + 1)], Pm[:, h, P:KW], ident).then_inc(q["pt_ready"], 1)
                        if 0 <= g < T0:
                            pe.wait_ge(q["ht_out"], g + 1)
                            pe.wait_ge(q["ot_ready"], g + 1)
                            if g:
                                pe.wait_ge(q["errt_ready"], g)
                            for k in range(HC):
                                pe.matmul(ps[:, EB, 0:D], hT[:, k, :], w("w2T")[:, P * k:P * (k + 1)], start=(k == 0), stop=False)
                            pe.matmul(ps[:, EB, 0:D], OT[:, P * g:P * (g + 1)], nwoT[:, :], start=False, stop=True).then_inc(q["err_psum"], 1)
                        if t < T0:
                            pe.wait_ge(q["rwide_ready"], t + 1)
                            if t:
                                pe.wait_ge(q["ot_ready"], t)
                            pe.matmul(ps[:, OB, P:2 * P], rwide[:, :, :].rearrange("p h d -> p (h d)"), ident,
                                      start=True, stop=True)
                            pe.wait_ge(q["pta_out"], t + 1)
                            pe.wait_ge(q["ptb_out"], t + 1)
                            for h in range(NH0):
                                hs = slice(DH0 * h, DH0 * (h + 1))
                                pe.matmul(ps[hs, OB, 0:P], V[:, t, hs], PTA[:, h, :], start=True, stop=False)
                            for h in range(NH0):
                                hs = slice(DH0 * h, DH0 * (h + 1))
                                ins = pe.matmul(ps[hs, OB, 0:P], V[0:WIN, t + 1, hs], PTB[:, h, :], start=False, stop=True,
                                                tile_position=(0, DH0 * h))
                            ins.then_inc(q["o_ready"], 1)
                        if 0 <= g < T0:
                            pe.wait_ge(q["err_ready"], g + 1)
                            pe.transpose(ps[:, EB, P:2 * P], err[:, :], ident).then_inc(q["errt_psum"], 1)
                            pe.matmul(G2, err[:, :], H2[:, :], start=(g == 0), stop=(g == T0 - 1)).then_inc(q["g2_done"], 1)
                            pe.wait_ge(q["errt_ready"], g + 1)
                            pe.wait_ge(q["h_ready"], g + 1)
                            pe.matmul(ps[:, ZB, :], errT[:, :], w("w2"), start=True, stop=True).then_inc(q["dh_ready"], 1)

                @block.scalar
                def _(act):
                    for s in range(T0 + 1):
                        t, g = s, s - 1
                        if 0 <= g < T0:
                            act.wait_ge(q["z_ready"], g + 1)
                            if g:
                                act.wait_ge(q["w_done"], g)
                            act.activation(Th[:, :], ps[:, ZB, :], ACT.Tanh, scale=0.5).then_inc(q["th_ready"], 1)
                        if t < T0:
                            act.wait_ge(q["nbias_ready"], t + 1)
                            if t:
                                act.wait_ge(q["pt_ready"], NH0 * t)
                                act.wait_ge(q["rwide_ready"], t)
                            for h in range(NH0):
                                act.activation(Pm[:, h, :], ps[:, SB[h // 2], KW * (h % 2):KW * (h % 2 + 1)], ACT.Exp,
                                               bias=nbias[:, h:h + 1], scale=SCALE,
                                               accum_out=rowsum[:, h:h + 1]).then_inc(q["p_ready"], 1)
                        if 0 <= g < T0:
                            act.wait_ge(q["ht_ready"], g + 1)
                            if g:
                                act.wait_ge(q["err_psum"], g)
                            act.activation(hT[:, :, :], ps[:, HB, :].rearrange("p (k n) -> p k n", k=HC), ACT.Copy,
                                           scale=0.5).then_inc(q["ht_out"], 1)
                        if t < T0:
                            act.wait_ge(q["pt_ready"], NH0 * (t + 1))
                            if t:
                                act.wait_ge(q["o_ready"], t)
                            act.activation(PTB[:, :, :], ps[0:WIN, SB[1], :].rearrange("p (k n) -> p k n", k=NH0),
                                           ACT.Copy).then_inc(q["ptb_out"], 1)
                        if 0 <= g < T0:
                            act.wait_ge(q["errt_psum"], g + 1)
                            if g:
                                act.wait_ge(q["dh_ready"], g)
                            act.activation(errT[:, :], ps[:, EB, P:2 * P], ACT.Copy).then_inc(q["errt_ready"], 1)
                        if t < T0:
                            act.wait_ge(q["o_ready"], t + 1)
                            if t:
                                act.wait_ge(q["ot_ready"], t)
                            act.activation(Osb[:, :], ps[:, OB, 0:P], ACT.Copy).then_inc(q["osb_ready"], 1)

                @block.vector
                def _(dve):
                    dve.wait_ge(x_in_ready, 16)
                    for s in range(T0 + 1):
                        t, g = s, s - 1
                        if t < T0:
                            dve.wait_ge(q["s_ready"], t + 1)
                            if t:
                                dve.wait_ge(q["nbias_ready"], t)
                                dve.wait_ge(q["p_ready"], NH0 * t)
                            for k in range(2):
                                dve.tensor_reduce(nmax[:, t % 2, 2 * k:2 * k + 2], ps[:, SB[k], 0:2 * KW].rearrange("p (h k) -> p h k", h=2),
                                                  AX.X, ALU.max, negate=True).then_inc(q["nmax_ready"], 1)
                            dve.wait_ge(q["nmax_ready"], 2 * (t + 1))
                            dve.tensor_scalar(nbias[:, :], nmax[:, t % 2, :], SCALE, None, ALU.mult).then_inc(q["nbias_ready"], 1)
                        if 0 <= g < T0:
                            dve.wait_ge(q["th_ready"], g + 1)
                            if g:
                                dve.wait_ge(q["g2_done"], g)
                                dve.wait_ge(q["ht_ready"], g)
                            dve.scalar_tensor_tensor(out=H2[:, :], in0=Th[:, :], scalar=1.0, in1=ps[:, ZB, :],
                                                     op0=ALU.add, op1=ALU.mult).then_inc(q["h_ready"], 1)
                            dve.wait_ge(q["h_ready"], g + 1)
                            dve.scalar_tensor_tensor(out=U[:, :], in0=Th[:, :], scalar=1.0, in1=H2[:, :],
                                                     op0=ALU.subtract, op1=ALU.mult).then_inc(q["u_done"], 1)
                        if t < T0:
                            dve.wait_ge(q["p_ready"], NH0 * (t + 1))
                            dve.reciprocal(rinv[:, :], rowsum[:, :]).then_inc(q["sum_e"], 1)
                            dve.wait_ge(q["sum_e"], t + 1)
                            if t:
                                dve.wait_ge(q["o_ready"], t)
                            dve.tensor_copy(rwide[:, :, :], rinv[:, :].unsqueeze(2).to_broadcast([P, NH0, DH0])).then_inc(q["rwide_ready"], 1)
                            dve.wait_ge(q["pt_ready"], NH0 * (t + 1))
                            dve.tensor_copy(PTA[:, :, :], ps[:, SB[0], :].rearrange("p (k n) -> p k n", k=NH0)).then_inc(q["pta_out"], 1)
                        if 0 <= g < T0:
                            dve.wait_ge(q["err_psum"], g + 1)
                            if g:
                                dve.wait_ge(q["g2_done"], g)
                                dve.wait_ge(q["sums_done"], 2 * g)
                            dve.tensor_tensor(err[:, :], ps[:, EB, 0:D], w("b2row"), ALU.add).then_inc(q["err_ready"], 1)
                            dve.wait_ge(q["u_done"], g + 1)
                            if g:
                                dve.wait_ge(q["dz_ready"], g)
                            dve.scalar_tensor_tensor(out=W2[:, :], in0=Th[:, :], scalar=2.0, in1=U[:, :],
                                                     op0=ALU.mult, op1=ALU.subtract).then_inc(q["w_done"], 1)
                        if t < T0:
                            dve.wait_ge(q["osb_ready"], t + 1)
                            dve.tensor_tensor(OT[:, P * t:P * (t + 1)], Osb[:, :], ps[:, OB, P:2 * P], ALU.mult).then_inc(q["ot_ready"], 1)
                        if 0 <= g < T0:
                            dve.wait_ge(q["dh_ready"], g + 1)
                            dve.wait_ge(q["w_done"], g + 1)
                            if g:
                                dve.wait_ge(q["g1_done"], g)
                                dve.wait_ge(q["sums_done"], 2 * g)
                            dve.scalar_tensor_tensor(out=dz[:, :], in0=W2[:, :], scalar=2.0, in1=ps[:, ZB, :],
                                                     op0=ALU.add, op1=ALU.mult).then_inc(q["dz_ready"], 1)

                @block.gpsimd
                def _(pool):
                    for g in range(T0):
                        if g:
                            pool.wait_ge(q["sums_done"], 2 * g)
                        pool.wait_ge(q["err_ready"], g + 1)
                        pool.tensor_tensor(errsum[:, :], errsum[:, :], err[:, :], ALU.add).then_inc(q["sums_done"], 1)
                        pool.wait_ge(q["dz_ready"], g + 1)
                        pool.tensor_tensor(dzsum[:, :], dzsum[:, :], dz[:, :], ALU.add).then_inc(q["sums_done"], 1)

        updated_mlp(nc, sem, w, ident, ps, XT, OT, dzsum, errsum, G1, G2, Y, loaded_b)


def updated_mlp(nc, sem, w, ident, ps, XT, OT, dzsum, errsum, G1, G2, Y, loaded_b):
    with ExitStack() as c:
        def sb(name, shape, dt=F32):
            return c.enter_context(nc.sbuf_tensor("um_" + name, shape, dt))

        keep, nth = sb("keep", [P, 1]), sb("nth", [P, 3])
        w1n, w2n = sb("w1n", [P, HID]), sb("w2n", [P, HID])
        w1k, w2k = sb("w1k", [P, HID]), sb("w2k", [P, HID])
        g2s = sb("g2s", [P, HID])
        b1k, b1n, b2k, b2n = sb("b1k", [P, HC]), sb("b1n", [P, HC]), sb("b2k", [P, 1]), sb("b2n", [P, 1])
        hT = sb("hT", [P, HC, NB])
        swaT, memT = sb("swaT", [P, NB]), sb("memT", [P, NB])
        t1, t2 = sb("t1", [P, NB]), sb("t2", [P, NB])
        a1, a2, mg = sb("a1", [P, NB]), sb("a2", [P, NB]), sb("mg", [P, NB])
        dve_done, bsum_ready, g2t_ready, g2s_ready, new_ready = (sem("um_dve_done"), sem("um_bsum_ready"),
                                                                 sem("um_g2t_ready"), sem("um_g2s_ready"), sem("um_new_ready"))
        z_ready, h_ready, swa_psum, swa_ready, mem_psum, mem_ready = (sem("um_z_ready"), sem("um_h_ready"), sem("um_swa_psum"),
                                                                      sem("um_swa_ready"), sem("um_mem_psum"), sem("um_mem_ready"))
        g_psum, tanh_ready, mg_ready, turned, y_ready = (sem("um_g_psum"), sem("um_tanh_ready"), sem("um_mg_ready"),
                                                         sem("um_turned"), sem("um_y_ready"))
        a_done = sem("um_a_done")
        NJ = TOK // NB
        cols = [SM * (j // 2) + NPM + NB * (j % 2) for j in range(NJ)]

        with nc.Block() as block:
            @block.vector
            def _(dve):
                chain = Count(dve_done)
                chain.add(dve.tensor_scalar(keep[:, :], w("alpha"), -1.0, 1.0, ALU.mult, ALU.add))
                for n in range(3):
                    chain.add(dve.tensor_scalar(nth[:, n:n + 1], w("theta"), -0.5 ** n, None, ALU.mult))
                dve.tensor_copy(g2s[:, :], G2).then_inc(g2s_ready, 1)
                dve.wait_ge(dve_done, chain.n)
                chain.add(dve.tensor_scalar(w1k[:, :], w("w1T"), keep[:, :], None, ALU.mult))
                chain.add(dve.tensor_scalar(w2k[:, :], w("w2T"), keep[:, :], None, ALU.mult))
                chain.add(dve.tensor_scalar(b1k[:, :], w("b1col"), keep[:, :], None, ALU.mult))
                chain.add(dve.tensor_scalar(b2k[:, :], w("b2col"), keep[:, :], None, ALU.mult))
                dve.wait_ge(dve_done, chain.n)
                dve.scalar_tensor_tensor(out=w1n[:, :], in0=G1, scalar=nth[:, 2:3], in1=w1k[:, :],
                                         op0=ALU.mult, op1=ALU.add).then_inc(new_ready, 1)
                dve.wait_ge(bsum_ready, 1)
                dve.scalar_tensor_tensor(out=b1n[:, :], in0=ps[:, 0, 0:HC], scalar=nth[:, 2:3], in1=b1k[:, :],
                                         op0=ALU.mult, op1=ALU.add).then_inc(new_ready, 1)
                dve.scalar_tensor_tensor(out=b2n[:, :], in0=ps[:, 0, HC:HC + 1], scalar=nth[:, 0:1], in1=b2k[:, :],
                                         op0=ALU.mult, op1=ALU.add).then_inc(new_ready, 1)
                dve.wait_ge(g2t_ready, 1)
                dve.scalar_tensor_tensor(out=w2n[:, :], in0=ps[:, 1, :], scalar=nth[:, 1:2], in1=w2k[:, :],
                                         op0=ALU.mult, op1=ALU.add).then_inc(new_ready, 1)
                for j in range(NJ):
                    dve.wait_ge(swa_psum, j + 1)
                    if j:
                        dve.wait_ge(mg_ready, j)
                        dve.wait_ge(g_psum, 2 * j)
                    dve.tensor_copy(swaT[:, :], ps[:, 5, :]).then_inc(swa_ready, 1)
                    dve.wait_ge(swa_ready, j + 1)
                    dve.wait_ge(tanh_ready, 2 * j + 1)
                    dve.scalar_tensor_tensor(out=a1[:, :], in0=t1[:, :], scalar=1.0, in1=swaT[:, :],
                                             op0=ALU.add, op1=ALU.mult).then_inc(a_done, 1)
                    dve.wait_ge(tanh_ready, 2 * j + 2)
                    dve.wait_ge(mem_ready, j + 1)
                    dve.scalar_tensor_tensor(out=a2[:, :], in0=t2[:, :], scalar=1.0, in1=memT[:, :],
                                             op0=ALU.add, op1=ALU.mult).then_inc(a_done, 1)
                    dve.wait_ge(a_done, 2 * j + 2)
                    if j:
                        dve.wait_ge(turned, j)
                    dve.tensor_tensor(mg[:, :], a1[:, :], a2[:, :], ALU.add).then_inc(mg_ready, 1)

            @block.tensor
            def _(pe):
                pe.wait_ge(loaded_b, 16)
                for k in range(HC):
                    pe.matmul(ps[:, 0, k:k + 1], dzsum[:, P * k:P * (k + 1)], w("ones"), start=True, stop=True)
                pe.matmul(ps[:, 0, HC:HC + 1], errsum[:, :], w("ones"), start=True, stop=True).then_inc(bsum_ready, 1)
                pe.wait_ge(g2s_ready, 1)
                for k in range(HC):
                    ins = pe.transpose(ps[:, 1, P * k:P * (k + 1)], g2s[:, P * k:P * (k + 1)], ident)
                ins.then_inc(g2t_ready, 1)

                def z_of(j):
                    for k in range(HC):
                        if j:
                            pe.wait_ge(h_ready, HC * (j - 1) + k + 1)
                            if k == 0:
                                pe.wait_ge(y_ready, j)
                        pe.matmul(ps[:, k, :], w1n[:, P * k:P * (k + 1)], XT[:, NPM + cols[j]:NPM + cols[j] + NB],
                                  start=True, stop=True).then_inc(z_ready, 1)

                pe.wait_ge(new_ready, 4)
                z_of(0)
                for j in range(NJ):
                    if j:
                        pe.wait_ge(swa_ready, j)
                    pe.matmul(ps[:, 5, :], w("woT"), OT[:, cols[j]:cols[j] + NB], start=True, stop=True).then_inc(swa_psum, 1)
                    if j:
                        pe.wait_ge(mem_ready, j)
                    for k in range(HC):
                        pe.wait_ge(h_ready, HC * j + k + 1)
                        ins = pe.matmul(ps[:, 4, :], w2n[:, P * k:P * (k + 1)], hT[:, k, :], start=(k == 0), stop=(k == HC - 1))
                    ins.then_inc(mem_psum, 1)
                    pe.wait_ge(swa_ready, j + 1)
                    if j:
                        pe.wait_ge(tanh_ready, 2 * j)
                    pe.matmul(ps[:, 6, :], w("lin1T"), swaT[:, :], start=True, stop=True).then_inc(g_psum, 1)
                    pe.wait_ge(mem_ready, j + 1)
                    pe.matmul(ps[:, 7, :], w("lin2T"), memT[:, :], start=True, stop=True).then_inc(g_psum, 1)
                    pe.wait_ge(mg_ready, j + 1)
                    for n in range(4):
                        ins = pe.transpose(ps[:, 0, P * n:P * (n + 1)], mg[:, P * n:P * (n + 1)], ident)
                    ins.then_inc(turned, 1)
                    if j + 1 < NJ:
                        z_of(j + 1)

            @block.scalar
            def _(act):
                act.wait_ge(new_ready, 4)
                for j in range(NJ):
                    for k in range(HC):
                        act.wait_ge(z_ready, HC * j + k + 1)
                        if j and k == 0:
                            act.wait_ge(mem_psum, j)
                        act.activation(hT[:, k, :], ps[:, k, :], ACT.Silu, bias=b1n[:, k:k + 1]).then_inc(h_ready, 1)
                    act.wait_ge(mem_psum, j + 1)
                    if j:
                        act.wait_ge(a_done, 2 * j)
                        act.wait_ge(g_psum, 2 * j)
                    act.activation(memT[:, :], ps[:, 4, :], ACT.Identity, bias=b2n[:, :]).then_inc(mem_ready, 1)
                    act.wait_ge(g_psum, 2 * j + 1)
                    act.activation(t1[:, :], ps[:, 6, :], ACT.Tanh, scale=0.5).then_inc(tanh_ready, 1)
                    act.wait_ge(g_psum, 2 * j + 2)
                    act.activation(t2[:, :], ps[:, 7, :], ACT.Tanh, scale=0.5).then_inc(tanh_ready, 1)
                    act.wait_ge(turned, j + 1)
                    act.activation(Y[:, 4 * j:4 * j + 4, :], ps[:, 0, :].rearrange("p (t d) -> p t d", d=D), ACT.Copy,
                                   scale=0.5).then_inc(y_ready, 1)
                act.wait_ge(y_ready, NJ)


def wait(eng, sem, value):
    if isinstance(value, int) and value <= 0:
        return
    eng.wait_ge(sem, value)


def experts(nc, sem, w, ident, ps, XNT, Y, loaded_b, WC, packC, loaded_c):
    with ExitStack() as c:
        def sb(name, shape, dt=F32):
            return c.enter_context(nc.sbuf_tensor("ex_" + name, shape, dt))

        L, M8, I8 = sb("L", [P, TT, E]), sb("M8", [P, TT, 8]), sb("I8", [P, TT, 8], U32)
        IF = sb("IF", [P, TT, 2])
        dd, ee, dn, w1, w2 = (sb(n, [P, TT, 1]) for n in ("dd", "ee", "dn", "w1", "w2"))
        c1, c2, C1, C2, COMB = (sb(n, [P, TT, E]) for n in ("c1", "c2", "C1", "C2", "COMB"))
        dve_done, logits_ready, d_ready, e_ready = sem("ex_dve_done"), sem("ex_logits_ready"), sem("ex_d_ready"), sem("ex_e_ready")

        with nc.Block() as block:
            @block.sync
            def _(sp):
                sp.dma_start(WC[:, :], packC).then_inc(loaded_c, 16)

            @block.tensor
            def _(pe):
                pe.wait_ge(loaded_b, 16)
                for t in range(TT):
                    ins = pe.matmul(ps[:, 0, E * t:E * (t + 1)], XNT[:, P * t:P * (t + 1)], w("routerT"), start=True, stop=True)
                ins.then_inc(logits_ready, 1)

            @block.scalar
            def _(act):
                act.wait_ge(d_ready, 1)
                act.activation(ee[:, :, :], dd[:, :, :], ACT.Exp).then_inc(e_ready, 1)

            @block.vector
            def _(dve):
                chain = Count(dve_done)

                def then(ins):
                    dve.wait_ge(dve_done, chain.add(ins))

                dve.wait_ge(logits_ready, 1)
                then(dve.tensor_copy(L[:, :, :], ps[:, 0, 0:TT * E].rearrange("p (t e) -> p t e", e=E)))
                for t in range(TT):
                    n = chain.add(dve.max(M8[:, t, :], L[:, t, :]))
                dve.wait_ge(dve_done, n)
                for t in range(TT):
                    n = chain.add(dve.max_index(I8[:, t, :], M8[:, t, :], L[:, t, :]))
                then(dve.tensor_tensor(dd[:, :, :], M8[:, :, 1:2], M8[:, :, 0:1], ALU.subtract))
                dve.nop().then_inc(d_ready, 1)
                dve.wait_ge(e_ready, 1)
                then(dve.tensor_scalar(dn[:, :, :], ee[:, :, :], 1.0, None, ALU.add))
                then(dve.reciprocal(w1[:, :, :], dn[:, :, :]))
                then(dve.tensor_tensor(w2[:, :, :], ee[:, :, :], w1[:, :, :], ALU.mult))
                then(dve.tensor_copy(IF[:, :, :], I8[:, :, 0:2]))
                no = w("expert_no").unsqueeze(1).to_broadcast([P, TT, E])
                for k, (cc, CC, ww) in enumerate(((c1, C1, w1), (c2, C2, w2))):
                    then(dve.tensor_tensor(cc[:, :, :], IF[:, :, k:k + 1].to_broadcast([P, TT, E]), no, ALU.is_equal))
                    then(dve.tensor_tensor(CC[:, :, :], cc[:, :, :], ww[:, :, :].to_broadcast([P, TT, E]), ALU.mult))
                then(dve.tensor_tensor(COMB[:, :, :], C1[:, :, :], C2[:, :, :], ALU.add))

        U = 2 * E
        xs = sb("xs", [P, 2, P])
        cs = sb("cs", [P, 2, E])
        sg, h = sb("sg", [P, 2, I]), sb("h", [P, 2, 3 * P])
        hT = sb("hT", [P, 2, 3, P])
        gu_ready, silu_ready, h_ready, turned, ht_out, down_done, y_out, staged, padded = (
            sem("ex_" + n) for n in "gu_ready silu_ready h_ready turned ht_out down_done y_out staged padded".split())
        GB, UB, TB, YB = 0, 2, 4, 6
        wg, wu = w("WgT"), w("WuT")
        wd = w("WdT")
        N = TT // 2

        with nc.Block() as block:
            @block.tensor
            def _(pe):
                pe.wait_ge(padded, 1)

                def gate_up(i, u):
                    b, e, tile = u % 2, u % E, (u // E) % 2
                    if u % E == 0:
                        wait(pe, staged, 2 * (2 * i + u // E + 1))
                    wait(pe, silu_ready, U * i + u - 1)
                    wait(pe, h_ready, U * i + u - 1)
                    pe.matmul(ps[:, GB + b, 0:I], xs[:, tile, :], wg[:, I * e:I * (e + 1)], start=True, stop=True)
                    pe.matmul(ps[:, UB + b, 0:I], xs[:, tile, :], wu[:, I * e:I * (e + 1)], start=True, stop=True).then_inc(gu_ready, 1)

                def down(i, u):
                    b, e, tile = u % 2, u % E, (u // E) % 2
                    wait(pe, ht_out, U * i + u + 1)
                    if e == 0:
                        wait(pe, y_out, 2 * i + u // E - 1)
                    for k in range(3):
                        ins = pe.matmul(ps[:, YB + tile, 0:D], hT[:, b, k, :], wd[:, D * (3 * e + k):D * (3 * e + k + 1)],
                                        start=(e == 0 and k == 0), stop=(e == E - 1 and k == 2))
                    ins.then_inc(down_done, 1)

                def body(i, first, last):
                    for u in range(U):
                        if not (last and u == U - 1):
                            gate_up(i, u + 1)
                        if not (first and u == 0):
                            down(i, u - 1)
                        wait(pe, h_ready, U * i + u + 1)
                        wait(pe, ht_out, U * i + u - 1)
                        for k in range(3):
                            ins = pe.transpose(ps[:, TB + u % 2, P * k:P * (k + 1)], h[:, u % 2, P * k:P * (k + 1)], ident)
                        ins.then_inc(turned, 1)

                gate_up(0, 0)
                body(0, True, False)
                with pe.Fori(1, N - 1) as i:
                    body(i, False, False)
                body(N - 1, False, True)
                down(N - 1, U - 1)

            @block.scalar
            def _(act):
                def silu(i, u):
                    wait(act, gu_ready, U * i + u + 1)
                    wait(act, h_ready, U * i + u - 1)
                    act.activation(sg[:, u % 2, :], ps[:, GB + u % 2, 0:I], ACT.Silu).then_inc(silu_ready, 1)

                def out_of_psum(i, u):
                    wait(act, turned, U * i + u + 1)
                    wait(act, down_done, U * i + u - 1)
                    act.activation(hT[:, u % 2, :, :], ps[:, TB + u % 2, 0:3 * P].rearrange("p (k n) -> p k n", k=3),
                                   ACT.Copy).then_inc(ht_out, 1)

                def body(i, first):
                    for u in range(U):
                        silu(i, u)
                        if not (first and u == 0):
                            out_of_psum(i, u - 1)

                body(0, True)
                with act.Fori(1, N) as i:
                    body(i, False)
                out_of_psum(N - 1, U - 1)

            @block.vector
            def _(dve):
                dve.wait_ge(padded, 1)

                def tile_out(i, k):
                    wait(dve, down_done, U * i + E * (k + 1))
                    dve.tensor_copy(Y[:, bass.ds(2 * i + k, 1), :], ps[:, YB + k % 2, 0:D].unsqueeze(1)).then_inc(y_out, 1)

                def body(i, first):
                    for u in range(U):
                        wait(dve, silu_ready, U * i + u + 1)
                        wait(dve, turned, U * i + u - 1)
                        wait(dve, staged, 2 * (2 * i + u // E + 1))
                        dve.scalar_tensor_tensor(out=h[:, u % 2, 0:I], in0=ps[:, UB + u % 2, 0:I],
                                                 scalar=cs[:, u // E, u % E:u % E + 1], in1=sg[:, u % 2, :],
                                                 op0=ALU.mult, op1=ALU.mult).then_inc(h_ready, 1)
                        if u == 2 and not first:
                            tile_out(i - 1, 1)
                        if u == E + 2:
                            tile_out(i, 0)

                body(0, True)
                with dve.Fori(1, N) as i:
                    body(i, False)
                tile_out(N - 1, 1)
                dve.wait_ge(y_out, TT)

            @block.gpsimd
            def _(pool):
                pool.memset(h[:, :, I:3 * P], 0.0).then_inc(padded, 1)

                def body(i):
                    for k in range(2):
                        wait(pool, gu_ready, E * (2 * i + k - 1))
                        pool.tensor_copy(xs[:, k, :], XNT[:, bass.ds(P * (2 * i + k), P)]).then_inc(staged, 1)
                        wait(pool, h_ready, E * (2 * i + k - 1))
                        pool.tensor_copy(cs[:, k, :].unsqueeze(1), COMB[:, bass.ds(2 * i + k, 1), :]).then_inc(staged, 1)

                body(0)
                with pool.Fori(1, N) as i:
                    body(i)


def second_attention(nc, sem, w, ident, idb, ps, XNT, Y, loaded_c):
    NG = B * NH1 // 4
    KC = S // P
    SCALE = 1.0 / float(np.sqrt(np.float32(NH1 + DC + DC)))
    NR, MR = 9 * DH1, 96
    KR = MR + 3
    NQ = 3
    with ExitStack() as c0:
        def sb(name, shape, dt=F32):
            return c0.enter_context(nc.sbuf_tensor("sa_" + name, shape, dt))

        VA = sb("VA", [P, NG, KC, 4, DH1 + 1])
        ATT = sb("ATT", [P, B, KC, 4, 4 * DH1])
        parts_q = nc.dram_tensor("parts_q", [NG, 3, 4 * DH1, S], BF16, kind="Internal").ap()
        parts_k = nc.dram_tensor("parts_k", [NG, 3, 4 * DH1, S], BF16, kind="Internal").ap()
        QS, KS = sb("QS", [P, NQ, 4, S], BF16), sb("KS", [P, NQ, 4, S], BF16)
        rows_set, parts_out, att_ready = sem("sa_rows_set"), sem("sa_parts_out"), sem("sa_att_ready")

        with ExitStack() as c:
            def sbi(name, shape, dt=F32):
                return c.enter_context(nc.sbuf_tensor("sp_" + name, shape, dt))

            CT = sbi("CT", [P, NB])
            r1, r2, r3, qk = (sbi(n, [P, NB]) for n in ("r1", "r2", "r3", "qk"))
            rest = sbi("rest", [P, NB])
            SPL = sbi("SPL", [P, 2, 3, NB], BF16)
            ct_psum, ct_ready, q_psum, k_psum, v_psum, q_read, k_read, v_read, dve_done, split = (
                sem("sp_" + n) for n in "ct_psum ct_ready q_psum k_psum v_psum q_read k_read v_read dve_done split".split())
            NJ = TOK // NB

            with nc.Block() as block:
                @block.gpsimd
                def _(pool):
                    pool.memset(VA[:, :, :, :, DH1:DH1 + 1], 1.0).then_inc(rows_set, 1)
                    k = 0
                    for n in range(NQ):
                        for dst, a, b, value in ((QS, 64, MR, 0.0), (KS, 64, MR, 0.0), (KS, MR, KR, 1.0)):
                            k += 1
                            pool.wait_ge(rows_set, k)
                            pool.memset(dst[a:b, n, :, :], value).then_inc(rows_set, 1)

                @block.tensor
                def _(pe):
                    pe.wait_ge(loaded_c, 16)
                    for j in range(NJ):
                        x = XNT[:, NB * j:NB * (j + 1)]
                        wait(pe, ct_ready, j)
                        pe.matmul(ps[:, 0, :], w("Wdown"), x, start=True, stop=True).then_inc(ct_psum, 1)
                        wait(pe, k_read, j)
                        pe.matmul(ps[:, 5, :], w("Wkr"), x, start=True, stop=True)
                        pe.matmul(ps[:, 6, :], w("Wkr_sw"), x, start=True, stop=True)
                        pe.wait_ge(ct_ready, j + 1)
                        wait(pe, q_read, j)
                        for n, name in ((2, "Wqr"), (3, "Wqr_sw"), (1, "Wuq")):
                            ins = pe.matmul(ps[:, n, :], w(name), CT[:, :], start=True, stop=True)
                        ins.then_inc(q_psum, 1)
                        pe.matmul(ps[:, 4, :], w("Wuk"), CT[:, :], start=True, stop=True).then_inc(k_psum, 1)
                        wait(pe, v_read, j)
                        for n in range(4):
                            ins = pe.matmul(ps[:, 7, P * n:P * (n + 1)], CT[:, P * n:P * (n + 1)], w("Wuv"), start=True, stop=True)
                        ins.then_inc(v_psum, 1)

                @block.scalar
                def _(act):
                    for j in range(NJ):
                        act.wait_ge(ct_psum, j + 1)
                        wait(act, v_psum, j)
                        act.activation(CT[:, :], ps[:, 0, :], ACT.Identity, bias=w("b_down")).then_inc(ct_ready, 1)

                @block.vector
                def _(dve):
                    chain = Count(dve_done)

                    def then(ins):
                        dve.wait_ge(dve_done, chain.add(ins))

                    dve.wait_ge(rows_set, 1)
                    for j in range(NJ):
                        pos = slice(NB * (j % 2), NB * (j % 2 + 1))
                        cos, sin = w("cos")[:, pos], w("sin")[:, pos]
                        for k, (bank, psum, read, bs) in enumerate((((1, 2, 3), q_psum, q_read, ("b_uq", "b_qr", "b_qr_sw")),
                                                                    ((4, 5, 6), k_psum, k_read, ("b_uk", "b_kr", "b_kr_sw")))):
                            dve.wait_ge(psum, j + 1)
                            chain.add(dve.scalar_tensor_tensor(out=r1[:, :], in0=ps[:, bank[1], :], scalar=w(bs[1]), in1=cos,
                                                               op0=ALU.add, op1=ALU.mult))
                            then(dve.scalar_tensor_tensor(out=r2[:, :], in0=ps[:, bank[2], :], scalar=w(bs[2]), in1=sin,
                                                          op0=ALU.add, op1=ALU.mult))
                            ins = dve.scalar_tensor_tensor(out=r3[:, :], in0=ps[:, bank[0], :], scalar=w(bs[0]), in1=r1[:, :],
                                                           op0=ALU.add, op1=ALU.add)
                            ins.then_inc(read, 1)
                            dve.wait_ge(read, j + 1)
                            then(dve.tensor_tensor(qk[:, :], r3[:, :], r2[:, :], ALU.add))
                            wait(dve, parts_out, 16 * 8 * j)
                            then(dve.tensor_copy(SPL[:, k, 0, :], qk[:, :]))
                            then(dve.tensor_tensor(rest[:, :], qk[:, :], SPL[:, k, 0, :], ALU.subtract))
                            then(dve.tensor_copy(SPL[:, k, 1, :], rest[:, :]))
                            dve.tensor_tensor(SPL[:, k, 2, :], rest[:, :], SPL[:, k, 1, :], ALU.subtract).then_inc(split, 1)
                            dve.wait_ge(split, 2 * j + k + 1)
                        dve.wait_ge(v_psum, j + 1)
                        b, kc = j // 2, 4 * (j % 2)
                        for n in range(4):
                            ins = dve.tensor_tensor(VA[:, 4 * b:4 * b + 4, kc + n, :, 0:DH1],
                                                    ps[:, 7, P * n:P * (n + 1)].rearrange("p (g h d) -> p g h d", h=4, d=DH1),
                                                    w("b_uv_row").rearrange("p (g h d) -> p g h d", h=4, d=DH1), ALU.add)
                            if n < 3:
                                chain.add(ins)
                        ins.then_inc(v_read, 1)
                    dve.wait_ge(v_read, NJ)

                @block.sync
                def _(sp):
                    for j in range(NJ):
                        b, pos = j // 2, slice(NB * (j % 2), NB * (j % 2 + 1))
                        for k, parts in enumerate((parts_q, parts_k)):
                            sp.wait_ge(split, 2 * j + k + 1)
                            for g in range(4):
                                sp.dma_start(parts[4 * b + g, :, :, pos].rearrange("i f n -> f i n"),
                                             SPL[4 * DH1 * g:4 * DH1 * (g + 1), k, :, :]).then_inc(parts_out, 16)
                    sp.wait_ge(parts_out, 16 * 8 * NJ)

        VG = sb("VG", [P, KC, 4, 32])
        PR = sb("PR", [P, 2, 4, S])
        OU = sb("OU", [P, S])
        MX = sb("MX", [P, 4, KC, 2])
        NM, R1, R2 = sb("NM", [P, KC]), sb("R1", [P, KC]), sb("R2", [P, KC])
        MS = sb("MS", [P, 2, KC, KR], BF16)
        RD = sb("RD", [P, KC, 4])
        (st_ready, st_used, pv_done, s_ready, smax_done, ms_ready, stacked, vg_ready, ou_ready, turned, small_done,
         rd_ready, zeroed) = (sem("sm_" + n) for n in
                              "st_ready st_used pv_done s_ready smax_done ms_ready stacked vg_ready ou_ready turned small_done rd_ready zeroed".split())
        SLOTS = 4 * KC
        IT = SLOTS + 4
        ST, PV = 4, 6
        NSTACK = 18
        NQR = S // 4

        def items(last):
            out = []
            for s in range(SLOTS):
                out.append(("scores", s // 4, s % 4))
                if s == 2:
                    out.append(("maxima", 0, 3))
                if s in (10, 18, 26) and not last:
                    out.append(("maxima", 1, s // 8 - 1))
            return out

        def item_count(g, k, half=1):
            return 2 * (IT * g + 3 + k) + half + 1

        def slot_count(g, s, half=1, last=False):
            return item_count(g, items(last).index(("scores", s // 4, s % 4)), half)

        def maxima_item(g, h):
            if h == 3:
                return item_count(g, 3)
            if isinstance(g, int) and g == 0:
                return 2 * (h + 1)
            return item_count(g - 1, items(False).index(("maxima", 1, h)))

        def sums_in_slot(s):
            if s == 0:
                return [(1, KC - 2, 3)]
            if s in (1, 2, 3, 4):
                return [(1, KC - 1, s - 1)]
            if s in (6, 7, 8):
                return [(0, 0, s - 6)]
            if s == 9:
                return [(0, 0, 3), (0, 1, 0)]
            return [(0, (s - 5) // 4, (s - 5) % 4)] if s > 9 else []

        with nc.Block() as block:
            @block.sync
            def _(sp):
                sp.wait_ge(rows_set, 1 + 3 * NQ)

                def stack(g):
                    wait(sp, stacked, 16 * NSTACK * g)
                    if not (isinstance(g, int) and g < NQ):
                        sp.wait_ge(st_ready, item_count(g - NQ, IT - 1))
                    for i in range(3):
                        for j in range(3):
                            r = DH1 * (3 * i + j)
                            for dst, parts, k in ((QS, parts_q, i), (KS, parts_k, j)):
                                src = parts[g, k, :, :] if isinstance(g, int) else parts[bass.ds(g, 1), k, :, :].rearrange("o f n -> (o f) n")
                                sp.dma_start(dst[r:r + DH1, bass.ds(g % NQ, 1), :, :].rearrange("d o h n -> d (o h) n"),
                                             src.rearrange("(h d) n -> d h n", d=DH1)).then_inc(stacked, 16)

                for g in range(NQ):
                    stack(g)
                with sp.Fori(NQ, NG) as g:
                    stack(g)

            @block.gpsimd
            def _(pool):
                pool.memset(VG[:, :, :, :], 0.0).then_inc(zeroed, 1)
                pool.memset(MS[:, :, :, :], 0.0).then_inc(zeroed, 1)
                pool.wait_ge(zeroed, 2)

                def values(g):
                    wait(pool, pv_done, SLOTS * g)
                    pool.tensor_copy(VG[:, :, :, 0:DH1 + 1],
                                     VA[:, bass.ds(g, 1), :, :, :].rearrange("p o k h d -> p (o k) h d")).then_inc(vg_ready, 1)

                values(0)
                with pool.Fori(1, NG) as g:
                    values(g)

            @block.tensor
            def _(pe):
                pe.wait_ge(zeroed, 2)

                def row_scores(g, x):
                    h, qt, par = x // KC, x % KC, g % NQ
                    if x == 0:
                        wait(pe, stacked, 16 * NSTACK * (g + 1))
                    wait(pe, smax_done, SLOTS * g + x - 1)
                    for n in range(2):
                        ins = pe.matmul(ps[:, 2 * (x % 2) + n, :], QS[0:MR, bass.ds(par, 1), h, P * qt:P * (qt + 1)].rearrange("p o n -> p (o n)"),
                                        KS[0:MR, bass.ds(par, 1), h, NB * n:NB * (n + 1)].rearrange("p o n -> p (o n)"),
                                        start=True, stop=True)
                    ins.then_inc(s_ready, 1)

                def maxima_rows(g, h, at):
                    wait(pe, ms_ready, 4 * g + h + 1)
                    for n in range(2):
                        wait(pe, st_used, at + n - 2)
                        for qt in range(4 * n, 4 * n + 4):
                            ins = pe.matmul(ps[0:KR, ST + n, P * (qt % 4):P * (qt % 4 + 1)], MS[:, h % 2, qt, :], idb[:, :],
                                            start=True, stop=True)
                        ins.then_inc(st_ready, 1)

                def key_scores(g, kc, h, at):
                    par = g % NQ
                    if kc == 0:
                        wait(pe, st_used, maxima_item(g, h))
                    for n in range(2):
                        wait(pe, st_used, at + n - 2)
                        pe.matmul(ps[:, ST + n, :], KS[0:KR, bass.ds(par, 1), h, P * kc:P * (kc + 1)].rearrange("p o n -> p (o n)"),
                                  QS[0:KR, bass.ds(par, 1), h, NB * n:NB * (n + 1)].rearrange("p o n -> p (o n)"),
                                  start=True, stop=True).then_inc(st_ready, 1)

                def values(g, kc, q, last=False):
                    if q == 0:
                        wait(pe, st_used, slot_count(g, 4 * kc + 3, 1, last))
                    if kc == 0:
                        wait(pe, vg_ready, g + 1)
                        wait(pe, rd_ready, 4 * (g - 1) + (4 if q > 1 else 2))
                    for h in range(4):
                        ins = pe.matmul(ps[32 * h:32 * (h + 1), PV + q // 2, NQR * (q % 2):NQR * (q % 2 + 1)], VG[:, kc, h, :],
                                        PR[:, kc % 2, h, NQR * q:NQR * (q + 1)], start=(kc == 0 and q % 2 == 0),
                                        stop=(kc == KC - 1), tile_position=(0, 32 * h), skip_group_check=True)
                    ins.then_inc(pv_done, 1)

                def turn(g, n):
                    wait(pe, ou_ready, 2 * g + n + 1)
                    for qt in range(4):
                        ins = pe.transpose(ps[:, PV + n, P * qt:P * (qt + 1)], OU[:, NB * n + P * qt:NB * n + P * (qt + 1)], ident)
                    ins.then_inc(turned, 1)

                def body(g, first, last):
                    s = 0
                    for k, (kind, kc, h) in enumerate(items(last)):
                        at = item_count(g, k, 0)
                        if kind == "maxima":
                            maxima_rows(g + kc, h, at)
                            continue
                        if s in (4, 6) and not first:
                            turn(g - 1, s // 2 - 2)
                        for back, chunk, q in sums_in_slot(s):
                            if not (first and back):
                                values(g - back, chunk, q, last and not back)
                        key_scores(g, kc, h, at)
                        if not last:
                            row_scores(g + 1, s)
                        s += 1

                for h in range(4):
                    for qt in range(KC):
                        row_scores(0, KC * h + qt)
                    if h:
                        maxima_rows(0, h - 1, 2 * h - 1)
                body(0, True, False)
                with pe.Fori(1, NG - 1) as g:
                    body(g, False, False)
                body(NG - 1, False, True)
                values(NG - 1, KC - 2, 3, True)
                for q in range(4):
                    values(NG - 1, KC - 1, q, True)
                for n in range(2):
                    turn(NG - 1, n)

            @block.scalar
            def _(act):
                def rows_out(g, h, at):
                    for n in range(2):
                        act.wait_ge(st_ready, at + n)
                        act.activation(QS[MR:KR, bass.ds(g % NQ, 1), h, NB * n:NB * (n + 1)], ps[MR:KR, ST + n, :].unsqueeze(1),
                                       ACT.Copy).then_inc(st_used, 1)

                def sums_out(g, n):
                    wait(act, pv_done, SLOTS * g + 4 * (KC - 1) + 2 * (n + 1))
                    act.activation(OU[:, NB * n:NB * (n + 1)], ps[:, PV + n, :], ACT.Copy).then_inc(ou_ready, 1)

                def body(g, first, last):
                    s = 0
                    for k, (kind, kc, h) in enumerate(items(last)):
                        at = item_count(g, k, 0)
                        if kind == "maxima":
                            rows_out(g + kc, h, at)
                            continue
                        for n in range(2):
                            act.wait_ge(st_ready, at + n)
                            wait(act, pv_done, SLOTS * g + 4 * (kc - 2) + 2 * (n + 1))
                            act.activation(PR[:, kc % 2, h, NB * n:NB * (n + 1)], ps[:, ST + n, :], ACT.Exp,
                                           scale=SCALE).then_inc(st_used, 1)
                        if s in (3, 5) and not first:
                            sums_out(g - 1, (s - 3) // 2)
                        s += 1

                for h in range(3):
                    rows_out(0, h, 2 * h + 1)
                body(0, True, False)
                with act.Fori(1, NG - 1) as g:
                    body(g, False, False)
                body(NG - 1, False, True)
                for n in range(2):
                    sums_out(NG - 1, n)

            @block.vector
            def _(dve):
                dve.wait_ge(zeroed, 2)

                def row_maxima(g, x):
                    h, qt = x // KC, x % KC
                    wait(dve, s_ready, SLOTS * g + x + 1)
                    if qt == 0:
                        wait(dve, small_done, 4 * (4 * g + h) - 12)
                    dve.tensor_reduce(MX[:, h, qt, :], ps[:, 2 * (x % 2):2 * (x % 2) + 2, :], AX.X, ALU.max).then_inc(smax_done, 1)

                def split_maxima(g, h):
                    par, base = h % 2, 4 * (4 * g + h)
                    wait(dve, smax_done, SLOTS * g + KC * (h + 1))
                    if not (isinstance(g, int) and g == 0 and h < 2):
                        wait(dve, st_ready, maxima_item(g, h - 2) if h >= 2 else maxima_item(g - 1, h + 2))
                    dve.tensor_reduce(NM[:, :], MX[:, h, :, :], AX.X, ALU.max, negate=True).then_inc(small_done, 1)
                    dve.wait_ge(small_done, base + 1)
                    dve.tensor_copy(MS[:, par, :, MR:MR + 1], NM[:, :].unsqueeze(2)).then_inc(small_done, 1)
                    dve.wait_ge(small_done, base + 2)
                    dve.tensor_tensor(R1[:, :].unsqueeze(2), NM[:, :].unsqueeze(2), MS[:, par, :, MR:MR + 1], ALU.subtract).then_inc(small_done, 1)
                    dve.wait_ge(small_done, base + 3)
                    dve.tensor_copy(MS[:, par, :, MR + 1:MR + 2], R1[:, :].unsqueeze(2)).then_inc(small_done, 1)
                    dve.wait_ge(small_done, base + 4)
                    dve.tensor_tensor(MS[:, par, :, MR + 2:MR + 3], R1[:, :].unsqueeze(2), MS[:, par, :, MR + 1:MR + 2],
                                      ALU.subtract).then_inc(ms_ready, 1)

                def divide(g, n):
                    wait(dve, turned, 2 * g + n + 1)
                    sums = ps[:, PV + n, :].rearrange("p (q h d) -> p q h d", h=4, d=32)
                    rd = RD[:, 4 * n:4 * n + 4, :].unsqueeze(3)
                    dve.reciprocal(rd, sums[:, :, :, DH1:DH1 + 1]).then_inc(rd_ready, 1)
                    dve.wait_ge(rd_ready, 4 * g + 2 * n + 1)
                    dve.tensor_tensor(ATT[:, bass.ds(g // 4, 1), 4 * n:4 * n + 4, bass.ds(g % 4, 1), :].rearrange("p o q r (h d) -> p (o q r) h d", h=4),
                                      sums[:, :, :, 0:DH1], rd.to_broadcast([P, 4, 4, DH1]), ALU.mult).then_inc(rd_ready, 1)

                def body(g, first, last):
                    for x in range(SLOTS):
                        if not last:
                            row_maxima(g + 1, x)
                            if x % KC == KC - 1:
                                split_maxima(g + 1, x // KC)
                        if x in (4, 6) and not first:
                            divide(g - 1, x // 2 - 2)

                for x in range(SLOTS):
                    row_maxima(0, x)
                    if x % KC == KC - 1:
                        split_maxima(0, x // KC)
                body(0, True, False)
                with dve.Fori(1, NG - 1) as g:
                    body(g, False, False)
                body(NG - 1, False, True)
                for n in range(2):
                    divide(NG - 1, n)
                dve.wait_ge(rd_ready, 4 * NG)

        attT = sb("attT", [P, 2, 4, P])
        t_ready, t_out, o_ready, y_ready = sem("so_t_ready"), sem("so_t_out"), sem("so_o_ready"), sem("so_y_ready")
        with nc.Block() as block:
            @block.tensor
            def _(pe):
                for j in range(TT // 4):
                    wait(pe, t_out, j - 1)
                    for n in range(4):
                        b, qt = (4 * j + n) // KC, (4 * j + n) % KC
                        ins = pe.transpose(ps[:, j % 2, P * n:P * (n + 1)], ATT[:, b, qt, :, :].rearrange("p g f -> p (g f)"), ident)
                    ins.then_inc(t_ready, 1)
                    pe.wait_ge(t_out, j + 1)
                    wait(pe, y_ready, j - 1)
                    for n in range(4):
                        ins = pe.matmul(ps[:, 2 + j % 2, P * n:P * (n + 1)], attT[:, j % 2, n, :], w("WoL1"), start=True, stop=True)
                    ins.then_inc(o_ready, 1)

            @block.scalar
            def _(act):
                for j in range(TT // 4):
                    act.wait_ge(t_ready, j + 1)
                    wait(act, o_ready, j - 1)
                    act.activation(attT[:, j % 2, :, :], ps[:, j % 2, :].rearrange("p (t d) -> p t d", d=P), ACT.Copy).then_inc(t_out, 1)

            @block.vector
            def _(dve):
                for j in range(TT // 4):
                    dve.wait_ge(o_ready, j + 1)
                    dve.tensor_tensor(Y[:, 4 * j:4 * j + 4, :], ps[:, 2 + j % 2, :].rearrange("p (t d) -> p t d", d=D),
                                      w("b_o_row").unsqueeze(1).to_broadcast([P, 4, D]), ALU.add).then_inc(y_ready, 1)
                dve.wait_ge(y_ready, TT // 4)


def channel_mix(nc, sem, w, ident, ps, XNT, Y):
    NJ = TOK // NB
    with ExitStack() as c:
        def sb(name, shape, dt=F32):
            return c.enter_context(nc.sbuf_tensor("cm_" + name, shape, dt))

        om = sb("om", [P, 2])
        pr, pk = sb("pr", [P, TOK]), sb("pk", [P, TOK])
        xr, xk = sb("xr", [P, TOK]), sb("xk", [P, TOK])
        r, kr, ka, o = sb("r", [P, 2, NB]), sb("kr", [P, 2, NB]), sb("ka", [P, 2, NB]), sb("o", [P, 2, NB])
        one_minus, shifted, zero, mixed = sem("cm_one_minus"), sem("cm_shifted"), sem("cm_zero"), sem("cm_mixed")
        rk_ready, r_out, k_out, ka_ready, v_ready, o_ready, turned, y_ready = (
            sem("cm_" + n) for n in "rk_ready r_out k_out ka_ready v_ready o_ready turned y_ready".split())

        with nc.Block() as block:
            @block.vector
            def _(dve):
                dve.tensor_scalar(om[:, 0:1], w("mu_r"), -1.0, 1.0, ALU.mult, ALU.add).then_inc(one_minus, 1)
                dve.tensor_scalar(om[:, 1:2], w("mu_k"), -1.0, 1.0, ALU.mult, ALU.add).then_inc(one_minus, 1)
                dve.wait_ge(one_minus, 2)
                dve.wait_ge(zero, 4)
                for b in range(B):
                    for n, dst in enumerate((pr, pk)):
                        dve.tensor_scalar(dst[:, S * b + 1:S * (b + 1)], XNT[:, S * b:S * (b + 1) - 1], om[:, n:n + 1], None,
                                          ALU.mult).then_inc(shifted, 1)
                for b in range(B):
                    for h in range(2):
                        a = S * b + NB * h
                        dve.wait_ge(shifted, 2 * (b + 1))
                        for mu, p, x in (("mu_r", pr, xr), ("mu_k", pk, xk)):
                            dve.scalar_tensor_tensor(out=x[:, a:a + NB], in0=XNT[:, a:a + NB], scalar=w(mu), in1=p[:, a:a + NB],
                                                     op0=ALU.mult, op1=ALU.add).then_inc(mixed, 1)
                for j in range(NJ):
                    dve.wait_ge(k_out, j + 1)
                    wait(dve, v_ready, j - 1)
                    dve.tensor_tensor(ka[:, j % 2, :], kr[:, j % 2, :], kr[:, j % 2, :], ALU.mult).then_inc(ka_ready, 1)
                    dve.wait_ge(v_ready, j + 1)
                    dve.wait_ge(r_out, j + 1)
                    wait(dve, turned, j - 1)
                    dve.tensor_tensor(o[:, j % 2, :], r[:, j % 2, :], ps[:, 4 + j % 2, :], ALU.mult).then_inc(o_ready, 1)

            @block.gpsimd
            def _(pool):
                for b in range(B):
                    for dst in (pr, pk):
                        pool.memset(dst[:, S * b:S * b + 1], 0.0).then_inc(zero, 1)

            @block.tensor
            def _(pe):
                def rk(j):
                    pe.wait_ge(mixed, 2 * (j + 1))
                    wait(pe, r_out, j - 1)
                    wait(pe, k_out, j - 1)
                    pe.matmul(ps[:, j % 2, :], w("W_rT"), xr[:, NB * j:NB * (j + 1)], start=True, stop=True)
                    pe.matmul(ps[:, 2 + j % 2, :], w("W_kT"), xk[:, NB * j:NB * (j + 1)], start=True, stop=True).then_inc(rk_ready, 1)

                rk(0)
                for j in range(NJ):
                    if j + 1 < NJ:
                        rk(j + 1)
                    pe.wait_ge(ka_ready, j + 1)
                    wait(pe, o_ready, j - 1)
                    pe.matmul(ps[:, 4 + j % 2, :], w("W_vT"), ka[:, j % 2, :], start=True, stop=True).then_inc(v_ready, 1)
                    pe.wait_ge(o_ready, j + 1)
                    wait(pe, y_ready, j - 1)
                    for n in range(4):
                        ins = pe.transpose(ps[:, 6 + j % 2, P * n:P * (n + 1)], o[:, j % 2, P * n:P * (n + 1)], ident)
                    ins.then_inc(turned, 1)

            @block.scalar
            def _(act):
                for j in range(NJ):
                    act.wait_ge(rk_ready, j + 1)
                    wait(act, ka_ready, j - 1)
                    act.activation(kr[:, j % 2, :], ps[:, 2 + j % 2, :], ACT.Relu).then_inc(k_out, 1)
                    wait(act, o_ready, j - 1)
                    act.activation(r[:, j % 2, :], ps[:, j % 2, :], ACT.Sigmoid).then_inc(r_out, 1)
                    act.wait_ge(turned, j + 1)
                    act.activation(Y[:, 4 * j:4 * j + 4, :], ps[:, 6 + j % 2, :].rearrange("p (t d) -> p t d", d=D),
                                   ACT.Copy).then_inc(y_ready, 1)
                act.wait_ge(y_ready, NJ)


def _packed(pack, parts):
    cols = []
    for name, n in pack:
        a = np.asarray(parts[name])
        full = np.zeros((P, n), np.float32)
        full[:a.shape[0], :] = a.reshape(a.shape[0], n)
        cols.append(full)
    return np.ascontiguousarray(np.concatenate(cols, axis=1))


def _layout(x):
    def col(v):
        return np.asarray(v).reshape(-1, 1)

    def rows(v, n=P):
        return np.broadcast_to(np.asarray(v).reshape(1, -1), (n, np.asarray(v).size))

    def low(a):
        return np.concatenate([a, np.zeros((P - a.shape[0], a.shape[1]), a.dtype)], 0)

    def high(a):
        return np.concatenate([np.zeros((P - a.shape[0], a.shape[1]), a.dtype), a], 0)

    g = {k: np.asarray(v) for k, v in x.items()}
    pair = np.arange(D) ^ 1
    b1row = np.zeros((P, HID), np.float32)
    b1row[[0, 32, 64]] = g["L0_attn_b1"]
    masks, ones3 = _constants()
    a = {
        "masks": masks, "ones3": ones3,
        "woT": g["L0_attn_wo"].T, "wqT": g["L0_attn_wq"].T, "wkT": g["L0_attn_wk"].T, "wvT": g["L0_attn_wv"].T,
        "ident": np.eye(P, dtype=np.float32),
        "headmask": (np.arange(P)[:, None] // DH0 == np.arange(NH0)).astype(np.float32),
        "b1row": b1row, "b2row": rows(g["L0_attn_b2"]), "alpha": rows(g["L0_attn_alpha"]), "theta": rows(g["L0_attn_theta"]),
        "b1col": g["L0_attn_b1"].reshape(HC, P).T, "b2col": col(g["L0_attn_b2"]), "ones": np.ones((P, 1), np.float32),
        "w1T": g["L0_attn_w1"].T, "w2": g["L0_attn_w2"],
        "w2T": g["L0_attn_w2"].T.reshape(HC, P, D).transpose(1, 0, 2).reshape(P, HID),
    }
    wd = np.zeros((E, 3 * P, D), np.float32)
    wd[:, :I] = g["L0_ffn_Wd"].transpose(0, 2, 1)
    b = {
        "lin1T": g["L0_attn_lin1"].T, "lin2T": g["L0_attn_lin2"].T, "routerT": g["L0_ffn_router_w"].T,
        "expert_no": rows(np.arange(E, dtype=np.float32)),
        "WgT": g["L0_ffn_Wg"].transpose(2, 0, 1).reshape(D, E * I), "WuT": g["L0_ffn_Wu"].transpose(2, 0, 1).reshape(D, E * I),
        "WdT": wd.reshape(E, 3, P, D).transpose(2, 0, 1, 3).reshape(P, E * 3 * D),
    }
    theta = np.float32(10000.0) ** (np.float32(-2.0) * np.arange(D // 2, dtype=np.float32)) / np.float32(D // 2)
    angle = (np.arange(S, dtype=np.float32)[:, None] * theta[None, :]).astype(np.float64)
    cos, sin = np.cos(angle).astype(np.float32), np.sin(angle).astype(np.float32)
    sin_signed = np.repeat(sin.T, 2, axis=0)
    sin_signed[0::2] = -sin_signed[0::2]
    q = {k[8:]: v for k, v in g.items() if k.startswith("L1_attn_")}
    cc = {
        "Wdown": np.concatenate([q["Wd_q_w"], q["Wd_kv_w"]], 1),
        "Wuq": low(q["Wu_q_w"]), "Wqr": low(q["Wq_r_w"]), "Wqr_sw": low(q["Wq_r_w"][:, pair]),
        "Wuk": high(q["Wu_k_w"]), "Wkr": q["Wk_r_w"], "Wkr_sw": q["Wk_r_w"][:, pair], "Wuv": high(q["Wu_v_w"]),
        "b_down": col(np.concatenate([q["Wd_q_b"], q["Wd_kv_b"]])), "b_uq": col(q["Wu_q_b"]), "b_qr": col(q["Wq_r_b"]),
        "b_qr_sw": col(q["Wq_r_b"][pair]), "b_uk": col(q["Wu_k_b"]), "b_kr": col(q["Wk_r_b"]), "b_kr_sw": col(q["Wk_r_b"][pair]),
        "b_uv_row": rows(q["Wu_v_b"]), "WoL1": q["Wo_w"], "b_o_row": rows(q["Wo_b"]),
        "cos": np.repeat(cos.T, 2, axis=0), "sin": sin_signed,
        "W_rT": g["L1_ffn_W_r"].T, "W_kT": g["L1_ffn_W_k"].T, "W_vT": g["L1_ffn_W_v"].T,
        "mu_r": col(g["L1_ffn_mu_r"]), "mu_k": col(g["L1_ffn_mu_k"]),
    }
    return _packed(PACK_A, a), _packed(PACK_B, b), _packed(PACK_C, cc)


def _constants():
    r, k = np.arange(P)[:, None], np.arange(KW)[None, :]
    seen = (k > r) & (k <= r + WIN)
    tiles = [seen, seen & (k >= NPM), seen & ((r < NPM) | (k >= P))]
    ones3 = np.zeros((P, P), np.float32)
    ones3[[0, 32, 64]] = 1
    return np.concatenate([np.where(m, 0.0, -2.0 ** 100) for m in tiles], 1).astype(np.float32), ones3


def kernel(**inputs):
    import concourse.bacc as bacc
    from concourse.bass_utils import run_bass_kernel_spmd

    pack_a, pack_b, pack_c = _layout({k: v for k, v in inputs.items() if k not in ("L0_attn_x", "L0_attn_mem")})
    arrays = {"pack_a": pack_a, "pack_b": pack_b, "pack_c": pack_c,
              "x_in": np.ascontiguousarray(np.asarray(inputs["L0_attn_x"]).reshape(TOK, D)),
              "mem": np.ascontiguousarray(np.asarray(inputs["L0_attn_mem"]))}
    nc = bacc.Bacc("TRN2", target_bir_lowering=False, num_devices=1)
    aps = [nc.dram_tensor(n, a.shape, mybir.dt.from_np(a.dtype), kind="ExternalInput").ap() for n, a in arrays.items()]
    out = nc.dram_tensor("out", [TOK, D], F32, kind="ExternalOutput").ap()
    build(nc, *aps, out)
    r = run_bass_kernel_spmd(nc, [arrays], core_ids=[0])
    return r.results[0]["out"].reshape(B, S, D)
```

```python
from contextlib import ExitStack

import numpy as np

import concourse.bass as bass
from concourse import mybir

F32 = mybir.dt.float32
BF16 = mybir.dt.bfloat16
U32 = mybir.dt.uint32
ALU = mybir.AluOpType
ACT = mybir.ActivationFunctionType
AX = mybir.AxisListType

P = 128
B, S, D = 2, 1024, 128
NPM = 64
SM = S + NPM
ROWS = B * SM
T0 = ROWS // P
TOK = B * S
TT = TOK // P
HID = 512
HC = HID // P
NH0, DH0, WIN = 4, 32, 64
KW = P + WIN
PADC = P * (T0 + 1)
E, TOPK, I = 8, 2, 352
NH1, DH1 = 16, 8
DC = 64
NB = 512
EPS = 1e-5

PACK_A = [("woT", D), ("wqT", D), ("wkT", D), ("wvT", D), ("ident", P), ("headmask", NH0), ("b1row", HID),
          ("b2row", D), ("alpha", 1), ("theta", 1), ("b1col", HC), ("b2col", 1), ("ones", 1), ("masks", 3 * KW), ("ones3", P),
          ("w1T", HID), ("w2", HID), ("w2T", HID)]
PACK_B = [("lin1T", D), ("lin2T", D), ("routerT", E), ("expert_no", E),
          ("WgT", E * I), ("WuT", E * I), ("WdT", E * I // P * D)]
PACK_C = [("Wdown", D), ("Wuq", D), ("Wqr", D), ("Wqr_sw", D), ("Wuk", D), ("Wkr", D), ("Wkr_sw", D), ("Wuv", D),
          ("b_down", 1), ("b_uq", 1), ("b_qr", 1), ("b_qr_sw", 1), ("b_uk", 1), ("b_kr", 1), ("b_kr_sw", 1),
          ("b_uv_row", D), ("WoL1", D), ("b_o_row", D), ("cos", S), ("sin", S),
          ("W_rT", D), ("W_kT", D), ("W_vT", D), ("mu_r", 1), ("mu_k", 1)]


def offsets(pack):
    at, out = 0, {}
    for name, n in pack:
        out[name] = (at, n)
        at += n
    return out, at


class Count:

    def __init__(self, sem):
        self.sem, self.n = sem, 0

    def add(self, ins):
        self.n += 1
        ins.then_inc(self.sem, 1)
        return self.n


def build(nc, packA, packB, packC, x_in, mem, out):
    offA, nA = offsets(PACK_A)
    offB, nB = offsets(PACK_B)
    offC, nC = offsets(PACK_C)
    ctx = ExitStack()
    with ctx:
        def sb(name, shape, dt=F32, c=ctx):
            return c.enter_context(nc.sbuf_tensor(name, shape, dt))

        def sem(name):
            return ctx.enter_context(nc.semaphore(name))

        WA = sb("WA", [P, nA])
        WB = sb("WB", [P, nB])
        held = [(offA, WA), (offB, WB)]

        def w(name):
            for off, t in held:
                if name in off:
                    a, n = off[name]
                    return t[:, a:a + n]

        ident = w("ident")
        idb = sb("idb", [P, P], BF16)
        X = sb("X", [P, TT, D])
        Y = sb("Y", [P, TT, D])
        stats, mv = sb("y_stats", [P, TT, 6]), sb("y_mv", [P, TT, 2])
        epsc = sb("epsc", [P, 1])
        ps = ctx.enter_context(nc.psum_tensor("ps", [P, 8, NB], F32))
        loaded_a, loaded_b, loaded_c, loaded_x = sem("loaded_a"), sem("loaded_b"), sem("loaded_c"), sem("loaded_x")

        y_summed, y_stats_done = sem("y_summed"), sem("y_stats_done")
        norm_sems = {n: sem("rn_" + n) for n in NORM_SEMS}

        def y_statistics(k):
            return RowStatistics(stats, mv, y_summed, y_stats_done, TT * k)

        first_layer(nc, sem, w, ident, idb, ps, X, Y, y_statistics(0), epsc, WA, WB, packA, packB, x_in, mem,
                    loaded_a, loaded_b, loaded_x)
        WC = sb("WC", [P, nC])
        held.append((offC, WC))
        XNT = sb("XNT", [P, TOK])
        residual_norm(nc, norm_sems, ident, ps, X, Y, mv, XNT, epsc, 0)
        experts(nc, sem, w, ident, ps, XNT, Y, y_statistics(1), loaded_b, WC, packC, loaded_c)
        residual_norm(nc, norm_sems, ident, ps, X, Y, mv, XNT, epsc, 1)
        second_attention(nc, sem, w, ident, idb, ps, XNT, Y, y_statistics(2), loaded_c)
        residual_norm(nc, norm_sems, ident, ps, X, Y, mv, XNT, epsc, 2)
        channel_mix(nc, sem, w, ident, ps, XNT, Y, y_statistics(3))
        residual_norm(nc, norm_sems, ident, ps, X, Y, mv, None, epsc, 3, out)


def norm_statistics(dve, chain, src, tiles, stats, mv):
    for t in range(tiles):
        last = chain.add(dve.bn_stats(stats[:, t, :], src[:, t, :]))
    for t in range(tiles):
        dve.wait_ge(chain.sem, last - tiles + 1 + t)
        n = chain.add(dve.bn_aggr(mv[:, t, :], stats[:, t, :]))
    return n


class RowStatistics:

    def __init__(self, stats, mv, summed, done, base):
        self.stats, self.mv, self.summed, self.done, self.base = stats, mv, summed, done, base

    def sums(self, dve, src, j):
        for n in range(4):
            dve.bn_stats(self.stats[:, bass.ds(4 * j + n, 1), :].rearrange("p o k -> p (o k)"),
                         src[:, bass.ds(4 * j + n, 1), :].rearrange("p o k -> p (o k)")).then_inc(self.summed, 1)

    def results(self, dve, j):
        for t in range(4 * j, 4 * j + 4):
            dve.wait_ge(self.summed, self.base + t + 1)
            dve.bn_aggr(self.mv[:, t, :], self.stats[:, t, :]).then_inc(self.done, 1)

    def block(self, dve, src, j):
        self.sums(dve, src, j)
        self.results(dve, j)

    def wait_all(self, dve):
        dve.wait_ge(self.done, self.base + TT)


NORM_SEMS = {"std_ready": TT // 4, "factors": TT // 2, "std2_ready": TT // 4, "factors2": TT // 2, "xp_ready": TT, "x_summed": TT, "x_stats": TT,
             "x_ready": TT // 4, "xn_ready": TT - 4, "xn_last": 4, "turned": TT // 4, "evac": TT // 4, "stored": 0}


def residual_norm(nc, sems, ident, ps, X, Y, mv, XNT, epsc, number, out=None):
    NJ = TT // 4
    with ExitStack() as c:
        def sb(name, shape, dt=F32):
            return c.enter_context(nc.sbuf_tensor("r%d_" % number + name, shape, dt))

        std, rstd, shift = sb("std", [P, TT, 1]), sb("rstd", [P, TT, 1]), sb("shift", [P, TT, 1])
        stats2, mv2 = sb("stats2", [P, TT, 6]), sb("mv2", [P, TT, 2])
        std2, rstd2, shift2 = sb("std2", [P, TT, 1]), sb("rstd2", [P, TT, 1]), sb("shift2", [P, TT, 1])
        XP = sb("XP", [P, TT, D])
        XN = sb("XN", [P, TT, D])

        def at_least(eng, name, value):
            eng.wait_ge(sems[name], NORM_SEMS[name] * number + value)

        block = c.enter_context(nc.Block())
        four = [slice(4 * j, 4 * j + 4) for j in range(NJ)]

        @block.vector
        def _(dve):
            own = RowStatistics(stats2, mv2, sems["x_summed"], sems["x_stats"], TT * number)

            def factors(j, src, std, rstd, shift, deviation, ready):
                at_least(dve, deviation, j + 1)
                dve.reciprocal(rstd[:, four[j], :], std[:, four[j], :]).then_inc(sems[ready], 1)
                at_least(dve, ready, 2 * j + 1)
                dve.scalar_tensor_tensor(out=shift[:, four[j], :], in0=src[:, four[j], 0:1], scalar=-1.0, in1=rstd[:, four[j], :],
                                         op0=ALU.mult, op1=ALU.mult).then_inc(sems[ready], 1)

            def factors_y(j):
                factors(j, mv, std, rstd, shift, "std_ready", "factors")

            def sum_x(j):
                for t in range(4 * j, 4 * j + 4):
                    dve.scalar_tensor_tensor(out=XP[:, t, :], in0=Y[:, t, :], scalar=rstd[:, t, :], in1=X[:, t, :],
                                             op0=ALU.mult, op1=ALU.add).then_inc(sems["xp_ready"], 1)
                at_least(dve, "xp_ready", 4 * j + 4)
                own.block(dve, XP, j)

            def factors_x(j):
                factors(j, mv2, std2, rstd2, shift2, "std2_ready", "factors2")

            for j in range(NJ):
                factors_y(j)
            for j in range(NJ):
                if out is None:
                    sum_x(j)
                    if j:
                        factors_x(j - 1)
                else:
                    at_least(dve, "xp_ready", 4 * j + 4)
                    dve.tensor_tensor(X[:, four[j], :], X[:, four[j], :], XP[:, four[j], :], ALU.add).then_inc(sems["x_ready"], 1)
            if out is None:
                factors_x(NJ - 1)
                at_least(dve, "factors2", 2 * NJ)
                for t in range(4 * (NJ - 1), TT):
                    dve.tensor_scalar(XN[:, t, :], XP[:, t, :], rstd2[:, t, :], shift2[:, t, :], ALU.mult,
                                      ALU.add).then_inc(sems["xn_last"], 1)

        @block.scalar
        def _(act):
            def scaled(dst, src, scale, bias, ready):
                for t in range(4 * j, 4 * j + 4):
                    act.activation(dst[:, t, :], src[:, t, :], ACT.Identity, bias=bias[:, t, :], scale=scale[:, t, :]).then_inc(sems[ready], 1)

            for j in range(NJ):
                act.activation(std[:, four[j], :], mv[:, four[j], 1:2], ACT.Sqrt, bias=epsc[:, :]).then_inc(sems["std_ready"], 1)
            if out is not None:
                for j in range(NJ):
                    at_least(act, "factors", 2 * j + 2)
                    scaled(XP, Y, rstd, shift, "xp_ready")
            else:
                def deviation(j):
                    at_least(act, "x_stats", 4 * j + 4)
                    act.activation(std2[:, four[j], :], mv2[:, four[j], 1:2], ACT.Sqrt, bias=epsc[:, :]).then_inc(sems["std2_ready"], 1)

                deviation(0)
                for j in range(NJ):
                    if j + 1 < NJ:
                        deviation(j + 1)
                    if j + 1 < NJ:
                        at_least(act, "factors2", 2 * j + 2)
                        scaled(XN, XP, rstd2, shift2, "xn_ready")
                    if j:
                        at_least(act, "turned", j)
                        act.activation(XNT[:, NB * (j - 1):NB * j], ps[:, j - 1, :], ACT.Copy).then_inc(sems["evac"], 1)
                at_least(act, "turned", NJ)
                act.activation(XNT[:, NB * (NJ - 1):NB * NJ], ps[:, NJ - 1, :], ACT.Copy).then_inc(sems["evac"], 1)
                at_least(act, "evac", NJ)

        @block.gpsimd
        def _(pool):
            if out is None:
                for j in range(NJ):
                    at_least(pool, "factors", 2 * j + 2)
                    at_least(pool, "xp_ready", 4 * j + 4)
                    pool.tensor_tensor(X[:, four[j], :], XP[:, four[j], :], shift[:, four[j], :].to_broadcast([P, 4, D]),
                                       ALU.add).then_inc(sems["x_ready"], 1)
                at_least(pool, "x_ready", NJ)

        @block.tensor
        def _(pe):
            if out is None:
                for t in range(TT):
                    if t < TT - 4:
                        at_least(pe, "xn_ready", t + 1)
                    else:
                        at_least(pe, "xn_last", t + 1 - (TT - 4))
                    ins = pe.transpose(ps[:, t // 4, P * (t % 4):P * (t % 4 + 1)], XN[:, t, :], ident)
                    if t % 4 == 3:
                        ins.then_inc(sems["turned"], 1)

        @block.sync
        def _(sp):
            if out is not None:
                rows = out.rearrange("(t p) d -> p t d", p=P)
                for j in range(NJ):
                    at_least(sp, "x_ready", j + 1)
                    sp.dma_start(rows[:, four[j], :], X[:, four[j], :]).then_inc(sems["stored"], 16)
                at_least(sp, "stored", 16 * NJ)


def first_layer(nc, sem, w, ident, idb, ps, X, Y, y_stat, epsc, WA, WB, packA, packB, x_in, mem,
                loaded_a, loaded_b, loaded_x):
    SCALE = 1.0 / float(np.sqrt(DH0).astype(np.float32))
    with ExitStack() as c0:
        def sb(name, shape, dt=F32):
            return c0.enter_context(nc.sbuf_tensor(name, shape, dt))

        XT = sb("XT", [P, PADC])
        OT = sb("OT", [P, ROWS])
        dzsum = sb("dzsum", [P, HID])
        errsum = sb("errsum", [P, D])
        G1, G2 = ps[:, 6, :], ps[:, 7, :]
        with ExitStack() as c:
            def sbi(name, shape, dt=F32):
                return c.enter_context(nc.sbuf_tensor(name, shape, dt))

            XR = sbi("XR", [P, T0, D])
            XN = sbi("XN", [P, T0, D])
            KM = sbi("KM", [P, NH0, PADC])
            QT = sbi("QT", [P, PADC])
            V = sbi("V", [P, T0 + 1, D])
            masks = sbi("masks", [P, 3, 2, KW], BF16)
            ones_b = sbi("ones_b", [P, P], BF16)
            stats, mv = sbi("stats", [P, T0, 6]), sbi("mv", [P, T0, 2])
            std, rstd = sbi("std", [P, T0, 1]), sbi("rstd", [P, T0, 1])
            b1s = sbi("b1s", [P, HID], BF16)
            b1t = sbi("b1t", [P, 2, HID])
            b1h = sbi("b1h", [P, 2, HID], BF16)
            nwoT = sbi("nwoT", [P, D])
            mem_in, dve_done, var_ready, std_ready = (sem("mem_in"), sem("l0_dve_done"), sem("l0_var_ready"),
                                                      sem("l0_std_ready"))
            x_padded = sem("x_padded")
            xn_ready, turned, xt_ready = sem("l0_xn_ready"), sem("l0_turned"), sem("l0_xt_ready")
            qk_ready, q_out, k_out, k_out_dve, v_ready, v_out, v_out_dve = (
                sem(n) for n in "qk_ready q_out k_out k_out_dve v_ready v_out v_out_dve".split())
            x_in_ready, cast = sem("x_in_ready"), sem("l0_cast")
            pool_init = sem("pool_init")
            OWN = [(0, 0, NPM), (8, NPM, P)]

            with nc.Block() as block:
                @block.sync
                def _(sp):
                    sp.dma_start(XR[NPM:P, 0, :], x_in[0:NPM, :]).then_inc(loaded_x, 16)
                    sp.dma_start(XR[:, 1:8, :], x_in[NPM:NPM + 7 * P, :].rearrange("(t p) d -> p t d", p=P)).then_inc(loaded_x, 16)
                    sp.dma_start(XR[0:NPM, 8, :], x_in[S - NPM:S, :]).then_inc(loaded_x, 16)
                    sp.dma_start(XR[:, 9:T0, :], x_in[S:TOK, :].rearrange("(t p) d -> p t d", p=P)).then_inc(loaded_x, 16)
                    for t, a, b in OWN:
                        sp.dma_start(XR[a:b, t, :], mem).then_inc(loaded_x, 16)
                        sp.dma_start(XN[a:b, t, :], mem).then_inc(mem_in, 16)
                    sp.dma_start(X[:, :, :], x_in.rearrange("(t p) d -> p t d", p=P)).then_inc(x_in_ready, 16)
                    sp.dma_start(WB[:, :], packB).then_inc(loaded_b, 16)

                @block.gpsimd
                def _(pool):
                    pool.memset(epsc[:, :], EPS).then_inc(pool_init, 1)
                    pool.memset(XT[:, 0:NPM], 0.0).then_inc(x_padded, 1)
                    pool.memset(XT[:, PADC - NPM:PADC], 0.0).then_inc(x_padded, 1)
                    pool.memset(b1s[:, :], 0.0).then_inc(pool_init, 1)
                    pool.memset(dzsum[:, :], 0.0).then_inc(pool_init, 1)
                    pool.memset(errsum[:, :], 0.0).then_inc(pool_init, 1)
                    pool.wait_ge(loaded_a, 16)
                    pool.tensor_copy(idb[:, :], ident).then_inc(cast, 1)
                    pool.tensor_copy(ones_b[:, :], w("ones3")).then_inc(cast, 1)
                    for n in range(2):
                        pool.tensor_copy(masks[:, :, n, :], w("masks").rearrange("p (m k) -> p m k", m=3)).then_inc(cast, 1)
                    pool.wait_ge(cast, 4)

                @block.vector
                def _(dve):
                    chain = Count(dve_done)
                    dve.wait_ge(loaded_x, 16 * 6)
                    dve.wait_ge(dve_done, norm_statistics(dve, chain, XR, T0, stats, mv))
                    dve.nop().then_inc(var_ready, 1)
                    dve.wait_ge(std_ready, 1)
                    dve.wait_ge(dve_done, chain.add(dve.reciprocal(rstd[:, :, :], std[:, :, :])))
                    for t in range(T0):
                        a, b = {0: (NPM, P), 8: (0, NPM)}.get(t, (0, P))
                        dve.tensor_scalar(XN[a:b, t, :], XR[a:b, t, :], mv[a:b, t, 0:1], rstd[a:b, t, :],
                                          ALU.subtract, ALU.mult).then_inc(xn_ready, 1)
                    dve.wait_ge(loaded_a, 16)
                    dve.wait_ge(pool_init, 2)
                    b1 = w("b1row")
                    dve.wait_ge(dve_done, chain.add(dve.tensor_copy(b1h[:, 0, :], b1)))
                    chain.add(dve.tensor_copy(b1s[0:1, :], b1h[0:1, 0, :]))
                    dve.wait_ge(dve_done, chain.add(dve.tensor_tensor(b1t[:, 0, :], b1, b1h[:, 0, :], ALU.subtract)))
                    dve.wait_ge(dve_done, chain.add(dve.tensor_copy(b1h[:, 1, :], b1t[:, 0, :])))
                    chain.add(dve.tensor_copy(b1s[32:33, :], b1h[32:33, 1, :]))
                    dve.wait_ge(dve_done, chain.add(dve.tensor_tensor(b1t[:, 1, :], b1t[:, 0, :], b1h[:, 1, :], ALU.subtract)))
                    dve.wait_ge(dve_done, chain.add(dve.tensor_copy(b1s[64:65, :], b1t[64:65, 1, :])))
                    dve.wait_ge(dve_done, chain.add(dve.tensor_scalar(nwoT[:, :], w("woT"), -1.0, None, ALU.mult)))
                    for j in range(5):
                        dve.wait_ge(qk_ready, 2 * j + 2)
                        n = NB if j < 4 else PADC - 4 * NB
                        dve.wait_ge(k_out, 2 * (j + 1))
                        for h in (2, 3):
                            dve.tensor_scalar(KM[:, h, NB * j:NB * j + n], ps[:, 4 + j % 2, 0:n],
                                              w("headmask")[:, h:h + 1], None, ALU.mult).then_inc(k_out_dve, 1)
                    for j in (1, 3):
                        dve.wait_ge(v_ready, j + 1)
                        dve.tensor_copy(V[:, 4 * j:4 * j + 4, :], ps[:, 6 + j % 2, :].rearrange("p (t d) -> p t d", d=P)).then_inc(v_out_dve, 1)
                    dve.wait_ge(v_out_dve, 2)

                @block.scalar
                def _(act):
                    act.dma_start(WA[:, :], packA).then_inc(loaded_a, 16)
                    act.wait_ge(pool_init, 1)
                    act.wait_ge(var_ready, 1)
                    act.activation(std[:, :, :], mv[:, :, 1:2], ACT.Sqrt, bias=epsc[:, :]).then_inc(std_ready, 1)
                    for j in range(5):
                        act.wait_ge(turned, j + 1)
                        n = NB if j < 4 else P
                        act.activation(XT[:, NPM + NB * j:NPM + NB * j + n], ps[:, j % 2, 0:n], ACT.Copy).then_inc(xt_ready, 1)
                    act.wait_ge(loaded_a, 16)
                    for j in range(5):
                        n = NB if j < 4 else PADC - 4 * NB
                        act.wait_ge(qk_ready, 2 * j + 1)
                        act.activation(QT[:, NB * j:NB * j + n], ps[:, 2 + j % 2, 0:n], ACT.Copy).then_inc(q_out, 1)
                        act.wait_ge(qk_ready, 2 * j + 2)
                        for h in (0, 1):
                            act.activation(KM[:, h, NB * j:NB * j + n], ps[:, 4 + j % 2, 0:n], ACT.Copy,
                                           scale=w("headmask")[:, h:h + 1]).then_inc(k_out, 1)
                    for j in (0, 2, 4):
                        act.wait_ge(v_ready, j + 1)
                        m = min(4, T0 + 1 - 4 * j)
                        act.activation(V[:, 4 * j:4 * j + m, :],
                                       ps[:, 6 + j % 2, 0:m * P].rearrange("p (t d) -> p t d", d=P),
                                       ACT.Copy).then_inc(v_out, 1)
                    act.wait_ge(v_out, 3)

                @block.tensor
                def _(pe):
                    pe.wait_ge(loaded_a, 16)
                    pe.wait_ge(mem_in, 32)
                    for t in range(T0):
                        pe.wait_ge(xn_ready, t + 1)
                        if t % 4 == 0 and t >= 8:
                            pe.wait_ge(xt_ready, t // 4 - 1)
                        ins = pe.transpose(ps[:, (t // 4) % 2, P * (t % 4):P * (t % 4 + 1)], XN[:, t, :], ident)
                        if t % 4 == 3 or t == T0 - 1:
                            ins.then_inc(turned, 1)
                    pe.wait_ge(x_padded, 2)
                    for j in range(5):
                        n = NB if j < 4 else PADC - 4 * NB
                        pe.wait_ge(xt_ready, min(j + 1, 5))
                        if j >= 2:
                            pe.wait_ge(q_out, j - 1)
                            pe.wait_ge(k_out, 2 * (j - 1))
                            pe.wait_ge(k_out_dve, 2 * (j - 1))
                        pe.matmul(ps[:, 2 + j % 2, 0:n], w("wqT"), XT[:, NB * j:NB * j + n], start=True, stop=True).then_inc(qk_ready, 1)
                        pe.matmul(ps[:, 4 + j % 2, 0:n], w("wkT"), XT[:, NB * j:NB * j + n], start=True, stop=True).then_inc(qk_ready, 1)
                    for t in range(T0 + 1):
                        j = t // 4
                        if t % 4 == 0 and j >= 2:
                            pe.wait_ge(v_out if j % 2 == 0 else v_out_dve, j // 2)
                        ins = pe.matmul(ps[:, 6 + j % 2, P * (t % 4):P * (t % 4 + 1)], XT[:, P * t:P * (t + 1)], w("wvT"),
                                        start=True, stop=True)
                        if t % 4 == 3 or t == T0:
                            ins.then_inc(v_ready, 1)

            Pm = sbi("Pm", [P, NH0, KW])
            PTA, PTB = sbi("PTA", [P, NH0, P]), sbi("PTB", [WIN, NH0, P])
            nmax, rowsum, rinv = sbi("nmax", [P, 2, NH0]), sbi("rowsum", [P, NH0]), sbi("rinv", [P, NH0])
            nbias = sbi("nbias", [P, NH0])
            rwide = sbi("rwide", [P, NH0, DH0])
            Osb = sbi("Osb", [P, P])
            Th, H2, U, W2 = sbi("Th", [P, HID]), sbi("H2", [P, HID]), sbi("U", [P, HID]), sbi("W2", [P, HID])
            dz = sbi("dz", [P, HID])
            hT, err, errT = sbi("hT", [P, HC, P]), sbi("err", [P, D]), sbi("errT", [P, P])
            names = ("s_ready nmax_ready nbias_ready p_ready rwide_ready pt_ready pta_out ptb_out o_ready osb_ready ot_ready "
                     "z_ready th_ready h_ready ht_ready ht_out err_psum err_ready errt_psum errt_ready dh_ready "
                     "dz_ready g1_done g2_done sums_done u_done w_done sum_e").split()
            q = {n: sem("l0_" + n) for n in names}
            SB = (0, 1)
            OB, ZB, HB, EB = 2, 3, 4, 5

            with nc.Block() as block:
                @block.tensor
                def _(pe):
                    pe.wait_ge(cast, 4)
                    for s in range(T0 + 2):
                        t, g, l = s, s - 1, s - 2
                        if t < T0:
                            m = 1 if t == 0 else 2 if t == 8 else 0
                            if t:
                                pe.wait_ge(q["pta_out"], t)
                                pe.wait_ge(q["ptb_out"], t)
                            for k in range(2):
                                dst = ps[:, SB[k], 0:2 * KW]
                                pe.matmul(dst, QT[:, NPM + P * t:NPM + P * (t + 1)],
                                          KM[:, 2 * k:2 * k + 2, P * t:P * t + KW], start=True, stop=False)
                                ins = pe.matmul(dst, idb[:, :], masks[:, m, :, :], start=False, stop=True)
                            ins.then_inc(q["s_ready"], 1)
                        if 0 <= g < T0:
                            if g:
                                pe.wait_ge(q["dz_ready"], g)
                            xt = XT[:, NPM + P * g:NPM + P * (g + 1)]
                            pe.matmul(ps[:, ZB, :], xt, w("w1T"), start=True, stop=False)
                            pe.matmul(ps[:, ZB, :], ones_b[:, :], b1s[:, :], start=False, stop=True).then_inc(q["z_ready"], 1)
                        if 0 <= l < T0:
                            pe.wait_ge(q["dz_ready"], l + 1)
                            pe.matmul(G1, XN[:, l, :], dz[:, :], start=(l == 0), stop=(l == T0 - 1)).then_inc(q["g1_done"], 1)
                        if 0 <= g < T0:
                            pe.wait_ge(q["h_ready"], g + 1)
                            if g:
                                pe.wait_ge(q["ht_out"], g)
                            for k in range(HC):
                                ins = pe.transpose(ps[:, HB, P * k:P * (k + 1)], H2[:, P * k:P * (k + 1)], ident)
                            ins.then_inc(q["ht_ready"], 1)
                        if t < T0:
                            for h in range(NH0):
                                pe.wait_ge(q["p_ready"], NH0 * t + max(h + 1, 2))
                                pe.transpose(ps[:, SB[0], P * h:P * (h + 1)], Pm[:, h, 0:P], ident)
                            for h in range(NH0):
                                pe.transpose(ps[0:WIN, SB[1], P * h:P * (h + 1)], Pm[:, h, P:KW], ident).then_inc(q["pt_ready"], 1)
                        if 0 <= g < T0:
                            pe.wait_ge(q["ht_out"], g + 1)
                            pe.wait_ge(q["ot_ready"], g + 1)
                            if g:
                                pe.wait_ge(q["errt_ready"], g)
                            for k in range(HC):
                                pe.matmul(ps[:, EB, 0:D], hT[:, k, :], w("w2T")[:, P * k:P * (k + 1)], start=(k == 0), stop=False)
                            pe.matmul(ps[:, EB, 0:D], OT[:, P * g:P * (g + 1)], nwoT[:, :], start=False, stop=True).then_inc(q["err_psum"], 1)
                        if t < T0:
                            pe.wait_ge(q["rwide_ready"], t + 1)
                            if t:
                                pe.wait_ge(q["ot_ready"], t)
                            pe.matmul(ps[:, OB, P:2 * P], rwide[:, :, :].rearrange("p h d -> p (h d)"), ident,
                                      start=True, stop=True)
                            pe.wait_ge(q["pta_out"], t + 1)
                            pe.wait_ge(q["ptb_out"], t + 1)
                            for h in range(NH0):
                                hs = slice(DH0 * h, DH0 * (h + 1))
                                pe.matmul(ps[hs, OB, 0:P], V[:, t, hs], PTA[:, h, :], start=True, stop=False)
                            for h in range(NH0):
                                hs = slice(DH0 * h, DH0 * (h + 1))
                                ins = pe.matmul(ps[hs, OB, 0:P], V[0:WIN, t + 1, hs], PTB[:, h, :], start=False, stop=True,
                                                tile_position=(0, DH0 * h))
                            ins.then_inc(q["o_ready"], 1)
                        if 0 <= g < T0:
                            pe.wait_ge(q["err_ready"], g + 1)
                            pe.transpose(ps[:, EB, P:2 * P], err[:, :], ident).then_inc(q["errt_psum"], 1)
                            pe.matmul(G2, err[:, :], H2[:, :], start=(g == 0), stop=(g == T0 - 1)).then_inc(q["g2_done"], 1)
                            pe.wait_ge(q["errt_ready"], g + 1)
                            pe.wait_ge(q["h_ready"], g + 1)
                            pe.matmul(ps[:, ZB, :], errT[:, :], w("w2"), start=True, stop=True).then_inc(q["dh_ready"], 1)

                @block.scalar
                def _(act):
                    for s in range(T0 + 1):
                        t, g = s, s - 1
                        if 0 <= g < T0:
                            act.wait_ge(q["z_ready"], g + 1)
                            if g:
                                act.wait_ge(q["w_done"], g)
                            act.activation(Th[:, :], ps[:, ZB, :], ACT.Tanh, scale=0.5).then_inc(q["th_ready"], 1)
                        if t < T0:
                            act.wait_ge(q["nbias_ready"], t + 1)
                            if t:
                                act.wait_ge(q["pt_ready"], NH0 * t)
                                act.wait_ge(q["rwide_ready"], t)
                            for h in range(NH0):
                                act.activation(Pm[:, h, :], ps[:, SB[h // 2], KW * (h % 2):KW * (h % 2 + 1)], ACT.Exp,
                                               bias=nbias[:, h:h + 1], scale=SCALE,
                                               accum_out=rowsum[:, h:h + 1]).then_inc(q["p_ready"], 1)
                        if 0 <= g < T0:
                            act.wait_ge(q["ht_ready"], g + 1)
                            if g:
                                act.wait_ge(q["err_psum"], g)
                            act.activation(hT[:, :, :], ps[:, HB, :].rearrange("p (k n) -> p k n", k=HC), ACT.Copy,
                                           scale=0.5).then_inc(q["ht_out"], 1)
                        if t < T0:
                            act.wait_ge(q["pt_ready"], NH0 * (t + 1))
                            if t:
                                act.wait_ge(q["o_ready"], t)
                            act.activation(PTB[:, :, :], ps[0:WIN, SB[1], :].rearrange("p (k n) -> p k n", k=NH0),
                                           ACT.Copy).then_inc(q["ptb_out"], 1)
                        if 0 <= g < T0:
                            act.wait_ge(q["errt_psum"], g + 1)
                            if g:
                                act.wait_ge(q["dh_ready"], g)
                            act.activation(errT[:, :], ps[:, EB, P:2 * P], ACT.Copy).then_inc(q["errt_ready"], 1)
                        if t < T0:
                            act.wait_ge(q["o_ready"], t + 1)
                            if t:
                                act.wait_ge(q["ot_ready"], t)
                            act.activation(Osb[:, :], ps[:, OB, 0:P], ACT.Copy).then_inc(q["osb_ready"], 1)

                @block.vector
                def _(dve):
                    dve.wait_ge(x_in_ready, 16)
                    for s in range(T0 + 1):
                        t, g = s, s - 1
                        if t < T0:
                            dve.wait_ge(q["s_ready"], t + 1)
                            if t:
                                dve.wait_ge(q["nbias_ready"], t)
                                dve.wait_ge(q["p_ready"], NH0 * t)
                            for k in range(2):
                                dve.tensor_reduce(nmax[:, t % 2, 2 * k:2 * k + 2], ps[:, SB[k], 0:2 * KW].rearrange("p (h k) -> p h k", h=2),
                                                  AX.X, ALU.max, negate=True).then_inc(q["nmax_ready"], 1)
                            dve.wait_ge(q["nmax_ready"], 2 * (t + 1))
                            dve.tensor_scalar(nbias[:, :], nmax[:, t % 2, :], SCALE, None, ALU.mult).then_inc(q["nbias_ready"], 1)
                        if 0 <= g < T0:
                            dve.wait_ge(q["th_ready"], g + 1)
                            if g:
                                dve.wait_ge(q["g2_done"], g)
                                dve.wait_ge(q["ht_ready"], g)
                            dve.scalar_tensor_tensor(out=H2[:, :], in0=Th[:, :], scalar=1.0, in1=ps[:, ZB, :],
                                                     op0=ALU.add, op1=ALU.mult).then_inc(q["h_ready"], 1)
                            dve.wait_ge(q["h_ready"], g + 1)
                            dve.scalar_tensor_tensor(out=U[:, :], in0=Th[:, :], scalar=1.0, in1=H2[:, :],
                                                     op0=ALU.subtract, op1=ALU.mult).then_inc(q["u_done"], 1)
                        if t < T0:
                            dve.wait_ge(q["p_ready"], NH0 * (t + 1))
                            dve.reciprocal(rinv[:, :], rowsum[:, :]).then_inc(q["sum_e"], 1)
                            dve.wait_ge(q["sum_e"], t + 1)
                            if t:
                                dve.wait_ge(q["o_ready"], t)
                            dve.tensor_copy(rwide[:, :, :], rinv[:, :].unsqueeze(2).to_broadcast([P, NH0, DH0])).then_inc(q["rwide_ready"], 1)
                            dve.wait_ge(q["pt_ready"], NH0 * (t + 1))
                            dve.tensor_copy(PTA[:, :, :], ps[:, SB[0], :].rearrange("p (k n) -> p k n", k=NH0)).then_inc(q["pta_out"], 1)
                        if 0 <= g < T0:
                            dve.wait_ge(q["err_psum"], g + 1)
                            if g:
                                dve.wait_ge(q["g2_done"], g)
                                dve.wait_ge(q["sums_done"], 2 * g)
                            dve.tensor_tensor(err[:, :], ps[:, EB, 0:D], w("b2row"), ALU.add).then_inc(q["err_ready"], 1)
                            dve.wait_ge(q["u_done"], g + 1)
                            if g:
                                dve.wait_ge(q["dz_ready"], g)
                            dve.scalar_tensor_tensor(out=W2[:, :], in0=Th[:, :], scalar=2.0, in1=U[:, :],
                                                     op0=ALU.mult, op1=ALU.subtract).then_inc(q["w_done"], 1)
                        if t < T0:
                            dve.wait_ge(q["osb_ready"], t + 1)
                            dve.tensor_tensor(OT[:, P * t:P * (t + 1)], Osb[:, :], ps[:, OB, P:2 * P], ALU.mult).then_inc(q["ot_ready"], 1)
                        if 0 <= g < T0:
                            dve.wait_ge(q["dh_ready"], g + 1)
                            dve.wait_ge(q["w_done"], g + 1)
                            if g:
                                dve.wait_ge(q["g1_done"], g)
                                dve.wait_ge(q["sums_done"], 2 * g)
                            dve.scalar_tensor_tensor(out=dz[:, :], in0=W2[:, :], scalar=2.0, in1=ps[:, ZB, :],
                                                     op0=ALU.add, op1=ALU.mult).then_inc(q["dz_ready"], 1)

                @block.gpsimd
                def _(pool):
                    for g in range(T0):
                        if g:
                            pool.wait_ge(q["sums_done"], 2 * g)
                        pool.wait_ge(q["err_ready"], g + 1)
                        pool.tensor_tensor(errsum[:, :], errsum[:, :], err[:, :], ALU.add).then_inc(q["sums_done"], 1)
                        pool.wait_ge(q["dz_ready"], g + 1)
                        pool.tensor_tensor(dzsum[:, :], dzsum[:, :], dz[:, :], ALU.add).then_inc(q["sums_done"], 1)

        updated_mlp(nc, sem, w, ident, ps, XT, OT, dzsum, errsum, G1, G2, Y, y_stat, loaded_b)


def updated_mlp(nc, sem, w, ident, ps, XT, OT, dzsum, errsum, G1, G2, Y, y_stat, loaded_b):
    with ExitStack() as c:
        def sb(name, shape, dt=F32):
            return c.enter_context(nc.sbuf_tensor("um_" + name, shape, dt))

        keep, nth = sb("keep", [P, 1]), sb("nth", [P, 3])
        w1n, w2n = sb("w1n", [P, HID]), sb("w2n", [P, HID])
        w1k, w2k = sb("w1k", [P, HID]), sb("w2k", [P, HID])
        g2s = sb("g2s", [P, HID])
        b1k, b1n, b2k, b2n = sb("b1k", [P, HC]), sb("b1n", [P, HC]), sb("b2k", [P, 1]), sb("b2n", [P, 1])
        hT = sb("hT", [P, HC, NB])
        swaT, memT = sb("swaT", [P, NB]), sb("memT", [P, NB])
        t1, t2 = sb("t1", [P, NB]), sb("t2", [P, NB])
        a1, a2, mg = sb("a1", [P, NB]), sb("a2", [P, NB]), sb("mg", [P, NB])
        dve_done, bsum_ready, g2t_ready, g2s_ready, new_ready = (sem("um_dve_done"), sem("um_bsum_ready"),
                                                                 sem("um_g2t_ready"), sem("um_g2s_ready"), sem("um_new_ready"))
        z_ready, h_ready, swa_psum, swa_ready, mem_psum, mem_ready = (sem("um_z_ready"), sem("um_h_ready"), sem("um_swa_psum"),
                                                                      sem("um_swa_ready"), sem("um_mem_psum"), sem("um_mem_ready"))
        g_psum, tanh_ready, mg_ready, turned, y_ready = (sem("um_g_psum"), sem("um_tanh_ready"), sem("um_mg_ready"),
                                                         sem("um_turned"), sem("um_y_ready"))
        a_done = sem("um_a_done")
        NJ = TOK // NB
        cols = [SM * (j // 2) + NPM + NB * (j % 2) for j in range(NJ)]

        with nc.Block() as block:
            @block.vector
            def _(dve):
                chain = Count(dve_done)
                chain.add(dve.tensor_scalar(keep[:, :], w("alpha"), -1.0, 1.0, ALU.mult, ALU.add))
                for n in range(3):
                    chain.add(dve.tensor_scalar(nth[:, n:n + 1], w("theta"), -0.5 ** n, None, ALU.mult))
                dve.tensor_copy(g2s[:, :], G2).then_inc(g2s_ready, 1)
                dve.wait_ge(dve_done, chain.n)
                chain.add(dve.tensor_scalar(w1k[:, :], w("w1T"), keep[:, :], None, ALU.mult))
                chain.add(dve.tensor_scalar(w2k[:, :], w("w2T"), keep[:, :], None, ALU.mult))
                chain.add(dve.tensor_scalar(b1k[:, :], w("b1col"), keep[:, :], None, ALU.mult))
                chain.add(dve.tensor_scalar(b2k[:, :], w("b2col"), keep[:, :], None, ALU.mult))
                dve.wait_ge(dve_done, chain.n)
                dve.scalar_tensor_tensor(out=w1n[:, :], in0=G1, scalar=nth[:, 2:3], in1=w1k[:, :],
                                         op0=ALU.mult, op1=ALU.add).then_inc(new_ready, 1)
                dve.wait_ge(bsum_ready, 1)
                dve.scalar_tensor_tensor(out=b1n[:, :], in0=ps[:, 0, 0:HC], scalar=nth[:, 2:3], in1=b1k[:, :],
                                         op0=ALU.mult, op1=ALU.add).then_inc(new_ready, 1)
                dve.scalar_tensor_tensor(out=b2n[:, :], in0=ps[:, 0, HC:HC + 1], scalar=nth[:, 0:1], in1=b2k[:, :],
                                         op0=ALU.mult, op1=ALU.add).then_inc(new_ready, 1)
                dve.wait_ge(g2t_ready, 1)
                dve.scalar_tensor_tensor(out=w2n[:, :], in0=ps[:, 1, :], scalar=nth[:, 1:2], in1=w2k[:, :],
                                         op0=ALU.mult, op1=ALU.add).then_inc(new_ready, 1)
                for j in range(NJ):
                    dve.wait_ge(swa_psum, j + 1)
                    if j:
                        dve.wait_ge(mg_ready, j)
                        dve.wait_ge(g_psum, 2 * j)
                    dve.tensor_copy(swaT[:, :], ps[:, 5, :]).then_inc(swa_ready, 1)
                    dve.wait_ge(swa_ready, j + 1)
                    dve.wait_ge(tanh_ready, 2 * j + 1)
                    dve.scalar_tensor_tensor(out=a1[:, :], in0=t1[:, :], scalar=1.0, in1=swaT[:, :],
                                             op0=ALU.add, op1=ALU.mult).then_inc(a_done, 1)
                    dve.wait_ge(tanh_ready, 2 * j + 2)
                    dve.wait_ge(mem_ready, j + 1)
                    dve.scalar_tensor_tensor(out=a2[:, :], in0=t2[:, :], scalar=1.0, in1=memT[:, :],
                                             op0=ALU.add, op1=ALU.mult).then_inc(a_done, 1)
                    dve.wait_ge(a_done, 2 * j + 2)
                    if j:
                        dve.wait_ge(turned, j)
                    dve.tensor_tensor(mg[:, :], a1[:, :], a2[:, :], ALU.add).then_inc(mg_ready, 1)
                    if j:
                        dve.wait_ge(y_ready, j)
                        y_stat.block(dve, Y, j - 1)
                dve.wait_ge(y_ready, NJ)
                y_stat.block(dve, Y, NJ - 1)
                y_stat.wait_all(dve)

            @block.tensor
            def _(pe):
                pe.wait_ge(loaded_b, 16)
                for k in range(HC):
                    pe.matmul(ps[:, 0, k:k + 1], dzsum[:, P * k:P * (k + 1)], w("ones"), start=True, stop=True)
                pe.matmul(ps[:, 0, HC:HC + 1], errsum[:, :], w("ones"), start=True, stop=True).then_inc(bsum_ready, 1)
                pe.wait_ge(g2s_ready, 1)
                for k in range(HC):
                    ins = pe.transpose(ps[:, 1, P * k:P * (k + 1)], g2s[:, P * k:P * (k + 1)], ident)
                ins.then_inc(g2t_ready, 1)

                def z_of(j):
                    for k in range(HC):
                        if j:
                            pe.wait_ge(h_ready, HC * (j - 1) + k + 1)
                        pe.matmul(ps[:, k, :], w1n[:, P * k:P * (k + 1)], XT[:, NPM + cols[j]:NPM + cols[j] + NB],
                                  start=True, stop=True).then_inc(z_ready, 1)

                def swa_of(j):
                    if j:
                        pe.wait_ge(swa_ready, j)
                    pe.matmul(ps[:, 5, :], w("woT"), OT[:, cols[j]:cols[j] + NB], start=True, stop=True).then_inc(swa_psum, 1)

                pe.wait_ge(new_ready, 4)
                z_of(0)
                swa_of(0)
                for j in range(NJ):
                    if j:
                        pe.wait_ge(mem_ready, j)
                    for k in range(HC):
                        pe.wait_ge(h_ready, HC * j + k + 1)
                        ins = pe.matmul(ps[:, 4, :], w2n[:, P * k:P * (k + 1)], hT[:, k, :], start=(k == 0), stop=(k == HC - 1))
                    ins.then_inc(mem_psum, 1)
                    pe.wait_ge(swa_ready, j + 1)
                    if j:
                        pe.wait_ge(y_ready, j)
                    pe.matmul(ps[:, 6, :], w("lin1T"), swaT[:, :], start=True, stop=True).then_inc(g_psum, 1)
                    pe.wait_ge(mem_ready, j + 1)
                    if j:
                        pe.wait_ge(tanh_ready, 2 * j)
                    pe.matmul(ps[:, 7, :], w("lin2T"), memT[:, :], start=True, stop=True).then_inc(g_psum, 1)
                    if j + 1 < NJ:
                        z_of(j + 1)
                    pe.wait_ge(mg_ready, j + 1)
                    pe.wait_ge(tanh_ready, 2 * j + 1)
                    for n in range(4):
                        ins = pe.transpose(ps[:, 6, P * n:P * (n + 1)], mg[:, P * n:P * (n + 1)], ident)
                    ins.then_inc(turned, 1)
                    if j + 1 < NJ:
                        swa_of(j + 1)

            @block.scalar
            def _(act):
                def y_of(j):
                    act.wait_ge(turned, j + 1)
                    act.activation(Y[:, 4 * j:4 * j + 4, :], ps[:, 6, :].rearrange("p (t d) -> p t d", d=D), ACT.Copy,
                                   scale=0.5).then_inc(y_ready, 1)

                act.wait_ge(new_ready, 4)
                for j in range(NJ):
                    for k in range(HC):
                        act.wait_ge(z_ready, HC * j + k + 1)
                        if j and k == 0:
                            act.wait_ge(mem_psum, j)
                        act.activation(hT[:, k, :], ps[:, k, :], ACT.Silu, bias=b1n[:, k:k + 1]).then_inc(h_ready, 1)
                    if j:
                        y_of(j - 1)
                    act.wait_ge(mem_psum, j + 1)
                    if j:
                        act.wait_ge(a_done, 2 * j)
                        act.wait_ge(g_psum, 2 * j)
                    act.activation(memT[:, :], ps[:, 4, :], ACT.Identity, bias=b2n[:, :]).then_inc(mem_ready, 1)
                    act.wait_ge(g_psum, 2 * j + 1)
                    act.activation(t1[:, :], ps[:, 6, :], ACT.Tanh, scale=0.5).then_inc(tanh_ready, 1)
                    act.wait_ge(g_psum, 2 * j + 2)
                    act.activation(t2[:, :], ps[:, 7, :], ACT.Tanh, scale=0.5).then_inc(tanh_ready, 1)
                y_of(NJ - 1)
                act.wait_ge(y_ready, NJ)


def wait(eng, sem, value):
    if isinstance(value, int) and value <= 0:
        return
    eng.wait_ge(sem, value)


def experts(nc, sem, w, ident, ps, XNT, Y, y_stat, loaded_b, WC, packC, loaded_c):
    with ExitStack() as c:
        def sb(name, shape, dt=F32):
            return c.enter_context(nc.sbuf_tensor("ex_" + name, shape, dt))

        L, M8, I8 = sb("L", [P, TT, E]), sb("M8", [P, TT, 8]), sb("I8", [P, TT, 8], U32)
        IF = sb("IF", [P, TT, 2])
        dd, ee, dn, w1, w2 = (sb(n, [P, TT, 1]) for n in ("dd", "ee", "dn", "w1", "w2"))
        c1, c2, C1, C2, COMB = (sb(n, [P, TT, E]) for n in ("c1", "c2", "C1", "C2", "COMB"))
        dve_done, logits_ready, d_ready, e_ready = sem("ex_dve_done"), sem("ex_logits_ready"), sem("ex_d_ready"), sem("ex_e_ready")

        with nc.Block() as block:
            @block.sync
            def _(sp):
                sp.dma_start(WC[:, :], packC).then_inc(loaded_c, 16)

            @block.tensor
            def _(pe):
                pe.wait_ge(loaded_b, 16)
                for t in range(TT):
                    ins = pe.matmul(ps[:, 0, E * t:E * (t + 1)], XNT[:, P * t:P * (t + 1)], w("routerT"), start=True, stop=True)
                ins.then_inc(logits_ready, 1)

            @block.scalar
            def _(act):
                act.wait_ge(d_ready, 1)
                act.activation(ee[:, :, :], dd[:, :, :], ACT.Exp).then_inc(e_ready, 1)

            @block.vector
            def _(dve):
                chain = Count(dve_done)

                def then(ins):
                    dve.wait_ge(dve_done, chain.add(ins))

                dve.wait_ge(logits_ready, 1)
                then(dve.tensor_copy(L[:, :, :], ps[:, 0, 0:TT * E].rearrange("p (t e) -> p t e", e=E)))
                for t in range(TT):
                    n = chain.add(dve.max(M8[:, t, :], L[:, t, :]))
                dve.wait_ge(dve_done, n)
                for t in range(TT):
                    n = chain.add(dve.max_index(I8[:, t, :], M8[:, t, :], L[:, t, :]))
                then(dve.tensor_tensor(dd[:, :, :], M8[:, :, 1:2], M8[:, :, 0:1], ALU.subtract))
                dve.nop().then_inc(d_ready, 1)
                dve.wait_ge(e_ready, 1)
                then(dve.tensor_scalar(dn[:, :, :], ee[:, :, :], 1.0, None, ALU.add))
                then(dve.reciprocal(w1[:, :, :], dn[:, :, :]))
                then(dve.tensor_tensor(w2[:, :, :], ee[:, :, :], w1[:, :, :], ALU.mult))
                then(dve.tensor_copy(IF[:, :, :], I8[:, :, 0:2]))
                no = w("expert_no").unsqueeze(1).to_broadcast([P, TT, E])
                for k, (cc, CC, ww) in enumerate(((c1, C1, w1), (c2, C2, w2))):
                    then(dve.tensor_tensor(cc[:, :, :], IF[:, :, k:k + 1].to_broadcast([P, TT, E]), no, ALU.is_equal))
                    then(dve.tensor_tensor(CC[:, :, :], cc[:, :, :], ww[:, :, :].to_broadcast([P, TT, E]), ALU.mult))
                then(dve.tensor_tensor(COMB[:, :, :], C1[:, :, :], C2[:, :, :], ALU.add))

        NJ, NC = TOK // NB, E * I // P
        combT = sb("combT", [P, P])
        CB = sb("CB", [P, E, NB])
        comb = nc.dram_tensor("comb", [NJ, E, 4, P], F32, kind="Internal").ap()
        sg, cw, h = sb("sg", [P, 2, NB]), sb("cw", [P, 2, NB]), sb("h", [P, 2, NB])
        yT = sb("yT", [P, NB])
        ct_psum, ct_out, comb_out, cb_ready, gu_ready, silu_ready, cw_ready, mixed, h_ready, down_done, yt_out, turned, y_out = (
            sem("ex_" + n) for n in ("ct_psum ct_out comb_out cb_ready gu_ready silu_ready cw_ready mixed h_ready down_done yt_out "
                                     "turned y_out").split())
        GB, UB, YB, TB = 0, 2, 6, 7
        wg, wu, wd = w("WgT"), w("WuT"), w("WdT")
        MIXED = [I * e // P for e in range(1, E) if I * e % P]

        def owners(ch):
            if ch not in MIXED:
                return P * ch // I, None
            low = P * ch // I
            cut = I * (low + 1) - P * ch
            return (low, (low + 1, cut, P)) if cut >= P // 2 else (low + 1, (low, 0, cut))

        def last_chunk(e):
            return (I * (e + 1) - 1) // P

        def mixed_count(i, ch):
            return len(MIXED) * i + sum(m <= ch for m in MIXED)

        def u_reader(i, ch):
            return NC * i + (ch - 4 if ch >= 4 else ch - 2 if ch < 2 else ch - 4) + 1

        with nc.Block() as block:
            @block.tensor
            def _(pe):
                pe.transpose(ps[:, TB, 0:P], COMB[:, :, :].rearrange("p t e -> p (t e)"), ident).then_inc(ct_psum, 1)

                def gate_up(i, ch):
                    n = NC * i + ch
                    x = XNT[:, bass.ds(NB * i, NB)]
                    wait(pe, silu_ready, n - 1)
                    wait(pe, h_ready, u_reader(i, ch))
                    pe.matmul(ps[:, GB + ch % 2, :], wg[:, P * ch:P * (ch + 1)], x, start=True, stop=True)
                    pe.matmul(ps[:, UB + ch % 4, :], wu[:, P * ch:P * (ch + 1)], x, start=True, stop=True).then_inc(gu_ready, 1)

                def down(i, ch):
                    wait(pe, h_ready, NC * i + ch + 1)
                    if ch == 0:
                        wait(pe, yt_out, i)
                    pe.matmul(ps[:, YB, :], wd[:, D * ch:D * (ch + 1)], h[:, ch % 2, :], start=(ch == 0),
                              stop=(ch == NC - 1)).then_inc(down_done, 1)

                def turn(i):
                    wait(pe, yt_out, i + 1)
                    if isinstance(i, int) and i == 0:
                        pe.wait_ge(ct_out, 1)
                    wait(pe, y_out, i)
                    for n in range(4):
                        ins = pe.transpose(ps[:, TB, P * n:P * (n + 1)], yT[:, P * n:P * (n + 1)], ident)
                    ins.then_inc(turned, 1)

                def body(i, first):
                    for ch in range(NC):
                        gate_up(i, ch)
                        if ch >= 2:
                            down(i, ch - 2)
                        elif not first:
                            down(i - 1, NC + ch - 2)
                        if ch == 3 and not first:
                            turn(i - 1)

                body(0, True)
                with pe.Fori(1, NJ - 1) as i:
                    body(i, False)
                body(NJ - 1, False)
                for ch in (NC - 2, NC - 1):
                    down(NJ - 1, ch)
                turn(NJ - 1)

            @block.scalar
            def _(act):
                act.wait_ge(ct_psum, 1)
                act.activation(combT[:, :], ps[:, TB, 0:P], ACT.Copy).then_inc(ct_out, 1)

                def sum_out(i):
                    wait(act, down_done, NC * (i + 1))
                    wait(act, turned, i)
                    act.activation(yT[:, :], ps[:, YB, :], ACT.Copy).then_inc(yt_out, 1)

                def y_of(i):
                    wait(act, turned, i + 1)
                    act.activation(Y[:, bass.ds(4 * i, 4), :], ps[:, TB, :].rearrange("p (t d) -> p t d", d=D),
                                   ACT.Copy).then_inc(y_out, 1)

                def body(i, first):
                    for ch in range(NC):
                        n = NC * i + ch
                        wait(act, gu_ready, n + 1)
                        wait(act, h_ready, n - 1)
                        act.activation(sg[:, ch % 2, :], ps[:, GB + ch % 2, :], ACT.Silu).then_inc(silu_ready, 1)
                        if ch == 2 and not first:
                            sum_out(i - 1)
                        if ch == 4 and not first:
                            y_of(i - 1)

                body(0, True)
                with act.Fori(1, NJ) as i:
                    body(i, False)
                sum_out(NJ - 1)
                y_of(NJ - 1)

            @block.gpsimd
            def _(pool):
                def body(i):
                    for ch in range(NC):
                        n = NC * i + ch
                        e, _ = owners(ch)
                        wait(pool, silu_ready, n + 1)
                        wait(pool, cb_ready, 16 * (E * i + e + 1))
                        wait(pool, h_ready, n - 1)
                        pool.tensor_tensor(cw[:, ch % 2, :], sg[:, ch % 2, :], CB[:, e, :], ALU.mult).then_inc(cw_ready, 1)

                body(0)
                with pool.Fori(1, NJ) as i:
                    body(i)

            @block.vector
            def _(dve):
                def body(i, first, last):
                    for ch in range(NC):
                        n = NC * i + ch
                        _, rest = owners(ch)
                        wait(dve, cw_ready, n + 1)
                        if rest:
                            e, a, b = rest
                            wait(dve, silu_ready, n + 1)
                            wait(dve, cb_ready, 16 * (E * i + e + 1))
                            dve.tensor_tensor(cw[a:b, ch % 2, :], sg[a:b, ch % 2, :], CB[a:b, e, :], ALU.mult).then_inc(mixed, 1)
                            wait(dve, mixed, mixed_count(i, ch))
                        wait(dve, gu_ready, n + 1)
                        wait(dve, down_done, n - 1)
                        dve.tensor_tensor(h[:, ch % 2, :], cw[:, ch % 2, :], ps[:, UB + ch % 4, :], ALU.mult).then_inc(h_ready, 1)
                        if ch == 7 and not first:
                            wait(dve, y_out, i)
                            y_stat.sums(dve, Y, i - 1)
                            if last:
                                for j in range(NJ - 1):
                                    y_stat.results(dve, j)

                body(0, True, False)
                with dve.Fori(1, NJ - 1) as i:
                    body(i, False, False)
                body(NJ - 1, False, True)
                dve.wait_ge(y_out, NJ)
                y_stat.block(dve, Y, NJ - 1)
                y_stat.wait_all(dve)

            @block.sync
            def _(sp):
                sp.wait_ge(ct_out, 1)
                for j in range(NJ):
                    sp.dma_start(comb[j, :, :, :].rearrange("e t p -> t e p"), combT[4 * E * j:4 * E * (j + 1), :]).then_inc(comb_out, 16)
                sp.wait_ge(comb_out, 16 * NJ)

                def body(i):
                    for e in range(E):
                        wait(sp, cb_ready, 16 * (E * i + e))
                        wait(sp, h_ready, NC * (i - 1) + last_chunk(e) + 1)
                        src = comb[bass.ds(i, 1), e, :, :].rearrange("o t p -> (o t p)")
                        sp.dma_start(CB[:, e, :], src.partition_broadcast(P)).then_inc(cb_ready, 16)

                for i in range(NJ):
                    body(i)
                sp.wait_ge(cb_ready, 16 * E * NJ)


def second_attention(nc, sem, w, ident, idb, ps, XNT, Y, y_stat, loaded_c):
    NG = B * NH1 // 4
    KC = S // P
    SCALE = 1.0 / float(np.sqrt(np.float32(NH1 + DC + DC)))
    NR, MR = 9 * DH1, 96
    KR = MR + 3
    NQ = 3
    with ExitStack() as c0:
        def sb(name, shape, dt=F32):
            return c0.enter_context(nc.sbuf_tensor("sa_" + name, shape, dt))

        VA = sb("VA", [P, NG, KC, 4, DH1 + 1])
        ATT = sb("ATT", [P, B, KC, 4, 4 * DH1])
        parts_q = nc.dram_tensor("parts_q", [3, NG * DH1, 4 * S], BF16, kind="Internal").ap()
        parts_k = nc.dram_tensor("parts_k", [3, NG * DH1, 4 * S], BF16, kind="Internal").ap()
        QS, KS = sb("QS", [P, NQ, 4, S], BF16), sb("KS", [P, NQ, 4, S], BF16)
        rows_set, parts_out = sem("sa_rows_set"), (sem("sa_parts_out0"), sem("sa_parts_out1"))

        VG = sb("VG", [P, KC, 4, 32])
        MS = sb("MS", [P, 2, KC, KR], BF16)
        stacked, st_ready, zeroed = sem("sa_stacked"), sem("sm_st_ready"), sem("sm_zeroed")
        NSTACK = 2 * 3
        IT = 4 * KC + 4

        def stack_rows(pool, n):
            for k, (dst, a, b, value) in enumerate(((QS, 64, MR, 0.0), (KS, 64, MR, 0.0), (KS, MR, KR, 1.0))):
                pool.wait_ge(rows_set, 1 + 3 * n + k)
                pool.memset(dst[a:b, n, :, :], value).then_inc(rows_set, 1)

        def stack(sp, g):
            wait(sp, stacked, 16 * NSTACK * g)
            if not (isinstance(g, int) and g < NQ):
                sp.wait_ge(st_ready, 2 * (IT * (g - NQ + 1) + 3))
            for i in range(3):
                rows = slice(3 * DH1 * i, 3 * DH1 * (i + 1))
                q_i = parts_q[i, bass.ds(DH1 * g, DH1), :].unsqueeze(0).to_broadcast([3, DH1, 4 * S])
                for dst, src in ((QS, q_i), (KS, parts_k[:, bass.ds(DH1 * g, DH1), :])):
                    sp.dma_start(dst[rows, bass.ds(g % NQ, 1), :, :].rearrange("r o h n -> r (o h n)"), src).then_inc(stacked, 16)

        with ExitStack() as c:
            def sbi(name, shape, dt=F32):
                return c.enter_context(nc.sbuf_tensor("sp_" + name, shape, dt))

            CT = sbi("CT", [P, 2, NB])
            r1, r2, r3 = (sbi(n, [P, NB]) for n in ("r1", "r2", "r3"))
            qk, rest = sbi("qk", [P, 2, NB]), sbi("rest", [P, 2, NB])
            SPL = sbi("SPL", [P, 2, 2, 3, NB], BF16)
            ct_psum, ct_ready, q_psum, k_psum, v_psum, q_read, k_read, v_read, dve_done = (
                sem("sp_" + n) for n in "ct_psum ct_ready q_psum k_psum v_psum q_read k_read v_read dve_done".split())
            qk_ready, first_part, rest_ready, second_part, split = (
                sem("sp_" + n) for n in "qk_ready first_part rest_ready second_part split".split())
            NJ = TOK // NB

            with nc.Block() as block:
                @block.gpsimd
                def _(pool):
                    pool.memset(VA[:, :, :, :, DH1:DH1 + 1], 1.0).then_inc(rows_set, 1)
                    stack_rows(pool, 0)
                    pool.wait_ge(rows_set, 4)
                    pool.memset(VG[:, :, :, :], 0.0).then_inc(zeroed, 1)
                    pool.memset(MS[:, :, :, :], 0.0).then_inc(zeroed, 1)
                    pool.wait_ge(zeroed, 2)

                @block.tensor
                def _(pe):
                    def down(j):
                        wait(pe, ct_ready, j)
                        pe.matmul(ps[:, 0, :], w("Wdown"), XNT[:, NB * j:NB * (j + 1)], start=True, stop=True).then_inc(ct_psum, 1)

                    pe.wait_ge(loaded_c, 16)
                    down(0)
                    for j in range(NJ):
                        x, ct = XNT[:, NB * j:NB * (j + 1)], CT[:, j % 2, :]
                        if j + 1 < NJ:
                            down(j + 1)
                        pe.wait_ge(ct_ready, j + 1)
                        wait(pe, q_read, j)
                        for n, name in ((2, "Wqr"), (3, "Wqr_sw"), (1, "Wuq")):
                            ins = pe.matmul(ps[:, n, :], w(name), ct, start=True, stop=True)
                        ins.then_inc(q_psum, 1)
                        wait(pe, k_read, j)
                        pe.matmul(ps[:, 5, :], w("Wkr"), x, start=True, stop=True)
                        pe.matmul(ps[:, 6, :], w("Wkr_sw"), x, start=True, stop=True)
                        pe.matmul(ps[:, 4, :], w("Wuk"), ct, start=True, stop=True).then_inc(k_psum, 1)
                        wait(pe, v_read, j)
                        for n in range(4):
                            ins = pe.matmul(ps[:, 7, P * n:P * (n + 1)], CT[:, j % 2, P * n:P * (n + 1)], w("Wuv"), start=True, stop=True)
                        ins.then_inc(v_psum, 1)

                @block.scalar
                def _(act):
                    def compressed(j):
                        act.wait_ge(ct_psum, j + 1)
                        wait(act, v_psum, j - 1)
                        act.activation(CT[:, j % 2, :], ps[:, 0, :], ACT.Identity, bias=w("b_down")).then_inc(ct_ready, 1)

                    compressed(0)
                    for j in range(NJ):
                        if j + 1 < NJ:
                            compressed(j + 1)
                        for k in range(2):
                            u = 2 * j + k
                            act.wait_ge(qk_ready, u + 1)
                            wait(act, parts_out[j % 2], 16 * 2 * (j // 2))
                            act.activation(SPL[:, j % 2, k, 0, :], qk[:, u % 2, :], ACT.Copy).then_inc(first_part, 1)
                            act.wait_ge(rest_ready, u + 1)
                            act.activation(SPL[:, j % 2, k, 1, :], rest[:, u % 2, :], ACT.Copy).then_inc(second_part, 1)

                @block.vector
                def _(dve):
                    chain = Count(dve_done)

                    def third_part(u):
                        dve.wait_ge(second_part, u + 1)
                        dve.tensor_tensor(SPL[:, (u // 2) % 2, u % 2, 2, :], rest[:, u % 2, :], SPL[:, (u // 2) % 2, u % 2, 1, :],
                                          ALU.subtract).then_inc(split, 1)

                    dve.wait_ge(rows_set, 1)
                    for j in range(NJ):
                        pos = slice(NB * (j % 2), NB * (j % 2 + 1))
                        cos, sin = w("cos")[:, pos], w("sin")[:, pos]
                        for k, (bank, psum, read, bs) in enumerate((((1, 2, 3), q_psum, q_read, ("b_uq", "b_qr", "b_qr_sw")),
                                                                    ((4, 5, 6), k_psum, k_read, ("b_uk", "b_kr", "b_kr_sw")))):
                            u = 2 * j + k
                            dve.wait_ge(psum, j + 1)
                            wait(dve, qk_ready, u)
                            chain.add(dve.scalar_tensor_tensor(out=r1[:, :], in0=ps[:, bank[1], :], scalar=w(bs[1]), in1=cos,
                                                               op0=ALU.add, op1=ALU.mult))
                            n = chain.add(dve.scalar_tensor_tensor(out=r2[:, :], in0=ps[:, bank[2], :], scalar=w(bs[2]), in1=sin,
                                                                   op0=ALU.add, op1=ALU.mult))
                            dve.wait_ge(dve_done, n - 1)
                            dve.scalar_tensor_tensor(out=r3[:, :], in0=ps[:, bank[0], :], scalar=w(bs[0]), in1=r1[:, :],
                                                     op0=ALU.add, op1=ALU.add).then_inc(read, 1)
                            dve.wait_ge(read, j + 1)
                            wait(dve, first_part, u - 1)
                            dve.tensor_tensor(qk[:, u % 2, :], r3[:, :], r2[:, :], ALU.add).then_inc(qk_ready, 1)
                            if u:
                                third_part(u - 1)
                            dve.wait_ge(first_part, u + 1)
                            wait(dve, split, u - 1)
                            dve.tensor_tensor(rest[:, u % 2, :], qk[:, u % 2, :], SPL[:, j % 2, k, 0, :], ALU.subtract).then_inc(rest_ready, 1)
                        dve.wait_ge(v_psum, j + 1)
                        b, kc = j // 2, 4 * (j % 2)
                        for n in range(4):
                            ins = dve.tensor_tensor(VA[:, 4 * b:4 * b + 4, kc + n, :, 0:DH1],
                                                    ps[:, 7, P * n:P * (n + 1)].rearrange("p (g h d) -> p g h d", h=4, d=DH1),
                                                    w("b_uv_row").rearrange("p (g h d) -> p g h d", h=4, d=DH1), ALU.add)
                            if n < 3:
                                chain.add(ins)
                        ins.then_inc(v_read, 1)
                    third_part(2 * NJ - 1)
                    dve.wait_ge(split, 2 * NJ)
                    dve.wait_ge(v_read, NJ)

                @block.sync
                def _(sp):
                    for j in range(NJ):
                        b, pos = j // 2, slice(NB * (j % 2), NB * (j % 2 + 1))
                        for k, parts in enumerate((parts_q, parts_k)):
                            sp.wait_ge(split, 2 * j + k + 1)
                            dst = parts[:, D // 4 * b:D // 4 * (b + 1), :].rearrange("i r (h n) -> (r h) i n", h=4)
                            sp.dma_start(dst[:, :, pos], SPL[:, j % 2, k, :, :]).then_inc(parts_out[j % 2], 16)
                        if j == 1:
                            sp.wait_ge(parts_out[0], 16 * 2)
                            sp.wait_ge(parts_out[1], 16 * 2)
                            sp.wait_ge(rows_set, 1 + 3)
                            stack(sp, 0)

        PR = sb("PR", [P, 2, 4, S])
        OU = sb("OU", [P, S])
        MX = sb("MX", [P, 4, KC, 2])
        NM, R1, R2 = sb("NM", [P, KC]), sb("R1", [P, KC]), sb("R2", [P, KC])
        RD = sb("RD", [P, KC, 4])
        (st_used, pv_done, s_ready, smax_done, ms_ready, vg_ready, ou_ready, turned, small_done,
         rd_ready) = (sem("sm_" + n) for n in
                              "st_used pv_done s_ready smax_done ms_ready vg_ready ou_ready turned small_done rd_ready".split())
        SLOTS = 4 * KC
        ST, PV = 4, 6
        NQR = S // 4

        def items(last):
            out = []
            for s in range(SLOTS):
                out.append(("scores", s // 4, s % 4))
                if s == 1:
                    out.append(("maxima", 0, 3))
                if s in (10, 18, 26) and not last:
                    out.append(("maxima", 1, s // 8 - 1))
            return out

        def item_count(g, k, half=1):
            return 2 * (IT * g + 3 + k) + half + 1

        def slot_count(g, s, half=1, last=False):
            return item_count(g, items(last).index(("scores", s // 4, s % 4)), half)

        def maxima_item(g, h):
            if h == 3:
                return item_count(g, 2)
            if isinstance(g, int) and g == 0:
                return 2 * (h + 1)
            return item_count(g - 1, items(False).index(("maxima", 1, h)))

        def sums_in_slot(s):
            if s == 0:
                return [(1, KC - 2, 3)]
            if s in (1, 2):
                return [(1, KC - 1, 2 * s - 2), (1, KC - 1, 2 * s - 1)]
            if s in (6, 7, 8):
                return [(0, 0, s - 6)]
            if s == 9:
                return [(0, 0, 3), (0, 1, 0)]
            return [(0, (s - 5) // 4, (s - 5) % 4)] if s > 9 else []

        with nc.Block() as block:
            @block.sync
            def _(sp):
                for k in range(2):
                    sp.wait_ge(parts_out[k], 16 * TOK // NB)
                for g in range(1, NQ):
                    sp.wait_ge(rows_set, 1 + 3 * (g + 1))
                    stack(sp, g)
                with sp.Fori(NQ, NG) as g:
                    stack(sp, g)

            @block.gpsimd
            def _(pool):
                def values(g):
                    wait(pool, pv_done, SLOTS * g)
                    pool.tensor_copy(VG[:, :, :, 0:DH1 + 1],
                                     VA[:, bass.ds(g, 1), :, :, :].rearrange("p o k h d -> p (o k) h d")).then_inc(vg_ready, 1)

                values(0)
                pool.wait_ge(vg_ready, 1)
                for n in range(1, NQ):
                    stack_rows(pool, n)
                pool.wait_ge(rows_set, 1 + 3 * NQ)
                with pool.Fori(1, NG) as g:
                    values(g)

            @block.tensor
            def _(pe):
                def row_scores(g, x):
                    h, qt, par = x // KC, x % KC, g % NQ
                    if x == 0:
                        wait(pe, stacked, 16 * NSTACK * (g + 1))
                    wait(pe, smax_done, SLOTS * g + x - 1)
                    for n in range(2):
                        ins = pe.matmul(ps[:, 2 * (x % 2) + n, :], QS[0:MR, bass.ds(par, 1), h, P * qt:P * (qt + 1)].rearrange("p o n -> p (o n)"),
                                        KS[0:MR, bass.ds(par, 1), h, NB * n:NB * (n + 1)].rearrange("p o n -> p (o n)"),
                                        start=True, stop=True)
                    ins.then_inc(s_ready, 1)

                def maxima_rows(g, h, at):
                    wait(pe, ms_ready, 4 * g + h + 1)
                    for n in range(2):
                        wait(pe, st_used, at + n - 2)
                        for qt in range(4 * n, 4 * n + 4):
                            ins = pe.matmul(ps[0:KR, ST + n, P * (qt % 4):P * (qt % 4 + 1)], MS[:, h % 2, qt, :], idb[:, :],
                                            start=True, stop=True)
                        ins.then_inc(st_ready, 1)

                def key_scores(g, kc, h, at):
                    par = g % NQ
                    if kc == 0:
                        wait(pe, st_used, maxima_item(g, h))
                    for n in range(2):
                        wait(pe, st_used, at + n - 2)
                        pe.matmul(ps[:, ST + n, :], KS[0:KR, bass.ds(par, 1), h, P * kc:P * (kc + 1)].rearrange("p o n -> p (o n)"),
                                  QS[0:KR, bass.ds(par, 1), h, NB * n:NB * (n + 1)].rearrange("p o n -> p (o n)"),
                                  start=True, stop=True).then_inc(st_ready, 1)

                def values(g, kc, q, last=False):
                    if q == 0:
                        wait(pe, st_used, slot_count(g, 4 * kc + 3, 1, last))
                    if kc == 0:
                        wait(pe, vg_ready, g + 1)
                        wait(pe, rd_ready, 4 * (g - 1) + (4 if q > 1 else 2))
                    for h in range(4):
                        ins = pe.matmul(ps[32 * h:32 * (h + 1), PV + q // 2, NQR * (q % 2):NQR * (q % 2 + 1)], VG[:, kc, h, :],
                                        PR[:, kc % 2, h, NQR * q:NQR * (q + 1)], start=(kc == 0 and q % 2 == 0),
                                        stop=(kc == KC - 1), tile_position=(0, 32 * h), skip_group_check=True)
                    ins.then_inc(pv_done, 1)

                def turn(g, n):
                    wait(pe, ou_ready, 2 * g + n + 1)
                    for qt in range(4):
                        ins = pe.transpose(ps[:, PV + n, P * qt:P * (qt + 1)], OU[:, NB * n + P * qt:NB * n + P * (qt + 1)], ident)
                    ins.then_inc(turned, 1)

                def body(g, first, last):
                    s = 0
                    for k, (kind, kc, h) in enumerate(items(last)):
                        at = item_count(g, k, 0)
                        if kind == "maxima":
                            maxima_rows(g + kc, h, at)
                            continue
                        if s in (4, 6) and not first:
                            turn(g - 1, s // 2 - 2)
                        for back, chunk, q in sums_in_slot(s):
                            if not (first and back):
                                values(g - back, chunk, q, last and not back)
                        key_scores(g, kc, h, at)
                        if not last:
                            row_scores(g + 1, s)
                        s += 1

                for h in range(4):
                    for qt in range(KC):
                        row_scores(0, KC * h + qt)
                    if h:
                        maxima_rows(0, h - 1, 2 * h - 1)
                body(0, True, False)
                with pe.Fori(1, NG - 1) as g:
                    body(g, False, False)
                body(NG - 1, False, True)
                values(NG - 1, KC - 2, 3, True)
                for q in range(4):
                    values(NG - 1, KC - 1, q, True)
                for n in range(2):
                    turn(NG - 1, n)

            @block.scalar
            def _(act):
                def rows_out(g, h, at):
                    for n in range(2):
                        act.wait_ge(st_ready, at + n)
                        act.activation(QS[MR:KR, bass.ds(g % NQ, 1), h, NB * n:NB * (n + 1)], ps[MR:KR, ST + n, :].unsqueeze(1),
                                       ACT.Copy).then_inc(st_used, 1)

                def sums_out(g, n):
                    wait(act, pv_done, SLOTS * g + 4 * (KC - 1) + 2 * (n + 1))
                    act.activation(OU[:, NB * n:NB * (n + 1)], ps[:, PV + n, :], ACT.Copy).then_inc(ou_ready, 1)

                def body(g, first, last):
                    s = 0
                    for k, (kind, kc, h) in enumerate(items(last)):
                        at = item_count(g, k, 0)
                        if kind == "maxima":
                            rows_out(g + kc, h, at)
                            continue
                        for n in range(2):
                            act.wait_ge(st_ready, at + n)
                            wait(act, pv_done, SLOTS * g + 4 * (kc - 2) + 2 * (n + 1))
                            act.activation(PR[:, kc % 2, h, NB * n:NB * (n + 1)], ps[:, ST + n, :], ACT.Exp,
                                           scale=SCALE).then_inc(st_used, 1)
                        if s in (2, 3) and not first:
                            sums_out(g - 1, s - 2)
                        s += 1

                for h in range(3):
                    rows_out(0, h, 2 * h + 1)
                body(0, True, False)
                with act.Fori(1, NG - 1) as g:
                    body(g, False, False)
                body(NG - 1, False, True)
                for n in range(2):
                    sums_out(NG - 1, n)

            @block.vector
            def _(dve):
                def row_maxima(g, x):
                    h, qt = x // KC, x % KC
                    wait(dve, s_ready, SLOTS * g + x + 1)
                    if qt == 0:
                        wait(dve, small_done, 4 * (4 * g + h) - 12)
                    dve.tensor_reduce(MX[:, h, qt, :], ps[:, 2 * (x % 2):2 * (x % 2) + 2, :], AX.X, ALU.max).then_inc(smax_done, 1)

                def split_maxima(g, h):
                    par, base = h % 2, 4 * (4 * g + h)
                    wait(dve, smax_done, SLOTS * g + KC * (h + 1))
                    if not (isinstance(g, int) and g == 0 and h < 2):
                        wait(dve, st_ready, maxima_item(g, h - 2) if h >= 2 else maxima_item(g - 1, h + 2))
                    dve.tensor_reduce(NM[:, :], MX[:, h, :, :], AX.X, ALU.max, negate=True).then_inc(small_done, 1)
                    dve.wait_ge(small_done, base + 1)
                    dve.tensor_copy(MS[:, par, :, MR:MR + 1], NM[:, :].unsqueeze(2)).then_inc(small_done, 1)
                    dve.wait_ge(small_done, base + 2)
                    dve.tensor_tensor(R1[:, :].unsqueeze(2), NM[:, :].unsqueeze(2), MS[:, par, :, MR:MR + 1], ALU.subtract).then_inc(small_done, 1)
                    dve.wait_ge(small_done, base + 3)
                    dve.tensor_copy(MS[:, par, :, MR + 1:MR + 2], R1[:, :].unsqueeze(2)).then_inc(small_done, 1)
                    dve.wait_ge(small_done, base + 4)
                    dve.tensor_tensor(MS[:, par, :, MR + 2:MR + 3], R1[:, :].unsqueeze(2), MS[:, par, :, MR + 1:MR + 2],
                                      ALU.subtract).then_inc(ms_ready, 1)

                def divide(g, n):
                    wait(dve, turned, 2 * g + n + 1)
                    sums = ps[:, PV + n, :].rearrange("p (q h d) -> p q h d", h=4, d=32)
                    rd = RD[:, 4 * n:4 * n + 4, :].unsqueeze(3)
                    dve.reciprocal(rd, sums[:, :, :, DH1:DH1 + 1]).then_inc(rd_ready, 1)
                    dve.wait_ge(rd_ready, 4 * g + 2 * n + 1)
                    dve.tensor_tensor(ATT[:, bass.ds(g // 4, 1), 4 * n:4 * n + 4, bass.ds(g % 4, 1), :].rearrange("p o q r (h d) -> p (o q r) h d", h=4),
                                      sums[:, :, :, 0:DH1], rd.to_broadcast([P, 4, 4, DH1]), ALU.mult).then_inc(rd_ready, 1)

                def body(g, first, last):
                    for x in range(SLOTS):
                        if not last:
                            row_maxima(g + 1, x)
                            if x % KC == KC - 1:
                                split_maxima(g + 1, x // KC)
                        if x in (4, 5) and not first:
                            divide(g - 1, x - 4)

                for x in range(SLOTS):
                    row_maxima(0, x)
                    if x % KC == KC - 1:
                        split_maxima(0, x // KC)
                body(0, True, False)
                with dve.Fori(1, NG - 1) as g:
                    body(g, False, False)
                body(NG - 1, False, True)
                for n in range(2):
                    divide(NG - 1, n)
                dve.wait_ge(rd_ready, 4 * NG)

        attT = sb("attT", [P, 2, 4, P])
        t_ready, t_out, o_ready, y_ready = sem("so_t_ready"), sem("so_t_out"), sem("so_o_ready"), sem("so_y_ready")
        with nc.Block() as block:
            @block.tensor
            def _(pe):
                for j in range(TT // 4):
                    wait(pe, t_out, j - 1)
                    for n in range(4):
                        b, qt = (4 * j + n) // KC, (4 * j + n) % KC
                        ins = pe.transpose(ps[:, j % 2, P * n:P * (n + 1)], ATT[:, b, qt, :, :].rearrange("p g f -> p (g f)"), ident)
                    ins.then_inc(t_ready, 1)
                    pe.wait_ge(t_out, j + 1)
                    wait(pe, y_ready, j - 1)
                    for n in range(4):
                        ins = pe.matmul(ps[:, 2 + j % 2, P * n:P * (n + 1)], attT[:, j % 2, n, :], w("WoL1"), start=True, stop=True)
                    ins.then_inc(o_ready, 1)

            @block.scalar
            def _(act):
                for j in range(TT // 4):
                    act.wait_ge(t_ready, j + 1)
                    wait(act, o_ready, j - 1)
                    act.activation(attT[:, j % 2, :, :], ps[:, j % 2, :].rearrange("p (t d) -> p t d", d=P), ACT.Copy).then_inc(t_out, 1)

            @block.vector
            def _(dve):
                for j in range(TT // 4):
                    dve.wait_ge(o_ready, j + 1)
                    dve.tensor_tensor(Y[:, 4 * j:4 * j + 4, :], ps[:, 2 + j % 2, :].rearrange("p (t d) -> p t d", d=D),
                                      w("b_o_row").unsqueeze(1).to_broadcast([P, 4, D]), ALU.add).then_inc(y_ready, 1)
                    dve.wait_ge(y_ready, j + 1)
                    y_stat.block(dve, Y, j)
                y_stat.wait_all(dve)


def channel_mix(nc, sem, w, ident, ps, XNT, Y, y_stat):
    NJ = TOK // NB
    with ExitStack() as c:
        def sb(name, shape, dt=F32):
            return c.enter_context(nc.sbuf_tensor("cm_" + name, shape, dt))

        om = sb("om", [P, 2])
        pr, pk = sb("pr", [P, TOK]), sb("pk", [P, TOK])
        xr, xk = sb("xr", [P, TOK]), sb("xk", [P, TOK])
        r, kr, ka, o = sb("r", [P, 2, NB]), sb("kr", [P, 2, NB]), sb("ka", [P, 2, NB]), sb("o", [P, 2, NB])
        one_minus, shifted, zero, mixed = sem("cm_one_minus"), sem("cm_shifted"), sem("cm_zero"), sem("cm_mixed")
        rk_ready, r_out, k_out, ka_ready, v_ready, o_ready, turned, y_ready = (
            sem("cm_" + n) for n in "rk_ready r_out k_out ka_ready v_ready o_ready turned y_ready".split())

        with nc.Block() as block:
            @block.vector
            def _(dve):
                dve.tensor_scalar(om[:, 0:1], w("mu_r"), -1.0, 1.0, ALU.mult, ALU.add).then_inc(one_minus, 1)
                dve.tensor_scalar(om[:, 1:2], w("mu_k"), -1.0, 1.0, ALU.mult, ALU.add).then_inc(one_minus, 1)
                dve.wait_ge(one_minus, 2)
                dve.wait_ge(zero, 4)
                for b in range(B):
                    for n, dst in enumerate((pr, pk)):
                        dve.tensor_scalar(dst[:, S * b + 1:S * (b + 1)], XNT[:, S * b:S * (b + 1) - 1], om[:, n:n + 1], None,
                                          ALU.mult).then_inc(shifted, 1)
                for b in range(B):
                    for h in range(2):
                        a = S * b + NB * h
                        dve.wait_ge(shifted, 2 * (b + 1))
                        for mu, p, x in (("mu_r", pr, xr), ("mu_k", pk, xk)):
                            dve.scalar_tensor_tensor(out=x[:, a:a + NB], in0=XNT[:, a:a + NB], scalar=w(mu), in1=p[:, a:a + NB],
                                                     op0=ALU.mult, op1=ALU.add).then_inc(mixed, 1)
                for j in range(NJ):
                    dve.wait_ge(k_out, j + 1)
                    wait(dve, v_ready, j - 1)
                    dve.tensor_tensor(ka[:, j % 2, :], kr[:, j % 2, :], kr[:, j % 2, :], ALU.mult).then_inc(ka_ready, 1)
                    dve.wait_ge(v_ready, j + 1)
                    dve.wait_ge(r_out, j + 1)
                    wait(dve, turned, j - 1)
                    dve.tensor_tensor(o[:, j % 2, :], r[:, j % 2, :], ps[:, 4 + j % 2, :], ALU.mult).then_inc(o_ready, 1)
                    if j:
                        dve.wait_ge(y_ready, j)
                        y_stat.block(dve, Y, j - 1)
                dve.wait_ge(y_ready, NJ)
                y_stat.block(dve, Y, NJ - 1)
                y_stat.wait_all(dve)

            @block.gpsimd
            def _(pool):
                for b in range(B):
                    for dst in (pr, pk):
                        pool.memset(dst[:, S * b:S * b + 1], 0.0).then_inc(zero, 1)

            @block.tensor
            def _(pe):
                def rk(j):
                    pe.wait_ge(mixed, 2 * (j + 1))
                    wait(pe, r_out, j - 1)
                    wait(pe, k_out, j - 1)
                    pe.matmul(ps[:, j % 2, :], w("W_rT"), xr[:, NB * j:NB * (j + 1)], start=True, stop=True)
                    pe.matmul(ps[:, 2 + j % 2, :], w("W_kT"), xk[:, NB * j:NB * (j + 1)], start=True, stop=True).then_inc(rk_ready, 1)

                rk(0)
                for j in range(NJ):
                    if j + 1 < NJ:
                        rk(j + 1)
                    pe.wait_ge(ka_ready, j + 1)
                    wait(pe, o_ready, j - 1)
                    pe.matmul(ps[:, 4 + j % 2, :], w("W_vT"), ka[:, j % 2, :], start=True, stop=True).then_inc(v_ready, 1)
                    pe.wait_ge(o_ready, j + 1)
                    wait(pe, y_ready, j - 1)
                    for n in range(4):
                        ins = pe.transpose(ps[:, 6 + j % 2, P * n:P * (n + 1)], o[:, j % 2, P * n:P * (n + 1)], ident)
                    ins.then_inc(turned, 1)

            @block.scalar
            def _(act):
                for j in range(NJ):
                    act.wait_ge(rk_ready, j + 1)
                    wait(act, ka_ready, j - 1)
                    act.activation(kr[:, j % 2, :], ps[:, 2 + j % 2, :], ACT.Relu).then_inc(k_out, 1)
                    wait(act, o_ready, j - 1)
                    act.activation(r[:, j % 2, :], ps[:, j % 2, :], ACT.Sigmoid).then_inc(r_out, 1)
                    act.wait_ge(turned, j + 1)
                    act.activation(Y[:, 4 * j:4 * j + 4, :], ps[:, 6 + j % 2, :].rearrange("p (t d) -> p t d", d=D),
                                   ACT.Copy).then_inc(y_ready, 1)
                act.wait_ge(y_ready, NJ)


def _packed(pack, parts):
    cols = []
    for name, n in pack:
        a = np.asarray(parts[name])
        full = np.zeros((P, n), np.float32)
        full[:a.shape[0], :] = a.reshape(a.shape[0], n)
        cols.append(full)
    return np.ascontiguousarray(np.concatenate(cols, axis=1))


def _layout(x):
    def col(v):
        return np.asarray(v).reshape(-1, 1)

    def rows(v, n=P):
        return np.broadcast_to(np.asarray(v).reshape(1, -1), (n, np.asarray(v).size))

    def low(a):
        return np.concatenate([a, np.zeros((P - a.shape[0], a.shape[1]), a.dtype)], 0)

    def high(a):
        return np.concatenate([np.zeros((P - a.shape[0], a.shape[1]), a.dtype), a], 0)

    g = {k: np.asarray(v) for k, v in x.items()}
    pair = np.arange(D) ^ 1
    b1row = np.zeros((P, HID), np.float32)
    b1row[[0, 32, 64]] = g["L0_attn_b1"]
    masks, ones3 = _constants()
    a = {
        "masks": masks, "ones3": ones3,
        "woT": g["L0_attn_wo"].T, "wqT": g["L0_attn_wq"].T, "wkT": g["L0_attn_wk"].T, "wvT": g["L0_attn_wv"].T,
        "ident": np.eye(P, dtype=np.float32),
        "headmask": (np.arange(P)[:, None] // DH0 == np.arange(NH0)).astype(np.float32),
        "b1row": b1row, "b2row": rows(g["L0_attn_b2"]), "alpha": rows(g["L0_attn_alpha"]), "theta": rows(g["L0_attn_theta"]),
        "b1col": g["L0_attn_b1"].reshape(HC, P).T, "b2col": col(g["L0_attn_b2"]), "ones": np.ones((P, 1), np.float32),
        "w1T": g["L0_attn_w1"].T, "w2": g["L0_attn_w2"],
        "w2T": g["L0_attn_w2"].T.reshape(HC, P, D).transpose(1, 0, 2).reshape(P, HID),
    }
    b = {
        "lin1T": g["L0_attn_lin1"].T, "lin2T": g["L0_attn_lin2"].T, "routerT": g["L0_ffn_router_w"].T,
        "expert_no": rows(np.arange(E, dtype=np.float32)),
        "WgT": g["L0_ffn_Wg"].transpose(2, 0, 1).reshape(D, E * I), "WuT": g["L0_ffn_Wu"].transpose(2, 0, 1).reshape(D, E * I),
        "WdT": g["L0_ffn_Wd"].transpose(0, 2, 1).reshape(E * I // P, P, D).transpose(1, 0, 2).reshape(P, E * I // P * D),
    }
    theta = np.float32(10000.0) ** (np.float32(-2.0) * np.arange(D // 2, dtype=np.float32)) / np.float32(D // 2)
    angle = (np.arange(S, dtype=np.float32)[:, None] * theta[None, :]).astype(np.float64)
    cos, sin = np.cos(angle).astype(np.float32), np.sin(angle).astype(np.float32)
    sin_signed = np.repeat(sin.T, 2, axis=0)
    sin_signed[0::2] = -sin_signed[0::2]
    q = {k[8:]: v for k, v in g.items() if k.startswith("L1_attn_")}
    order = np.arange(D).reshape(NH1 // 4, 4, DH1).transpose(0, 2, 1).reshape(D)
    pair = pair[order]
    cc = {
        "Wdown": np.concatenate([q["Wd_q_w"], q["Wd_kv_w"]], 1),
        "Wuq": low(q["Wu_q_w"][:, order]), "Wqr": low(q["Wq_r_w"][:, order]), "Wqr_sw": low(q["Wq_r_w"][:, pair]),
        "Wuk": high(q["Wu_k_w"][:, order]), "Wkr": q["Wk_r_w"][:, order], "Wkr_sw": q["Wk_r_w"][:, pair], "Wuv": high(q["Wu_v_w"]),
        "b_down": col(np.concatenate([q["Wd_q_b"], q["Wd_kv_b"]])), "b_uq": col(q["Wu_q_b"][order]), "b_qr": col(q["Wq_r_b"][order]),
        "b_qr_sw": col(q["Wq_r_b"][pair]), "b_uk": col(q["Wu_k_b"][order]), "b_kr": col(q["Wk_r_b"][order]), "b_kr_sw": col(q["Wk_r_b"][pair]),
        "b_uv_row": rows(q["Wu_v_b"]), "WoL1": q["Wo_w"], "b_o_row": rows(q["Wo_b"]),
        "cos": np.repeat(cos.T, 2, axis=0)[order], "sin": sin_signed[order],
        "W_rT": g["L1_ffn_W_r"].T, "W_kT": g["L1_ffn_W_k"].T, "W_vT": g["L1_ffn_W_v"].T,
        "mu_r": col(g["L1_ffn_mu_r"]), "mu_k": col(g["L1_ffn_mu_k"]),
    }
    return _packed(PACK_A, a), _packed(PACK_B, b), _packed(PACK_C, cc)


def _constants():
    r, k = np.arange(P)[:, None], np.arange(KW)[None, :]
    seen = (k > r) & (k <= r + WIN)
    tiles = [seen, seen & (k >= NPM), seen & ((r < NPM) | (k >= P))]
    ones3 = np.zeros((P, P), np.float32)
    ones3[[0, 32, 64]] = 1
    return np.concatenate([np.where(m, 0.0, -2.0 ** 100) for m in tiles], 1).astype(np.float32), ones3


def kernel(**inputs):
    import concourse.bacc as bacc
    from concourse.bass_utils import run_bass_kernel_spmd

    pack_a, pack_b, pack_c = _layout({k: v for k, v in inputs.items() if k not in ("L0_attn_x", "L0_attn_mem")})
    arrays = {"pack_a": pack_a, "pack_b": pack_b, "pack_c": pack_c,
              "x_in": np.ascontiguousarray(np.asarray(inputs["L0_attn_x"]).reshape(TOK, D)),
              "mem": np.ascontiguousarray(np.asarray(inputs["L0_attn_mem"]))}
    nc = bacc.Bacc("TRN2", target_bir_lowering=False, num_devices=1)
    aps = [nc.dram_tensor(n, a.shape, mybir.dt.from_np(a.dtype), kind="ExternalInput").ap() for n, a in arrays.items()]
    out = nc.dram_tensor("out", [TOK, D], F32, kind="ExternalOutput").ap()
    build(nc, *aps, out)
    r = run_bass_kernel_spmd(nc, [arrays], core_ids=[0])
    return r.results[0]["out"].reshape(B, S, D)
```

```python
from contextlib import ExitStack

import numpy as np

import concourse.bass as bass
from concourse import mybir

F32 = mybir.dt.float32
BF16 = mybir.dt.bfloat16
U32 = mybir.dt.uint32
ALU = mybir.AluOpType
ACT = mybir.ActivationFunctionType
AX = mybir.AxisListType

P = 128
B, S, D = 2, 1024, 128
NPM = 64
SM = S + NPM
ROWS = B * SM
T0 = ROWS // P
TOK = B * S
TT = TOK // P
HID = 512
HC = HID // P
NH0, DH0, WIN = 4, 32, 64
KW = P + WIN
PADC = P * (T0 + 1)
E, TOPK, I = 8, 2, 352
NH1, DH1 = 16, 8
DC = 64
NB = 512
NJT = TOK // NB
EPS = 1e-5

PACK_A = [("woT", D), ("wqT", D), ("wkT", D), ("wvT", D), ("ident", P), ("headmask", NH0), ("b1row", HID),
          ("b2row", D), ("alpha", 1), ("theta", 1), ("b1col", HC), ("b2col", 1), ("ones", 1), ("masks", 3 * KW), ("ones3", P),
          ("w1T", HID), ("w2", HID), ("w2T", HID)]
PACK_B = [("lin1T", D), ("lin2T", D), ("routerT", E), ("expert_no", E),
          ("WgT", E * I), ("WuT", E * I), ("WdT", E * I // P * D)]
PACK_C = [("Wdown", D), ("Wuq", D), ("Wqr", D), ("Wqr_sw", D), ("Wuk", D), ("Wkr", D), ("Wkr_sw", D), ("Wuv", D),
          ("b_down", 1), ("b_uq", 1), ("b_qr", 1), ("b_qr_sw", 1), ("b_uk", 1), ("b_kr", 1), ("b_kr_sw", 1),
          ("b_uv_row", D), ("WoL1", D), ("b_o_row", D), ("cos", S), ("sin", S),
          ("W_rT", D), ("W_kT", D), ("W_vT", D), ("mu_r", 1), ("mu_k", 1)]


def offsets(pack):
    at, out = 0, {}
    for name, n in pack:
        out[name] = (at, n)
        at += n
    return out, at


class Count:

    def __init__(self, sem):
        self.sem, self.n = sem, 0

    def add(self, ins):
        self.n += 1
        ins.then_inc(self.sem, 1)
        return self.n


def build(nc, packA, packB, packC, x_in, mem, out):
    offA, nA = offsets(PACK_A)
    offB, nB = offsets(PACK_B)
    offC, nC = offsets(PACK_C)
    ctx = ExitStack()
    with ctx:
        def sb(name, shape, dt=F32, c=ctx):
            return c.enter_context(nc.sbuf_tensor(name, shape, dt))

        def sem(name):
            return ctx.enter_context(nc.semaphore(name))

        WA = sb("WA", [P, nA])
        WB = sb("WB", [P, nB])
        held = [(offA, WA), (offB, WB)]

        def w(name):
            for off, t in held:
                if name in off:
                    a, n = off[name]
                    return t[:, a:a + n]

        ident = w("ident")
        idb = sb("idb", [P, P], BF16)
        X = sb("X", [P, TT, D])
        Y = sb("Y", [P, TT, D])
        stats, mv = sb("y_stats", [P, TT, 6]), sb("y_mv", [P, TT, 2])
        epsc = sb("epsc", [P, 1])
        ps = ctx.enter_context(nc.psum_tensor("ps", [P, 8, NB], F32))
        loaded_a, loaded_b, loaded_c, loaded_x = sem("loaded_a"), sem("loaded_b"), sem("loaded_c"), sem("loaded_x")

        y_summed, y_stats_done = sem("y_summed"), sem("y_stats_done")
        norm_sems = {n: sem("rn_" + n) for n in (*NORM_SEMS, "xn_scalar", "xn_vector")}

        def y_statistics(k):
            return RowStatistics(stats, mv, y_summed, y_stats_done, TT * k)

        def norm(number, c, banks, out=None, places=None):
            return ResidualNorm(nc, c, norm_sems, ident, ps, X, Y, y_statistics(number), epsc, number, banks, out, places)

        ATT = sb("ATT", [P, TT, D])
        n0 = norm(0, ctx, (0, 1, 2, 3), places=(Y, ATT))
        n1 = norm(1, ctx, (7, 6, 5, 4), places=(Y, ATT))
        n2 = norm(2, ctx, (4, 5, 6, 7), places=(Y, ATT))
        first_layer(nc, sem, w, ident, idb, ps, X, Y, n0, epsc, WA, WB, packA, packB, x_in, mem,
                    loaded_a, loaded_b, loaded_x)
        WC = sb("WC", [P, nC])
        held.append((offC, WC))
        XNT = sb("XNT", [P, TOK])
        experts(nc, sem, w, ident, ps, XNT, Y, n0, n1, y_statistics(1), loaded_b, WC, packC, loaded_c)
        second_attention(nc, sem, w, ident, idb, ps, XNT, Y, ATT, n1, n2, loaded_c)
        channel_mix(nc, sem, w, ident, ps, XNT, Y, n2, norm, y_statistics(3), out)


def norm_statistics(dve, chain, src, tiles, stats, mv):
    for t in range(tiles):
        last = chain.add(dve.bn_stats(stats[:, t, :], src[:, t, :]))
    for t in range(tiles):
        dve.wait_ge(chain.sem, last - tiles + 1 + t)
        n = chain.add(dve.bn_aggr(mv[:, t, :], stats[:, t, :]))
    return n


class RowStatistics:

    def __init__(self, stats, mv, summed, done, base):
        self.stats, self.mv, self.summed, self.done, self.base = stats, mv, summed, done, base

    def sums(self, dve, src, j):
        for n in range(4):
            dve.bn_stats(self.stats[:, bass.ds(4 * j + n, 1), :].rearrange("p o k -> p (o k)"),
                         src[:, bass.ds(4 * j + n, 1), :].rearrange("p o k -> p (o k)")).then_inc(self.summed, 1)

    def results(self, dve, j):
        for t in range(4 * j, 4 * j + 4):
            dve.wait_ge(self.summed, self.base + t + 1)
            dve.bn_aggr(self.mv[:, t, :], self.stats[:, t, :]).then_inc(self.done, 1)

    def block(self, dve, src, j):
        self.sums(dve, src, j)
        self.results(dve, j)

    def wait_all(self, dve):
        dve.wait_ge(self.done, self.base + TT)


NORM_SEMS = {"std_ready": TT // 4, "factors": TT // 2, "std2_ready": TT // 4, "factors2": TT // 2, "xp_ready": TT, "x_summed": TT, "x_stats": TT,
             "x_ready": TT // 4, "turned": TT // 4, "evac": TT // 4, "stored": 0}
XN_BY_SCALAR = (3, 1, 3, 0)


class ResidualNorm:

    def __init__(self, nc, c, sems, ident, ps, X, Y, y_stat, epsc, number, banks, out=None, places=None):
        def sb(name, shape, dt=F32):
            return c.enter_context(nc.sbuf_tensor("r%d_" % number + name, shape, dt))

        self.sems, self.ident, self.ps, self.X, self.Y, self.epsc = sems, ident, ps, X, Y, epsc
        self.number, self.banks, self.out, self.y_stat, self.mv = number, banks, out, y_stat, y_stat.mv
        self.std, self.rstd, self.shift = sb("std", [P, TT, 1]), sb("rstd", [P, TT, 1]), sb("shift", [P, TT, 1])
        self.XP, self.XN = places or (sb("XP", [P, TT, D]), None if out is not None else sb("XN", [P, TT, D]))
        if out is None:
            self.mv2 = sb("mv2", [P, TT, 2])
            self.own = RowStatistics(sb("stats2", [P, TT, 6]), self.mv2, sems["x_summed"], sems["x_stats"], TT * number)
            self.std2, self.rstd2, self.shift2 = sb("std2", [P, TT, 1]), sb("rstd2", [P, TT, 1]), sb("shift2", [P, TT, 1])

    def at_least(self, eng, name, value):
        if name == "xn_scalar":
            base = 4 * sum(XN_BY_SCALAR[:self.number])
        elif name == "xn_vector":
            base = sum(TT - 4 * n for n in XN_BY_SCALAR[:self.number])
        else:
            base = NORM_SEMS[name] * self.number
        eng.wait_ge(self.sems[name], base + value)

    def factors(self, dve, j, src, std, rstd, shift, deviation, ready):
        g = slice(4 * j, 4 * j + 4)
        self.at_least(dve, deviation, j + 1)
        dve.reciprocal(rstd[:, g, :], std[:, g, :]).then_inc(self.sems[ready], 1)
        self.at_least(dve, ready, 2 * j + 1)
        dve.scalar_tensor_tensor(out=shift[:, g, :], in0=src[:, g, 0:1], scalar=-1.0, in1=rstd[:, g, :],
                                 op0=ALU.mult, op1=ALU.mult).then_inc(self.sems[ready], 1)

    def factors_y(self, dve, j):
        self.factors(dve, j, self.mv, self.std, self.rstd, self.shift, "std_ready", "factors")

    def factors_x(self, dve, j):
        self.factors(dve, j, self.mv2, self.std2, self.rstd2, self.shift2, "std2_ready", "factors2")

    def sum_x(self, dve, j):
        for t in range(4 * j, 4 * j + 4):
            dve.scalar_tensor_tensor(out=self.XP[:, t, :], in0=self.Y[:, t, :], scalar=self.rstd[:, t, :], in1=self.X[:, t, :],
                                     op0=ALU.mult, op1=ALU.add).then_inc(self.sems["xp_ready"], 1)
        self.at_least(dve, "xp_ready", 4 * j + 4)
        self.own.block(dve, self.XP, j)

    def sum_tile(self, dve, t):
        dve.scalar_tensor_tensor(out=self.XP[:, t, :], in0=self.Y[:, t, :], scalar=self.rstd[:, t, :], in1=self.X[:, t, :],
                                 op0=ALU.mult, op1=ALU.add).then_inc(self.sems["xp_ready"], 1)
        self.at_least(dve, "xp_ready", t + 1)
        dve.bn_stats(self.own.stats[:, t, :], self.XP[:, t, :]).then_inc(self.own.summed, 1)

    def xn_by_vector(self, dve, j):
        self.at_least(dve, "factors2", 2 * j + 2)
        for t in range(4 * j, 4 * j + 4):
            dve.tensor_scalar(self.XN[:, t, :], self.XP[:, t, :], self.rstd2[:, t, :], self.shift2[:, t, :], ALU.mult,
                              ALU.add).then_inc(self.sems["xn_vector"], 1)

    def vector(self, dve, begun=False):
        if not begun:
            for j in range(NJT):
                self.factors_y(dve, j)
            self.sum_x(dve, 0)
        for j in range(1, NJT):
            self.sum_x(dve, j)
            if not (begun and j == 1):
                self.factors_x(dve, j - 1)
        self.factors_x(dve, NJT - 1)
        self.xn_by_vector(dve, NJT - 1)

    def deviation_y(self, act, j):
        g = slice(4 * j, 4 * j + 4)
        act.wait_ge(self.y_stat.done, self.y_stat.base + 4 * j + 4)
        act.activation(self.std[:, g, :], self.mv[:, g, 1:2], ACT.Sqrt, bias=self.epsc[:, :]).then_inc(self.sems["std_ready"], 1)

    def deviation_x(self, act, j):
        g = slice(4 * j, 4 * j + 4)
        self.at_least(act, "x_stats", 4 * j + 4)
        act.activation(self.std2[:, g, :], self.mv2[:, g, 1:2], ACT.Sqrt, bias=self.epsc[:, :]).then_inc(self.sems["std2_ready"], 1)

    def scaled(self, act, j, dst, src, scale, bias, ready):
        for t in range(4 * j, 4 * j + 4):
            act.activation(dst[:, t, :], src[:, t, :], ACT.Identity, bias=bias[:, t, :], scale=scale[:, t, :]).then_inc(self.sems[ready], 1)

    def xnt_of(self, act, j, XNT):
        self.at_least(act, "turned", j + 1)
        act.activation(XNT[:, NB * j:NB * (j + 1)], self.ps[:, self.banks[j], :], ACT.Copy).then_inc(self.sems["evac"], 1)

    def scalar(self, act, XNT, after, begun=False):
        if not begun:
            for j in range(NJT):
                self.deviation_y(act, j)
            self.deviation_x(act, 0)
        for j in range(NJT):
            if j + 1 < NJT:
                self.deviation_x(act, j + 1)
                self.at_least(act, "factors2", 2 * j + 2)
                self.scaled(act, j, self.XN, self.XP, self.rstd2, self.shift2, "xn_scalar")
            if j:
                self.xnt_of(act, j - 1, XNT)
                after(j - 1)
        self.xnt_of(act, NJT - 1, XNT)
        after(NJT - 1)

    def gpsimd(self, pool):
        for j in range(NJT):
            g = slice(4 * j, 4 * j + 4)
            self.at_least(pool, "factors", 2 * j + 2)
            self.at_least(pool, "xp_ready", 4 * j + 4)
            pool.tensor_tensor(self.X[:, g, :], self.XP[:, g, :], self.shift[:, g, :].to_broadcast([P, 4, D]),
                               ALU.add).then_inc(self.sems["x_ready"], 1)
        self.at_least(pool, "x_ready", NJT)

    def turn(self, pe, j):
        for n in range(4):
            t = 4 * j + n
            if j < XN_BY_SCALAR[self.number]:
                self.at_least(pe, "xn_scalar", t + 1)
            else:
                self.at_least(pe, "xn_vector", t + 1 - 4 * XN_BY_SCALAR[self.number])
            ins = pe.transpose(self.ps[:, self.banks[j], P * n:P * (n + 1)], self.XN[:, t, :], self.ident)
        ins.then_inc(self.sems["turned"], 1)

    def last_by_scalar(self, act, j):
        self.at_least(act, "factors", 2 * j + 2)
        self.scaled(act, j, self.XP, self.Y, self.rstd, self.shift, "xp_ready")

    def last_by_vector(self, dve, j):
        self.at_least(dve, "factors", 2 * j + 2)
        for t in range(4 * j, 4 * j + 4):
            dve.tensor_scalar(self.XP[:, t, :], self.Y[:, t, :], self.rstd[:, t, :], self.shift[:, t, :], ALU.mult,
                              ALU.add).then_inc(self.sems["xn_vector"], 1)

    def last_sum(self, dve, j):
        g = slice(4 * j, 4 * j + 4)
        if j < NJT // 2:
            self.at_least(dve, "xp_ready", 4 * j + 4)
        else:
            self.at_least(dve, "xn_vector", 4 * (j - NJT // 2) + 4)
        dve.tensor_tensor(self.X[:, g, :], self.X[:, g, :], self.XP[:, g, :], ALU.add).then_inc(self.sems["x_ready"], 1)

    def store(self, sp):
        rows = self.out.rearrange("(t p) d -> p t d", p=P)
        for j in range(NJT):
            self.at_least(sp, "x_ready", j + 1)
            sp.dma_start(rows[:, 4 * j:4 * j + 4, :], self.X[:, 4 * j:4 * j + 4, :]).then_inc(self.sems["stored"], 16)
        self.at_least(sp, "stored", 16 * NJT)


def first_layer(nc, sem, w, ident, idb, ps, X, Y, n0, epsc, WA, WB, packA, packB, x_in, mem,
                loaded_a, loaded_b, loaded_x):
    SCALE = 1.0 / float(np.sqrt(DH0).astype(np.float32))
    with ExitStack() as c0:
        def sb(name, shape, dt=F32):
            return c0.enter_context(nc.sbuf_tensor(name, shape, dt))

        XT = sb("XT", [P, PADC])
        OT = sb("OT", [P, ROWS])
        dzsum = sb("dzsum", [P, HID])
        errsum = sb("errsum", [P, D])
        G1, G2 = ps[:, 6, :], ps[:, 7, :]
        with ExitStack() as c:
            def sbi(name, shape, dt=F32):
                return c.enter_context(nc.sbuf_tensor(name, shape, dt))

            XR = sbi("XR", [P, T0, D])
            XN = sbi("XN", [P, T0, D])
            KM = sbi("KM", [P, NH0, PADC])
            QT = sbi("QT", [P, PADC])
            V = sbi("V", [P, T0 + 1, D])
            masks = sbi("masks", [P, 3, 2, KW], BF16)
            ones_b = sbi("ones_b", [P, P], BF16)
            stats, mv = sbi("stats", [P, T0, 6]), sbi("mv", [P, T0, 2])
            std, rstd = sbi("std", [P, T0, 1]), sbi("rstd", [P, T0, 1])
            b1s = sbi("b1s", [P, HID], BF16)
            b1t = sbi("b1t", [P, 2, HID])
            b1h = sbi("b1h", [P, 2, HID], BF16)
            nwoT = sbi("nwoT", [P, D])
            mem_in, dve_done, var_ready, std_ready = (sem("mem_in"), sem("l0_dve_done"), sem("l0_var_ready"),
                                                      sem("l0_std_ready"))
            x_padded = sem("x_padded")
            xn_ready, turned, xt_ready = sem("l0_xn_ready"), sem("l0_turned"), sem("l0_xt_ready")
            qk_ready, q_out, k_out, k_out_dve, v_ready, v_out, v_out_dve = (
                sem(n) for n in "qk_ready q_out k_out k_out_dve v_ready v_out v_out_dve".split())
            x_in_ready, cast = sem("x_in_ready"), sem("l0_cast")
            pool_init = sem("pool_init")
            GROUPS = [range(0, 4), range(4, 8), range(8, 12), range(12, T0)]
            OWN = [(0, 0, NPM), (8, NPM, P)]

            with nc.Block() as block:
                @block.sync
                def _(sp):
                    sp.dma_start(XR[NPM:P, 0, :], x_in[0:NPM, :]).then_inc(loaded_x, 16)
                    sp.dma_start(XR[:, 1:8, :], x_in[NPM:NPM + 7 * P, :].rearrange("(t p) d -> p t d", p=P)).then_inc(loaded_x, 16)
                    sp.dma_start(XR[0:NPM, 8, :], x_in[S - NPM:S, :]).then_inc(loaded_x, 16)
                    sp.dma_start(XR[:, 9:T0, :], x_in[S:TOK, :].rearrange("(t p) d -> p t d", p=P)).then_inc(loaded_x, 16)
                    for t, a, b in OWN:
                        sp.dma_start(XR[a:b, t, :], mem).then_inc(loaded_x, 16)
                        sp.dma_start(XN[a:b, t, :], mem).then_inc(mem_in, 16)
                    sp.dma_start(X[:, :, :], x_in.rearrange("(t p) d -> p t d", p=P)).then_inc(x_in_ready, 16)
                    sp.dma_start(WB[:, :], packB).then_inc(loaded_b, 16)

                @block.gpsimd
                def _(pool):
                    pool.memset(epsc[:, :], EPS).then_inc(pool_init, 1)
                    pool.memset(XT[:, 0:NPM], 0.0).then_inc(x_padded, 1)
                    pool.memset(XT[:, PADC - NPM:PADC], 0.0).then_inc(x_padded, 1)
                    pool.memset(b1s[:, :], 0.0).then_inc(pool_init, 1)
                    pool.memset(dzsum[:, :], 0.0).then_inc(pool_init, 1)
                    pool.memset(errsum[:, :], 0.0).then_inc(pool_init, 1)
                    pool.wait_ge(loaded_a, 16)
                    pool.tensor_copy(idb[:, :], ident).then_inc(cast, 1)
                    pool.tensor_copy(ones_b[:, :], w("ones3")).then_inc(cast, 1)
                    for n in range(2):
                        pool.tensor_copy(masks[:, :, n, :], w("masks").rearrange("p (m k) -> p m k", m=3)).then_inc(cast, 1)

                    def then(ins):
                        pool.wait_ge(cast, casts.add(ins))

                    casts = Count(cast)
                    casts.n = 4
                    pool.wait_ge(cast, 4)
                    b1 = w("b1row")
                    pool.wait_ge(pool_init, 2)
                    then(pool.tensor_copy(b1h[:, 0, :], b1))
                    then(pool.tensor_tensor(b1t[:, 0, :], b1, b1h[:, 0, :], ALU.subtract))
                    then(pool.tensor_copy(b1h[:, 1, :], b1t[:, 0, :]))
                    then(pool.tensor_tensor(b1t[:, 1, :], b1t[:, 0, :], b1h[:, 1, :], ALU.subtract))
                    then(pool.tensor_copy(b1s[0:1, :], b1h[0:1, 0, :]))
                    then(pool.tensor_copy(b1s[32:33, :], b1h[32:33, 1, :]))
                    then(pool.tensor_copy(b1s[64:65, :], b1t[64:65, 1, :]))
                    then(pool.tensor_scalar(nwoT[:, :], w("woT"), -1.0, None, ALU.mult))

                @block.vector
                def _(dve):
                    chain = Count(dve_done)
                    dve.wait_ge(loaded_x, 16 * 6)

                    def statistics(k):
                        for t in GROUPS[k]:
                            last = chain.add(dve.bn_stats(stats[:, t, :], XR[:, t, :]))
                        for n, t in enumerate(GROUPS[k]):
                            dve.wait_ge(dve_done, last - len(GROUPS[k]) + 1 + n)
                            ins = dve.bn_aggr(mv[:, t, :], stats[:, t, :])
                            if t == GROUPS[k][-1]:
                                ins.then_inc(var_ready, 1)
                            else:
                                chain.add(ins)

                    def normalise(k):
                        g = slice(GROUPS[k][0], GROUPS[k][-1] + 1)
                        dve.wait_ge(std_ready, k + 1)
                        dve.wait_ge(dve_done, chain.add(dve.reciprocal(rstd[:, g, :], std[:, g, :])))
                        for t in GROUPS[k]:
                            a, b = {0: (NPM, P), 8: (0, NPM)}.get(t, (0, P))
                            dve.tensor_scalar(XN[a:b, t, :], XR[a:b, t, :], mv[a:b, t, 0:1], rstd[a:b, t, :],
                                              ALU.subtract, ALU.mult).then_inc(xn_ready, 1)

                    statistics(0)
                    statistics(1)
                    for k in range(len(GROUPS)):
                        normalise(k)
                        if k + 2 < len(GROUPS):
                            statistics(k + 2)
                    dve.wait_ge(loaded_a, 16)
                    for j in range(5):
                        dve.wait_ge(qk_ready, 2 * j + 2)
                        n = NB if j < 4 else PADC - 4 * NB
                        dve.wait_ge(k_out, 2 * (j + 1))
                        for h in (2, 3):
                            dve.tensor_scalar(KM[:, h, NB * j:NB * j + n], ps[:, 4 + j % 2, 0:n],
                                              w("headmask")[:, h:h + 1], None, ALU.mult).then_inc(k_out_dve, 1)
                    for j in (1, 3):
                        dve.wait_ge(v_ready, j + 1)
                        dve.tensor_copy(V[:, 4 * j:4 * j + 4, :], ps[:, 6 + j % 2, :].rearrange("p (t d) -> p t d", d=P)).then_inc(v_out_dve, 1)
                    dve.wait_ge(v_out_dve, 2)

                @block.scalar
                def _(act):
                    act.dma_start(WA[:, :], packA).then_inc(loaded_a, 16)
                    act.wait_ge(pool_init, 1)

                    def deviations(k):
                        g = slice(GROUPS[k][0], GROUPS[k][-1] + 1)
                        act.wait_ge(var_ready, k + 1)
                        act.activation(std[:, g, :], mv[:, g, 1:2], ACT.Sqrt, bias=epsc[:, :]).then_inc(std_ready, 1)

                    def xt_of(j):
                        act.wait_ge(turned, j + 1)
                        n = NB if j < 4 else P
                        act.activation(XT[:, NPM + NB * j:NPM + NB * j + n], ps[:, j % 2, 0:n], ACT.Copy).then_inc(xt_ready, 1)

                    def qk_of(j):
                        n = NB if j < 4 else PADC - 4 * NB
                        act.wait_ge(qk_ready, 2 * j + 1)
                        act.activation(QT[:, NB * j:NB * j + n], ps[:, 2 + j % 2, 0:n], ACT.Copy).then_inc(q_out, 1)
                        act.wait_ge(qk_ready, 2 * j + 2)
                        for h in (0, 1):
                            act.activation(KM[:, h, NB * j:NB * j + n], ps[:, 4 + j % 2, 0:n], ACT.Copy,
                                           scale=w("headmask")[:, h:h + 1]).then_inc(k_out, 1)

                    deviations(0)
                    deviations(1)
                    act.wait_ge(loaded_a, 16)
                    for j in range(5):
                        xt_of(j)
                        if j + 2 < len(GROUPS):
                            deviations(j + 2)
                        if j:
                            qk_of(j - 1)
                    qk_of(4)
                    for j in (0, 2, 4):
                        act.wait_ge(v_ready, j + 1)
                        m = min(4, T0 + 1 - 4 * j)
                        act.activation(V[:, 4 * j:4 * j + m, :],
                                       ps[:, 6 + j % 2, 0:m * P].rearrange("p (t d) -> p t d", d=P),
                                       ACT.Copy).then_inc(v_out, 1)
                    act.wait_ge(v_out, 3)

                @block.tensor
                def _(pe):
                    pe.wait_ge(loaded_a, 16)
                    pe.wait_ge(mem_in, 32)

                    def turn(j):
                        if j >= 2:
                            pe.wait_ge(xt_ready, j - 1)
                        for t in range(4 * j, min(4 * j + 4, T0)):
                            pe.wait_ge(xn_ready, t + 1)
                            ins = pe.transpose(ps[:, j % 2, P * (t % 4):P * (t % 4 + 1)], XN[:, t, :], ident)
                        ins.then_inc(turned, 1)

                    def qk_of(j):
                        n = NB if j < 4 else PADC - 4 * NB
                        pe.wait_ge(xt_ready, j + 1)
                        if j >= 2:
                            pe.wait_ge(q_out, j - 1)
                            pe.wait_ge(k_out, 2 * (j - 1))
                            pe.wait_ge(k_out_dve, 2 * (j - 1))
                        pe.matmul(ps[:, 2 + j % 2, 0:n], w("wqT"), XT[:, NB * j:NB * j + n], start=True, stop=True).then_inc(qk_ready, 1)
                        pe.matmul(ps[:, 4 + j % 2, 0:n], w("wkT"), XT[:, NB * j:NB * j + n], start=True, stop=True).then_inc(qk_ready, 1)

                    turn(0)
                    pe.wait_ge(x_padded, 2)
                    for j in range(5):
                        if j + 1 < 5:
                            turn(j + 1)
                        qk_of(j)
                    for t in range(T0 + 1):
                        j = t // 4
                        if t % 4 == 0 and j >= 2:
                            pe.wait_ge(v_out if j % 2 == 0 else v_out_dve, j // 2)
                        ins = pe.matmul(ps[:, 6 + j % 2, P * (t % 4):P * (t % 4 + 1)], XT[:, P * t:P * (t + 1)], w("wvT"),
                                        start=True, stop=True)
                        if t % 4 == 3 or t == T0:
                            ins.then_inc(v_ready, 1)

            Pm = sbi("Pm", [P, NH0, KW])
            PTA, PTB = sbi("PTA", [P, NH0, P]), sbi("PTB", [WIN, NH0, P])
            nmax, rowsum, rinv = sbi("nmax", [P, 2, NH0]), sbi("rowsum", [P, NH0]), sbi("rinv", [P, NH0])
            nbias = sbi("nbias", [P, NH0])
            rwide = sbi("rwide", [P, NH0, DH0])
            Osb = sbi("Osb", [P, P])
            Th, H2, U, W2 = sbi("Th", [P, HID]), sbi("H2", [P, 2, HID]), sbi("U", [P, HID]), sbi("W2", [P, HID])
            dz = sbi("dz", [P, HID])
            hT, err, errT = sbi("hT", [P, HC, P]), sbi("err", [P, D]), sbi("errT", [P, P])
            names = ("s_ready nmax_ready nbias_ready p_ready rwide_ready pt_ready pta_out ptb_out o_ready osb_ready ot_ready "
                     "z_ready th_ready h_ready ht_ready ht_out err_psum err_ready errt_psum errt_ready dh_ready "
                     "dz_ready g1_done g2_done sums_done u_done w_done sum_e").split()
            q = {n: sem("l0_" + n) for n in names}
            SB = (0, 1)
            OB, ZB, HB, EB = 2, 3, 4, 5

            with nc.Block() as block:
                @block.tensor
                def _(pe):
                    pe.wait_ge(cast, 4)
                    for s in range(T0 + 2):
                        t, g, l = s, s - 1, s - 2
                        if t < T0:
                            m = 1 if t == 0 else 2 if t == 8 else 0
                            if t:
                                pe.wait_ge(q["pta_out"], t)
                                pe.wait_ge(q["ptb_out"], t)
                            for k in range(2):
                                dst = ps[:, SB[k], 0:2 * KW]
                                pe.matmul(dst, QT[:, NPM + P * t:NPM + P * (t + 1)],
                                          KM[:, 2 * k:2 * k + 2, P * t:P * t + KW], start=True, stop=False)
                                ins = pe.matmul(dst, idb[:, :], masks[:, m, :, :], start=False, stop=True)
                            ins.then_inc(q["s_ready"], 1)
                        if 0 <= g < T0:
                            if g:
                                pe.wait_ge(q["dz_ready"], g)
                            xt = XT[:, NPM + P * g:NPM + P * (g + 1)]
                            pe.matmul(ps[:, ZB, :], xt, w("w1T"), start=True, stop=False)
                            pe.matmul(ps[:, ZB, :], ones_b[:, :], b1s[:, :], start=False, stop=True).then_inc(q["z_ready"], 1)
                        if 0 <= l < T0:
                            pe.matmul(G2, err[:, :], H2[:, l % 2, :], start=(l == 0), stop=(l == T0 - 1)).then_inc(q["g2_done"], 1)
                            pe.wait_ge(q["dz_ready"], l + 1)
                            pe.matmul(G1, XN[:, l, :], dz[:, :], start=(l == 0), stop=(l == T0 - 1)).then_inc(q["g1_done"], 1)
                        if 0 <= g < T0:
                            pe.wait_ge(q["h_ready"], g + 1)
                            if g:
                                pe.wait_ge(q["ht_out"], g)
                            for k in range(HC):
                                ins = pe.transpose(ps[:, HB, P * k:P * (k + 1)], H2[:, g % 2, P * k:P * (k + 1)], ident)
                            ins.then_inc(q["ht_ready"], 1)
                        if t < T0:
                            for h in range(NH0):
                                pe.wait_ge(q["p_ready"], NH0 * t + max(h + 1, 2))
                                pe.transpose(ps[:, SB[0], P * h:P * (h + 1)], Pm[:, h, 0:P], ident)
                            for h in range(NH0):
                                pe.transpose(ps[0:WIN, SB[1], P * h:P * (h + 1)], Pm[:, h, P:KW], ident).then_inc(q["pt_ready"], 1)
                        if 0 <= g < T0:
                            pe.wait_ge(q["ht_out"], g + 1)
                            pe.wait_ge(q["ot_ready"], g + 1)
                            if g:
                                pe.wait_ge(q["errt_ready"], g)
                            for k in range(HC):
                                pe.matmul(ps[:, EB, 0:D], hT[:, k, :], w("w2T")[:, P * k:P * (k + 1)], start=(k == 0), stop=False)
                            pe.matmul(ps[:, EB, 0:D], OT[:, P * g:P * (g + 1)], nwoT[:, :], start=False, stop=True).then_inc(q["err_psum"], 1)
                        if t < T0:
                            pe.wait_ge(q["rwide_ready"], t + 1)
                            if t:
                                pe.wait_ge(q["ot_ready"], t)
                            pe.matmul(ps[:, OB, P:2 * P], rwide[:, :, :].rearrange("p h d -> p (h d)"), ident,
                                      start=True, stop=True)
                            pe.wait_ge(q["pta_out"], t + 1)
                            pe.wait_ge(q["ptb_out"], t + 1)
                            for h in range(NH0):
                                hs = slice(DH0 * h, DH0 * (h + 1))
                                pe.matmul(ps[hs, OB, 0:P], V[:, t, hs], PTA[:, h, :], start=True, stop=False)
                        if 0 <= g < T0:
                            pe.wait_ge(q["err_ready"], g + 1)
                            pe.transpose(ps[:, EB, P:2 * P], err[:, :], ident).then_inc(q["errt_psum"], 1)
                        if t < T0:
                            for h in range(NH0):
                                hs = slice(DH0 * h, DH0 * (h + 1))
                                ins = pe.matmul(ps[hs, OB, 0:P], V[0:WIN, t + 1, hs], PTB[:, h, :], start=False, stop=True,
                                                tile_position=(0, DH0 * h))
                            ins.then_inc(q["o_ready"], 1)
                        if 0 <= g < T0:
                            pe.wait_ge(q["errt_ready"], g + 1)
                            pe.wait_ge(q["h_ready"], g + 1)
                            pe.matmul(ps[:, ZB, :], errT[:, :], w("w2"), start=True, stop=True).then_inc(q["dh_ready"], 1)

                @block.scalar
                def _(act):
                    for s in range(T0 + 1):
                        t, g = s, s - 1
                        if 0 <= g < T0:
                            act.wait_ge(q["z_ready"], g + 1)
                            if g:
                                act.wait_ge(q["w_done"], g)
                            act.activation(Th[:, :], ps[:, ZB, :], ACT.Tanh, scale=0.5).then_inc(q["th_ready"], 1)
                        if t < T0:
                            act.wait_ge(q["nbias_ready"], t + 1)
                            if t:
                                act.wait_ge(q["pt_ready"], NH0 * t)
                                act.wait_ge(q["rwide_ready"], t)
                            for h in range(NH0):
                                act.activation(Pm[:, h, :], ps[:, SB[h // 2], KW * (h % 2):KW * (h % 2 + 1)], ACT.Exp,
                                               bias=nbias[:, h:h + 1], scale=SCALE,
                                               accum_out=rowsum[:, h:h + 1]).then_inc(q["p_ready"], 1)
                        if 0 <= g < T0:
                            act.wait_ge(q["ht_ready"], g + 1)
                            if g:
                                act.wait_ge(q["err_psum"], g)
                            act.activation(hT[:, :, :], ps[:, HB, :].rearrange("p (k n) -> p k n", k=HC), ACT.Copy,
                                           scale=0.5).then_inc(q["ht_out"], 1)
                        if t < T0:
                            act.wait_ge(q["pt_ready"], NH0 * (t + 1))
                            if t:
                                act.wait_ge(q["o_ready"], t)
                            act.activation(PTB[:, :, :], ps[0:WIN, SB[1], :].rearrange("p (k n) -> p k n", k=NH0),
                                           ACT.Copy).then_inc(q["ptb_out"], 1)
                        if 0 <= g < T0:
                            act.wait_ge(q["errt_psum"], g + 1)
                            if g:
                                act.wait_ge(q["dh_ready"], g)
                            act.activation(errT[:, :], ps[:, EB, P:2 * P], ACT.Copy).then_inc(q["errt_ready"], 1)
                        if t < T0:
                            act.wait_ge(q["o_ready"], t + 1)
                            if t:
                                act.wait_ge(q["ot_ready"], t)
                            act.activation(Osb[:, :], ps[:, OB, 0:P], ACT.Copy).then_inc(q["osb_ready"], 1)

                @block.vector
                def _(dve):
                    dve.wait_ge(x_in_ready, 16)
                    for s in range(T0 + 1):
                        t, g = s, s - 1
                        if t < T0:
                            dve.wait_ge(q["s_ready"], t + 1)
                            if t:
                                dve.wait_ge(q["nbias_ready"], t)
                                dve.wait_ge(q["p_ready"], NH0 * t)
                            for k in range(2):
                                dve.tensor_reduce(nmax[:, t % 2, 2 * k:2 * k + 2], ps[:, SB[k], 0:2 * KW].rearrange("p (h k) -> p h k", h=2),
                                                  AX.X, ALU.max, negate=True).then_inc(q["nmax_ready"], 1)
                            dve.wait_ge(q["nmax_ready"], 2 * (t + 1))
                            dve.tensor_scalar(nbias[:, :], nmax[:, t % 2, :], SCALE, None, ALU.mult).then_inc(q["nbias_ready"], 1)
                        if 0 <= g < T0:
                            dve.wait_ge(q["th_ready"], g + 1)
                            if g:
                                dve.wait_ge(q["ht_ready"], g)
                            if g >= 2:
                                dve.wait_ge(q["g2_done"], g - 1)
                            dve.scalar_tensor_tensor(out=H2[:, g % 2, :], in0=Th[:, :], scalar=1.0, in1=ps[:, ZB, :],
                                                     op0=ALU.add, op1=ALU.mult).then_inc(q["h_ready"], 1)
                            dve.wait_ge(q["h_ready"], g + 1)
                            dve.scalar_tensor_tensor(out=U[:, :], in0=Th[:, :], scalar=1.0, in1=H2[:, g % 2, :],
                                                     op0=ALU.subtract, op1=ALU.mult).then_inc(q["u_done"], 1)
                        if t < T0:
                            dve.wait_ge(q["p_ready"], NH0 * (t + 1))
                            dve.reciprocal(rinv[:, :], rowsum[:, :]).then_inc(q["sum_e"], 1)
                            dve.wait_ge(q["sum_e"], t + 1)
                            if t:
                                dve.wait_ge(q["o_ready"], t)
                            dve.tensor_copy(rwide[:, :, :], rinv[:, :].unsqueeze(2).to_broadcast([P, NH0, DH0])).then_inc(q["rwide_ready"], 1)
                            dve.wait_ge(q["pt_ready"], NH0 * (t + 1))
                            dve.tensor_copy(PTA[:, :, :], ps[:, SB[0], :].rearrange("p (k n) -> p k n", k=NH0)).then_inc(q["pta_out"], 1)
                        if 0 <= g < T0:
                            dve.wait_ge(q["err_psum"], g + 1)
                            if g:
                                dve.wait_ge(q["g2_done"], g)
                                dve.wait_ge(q["sums_done"], 2 * g)
                            dve.tensor_tensor(err[:, :], ps[:, EB, 0:D], w("b2row"), ALU.add).then_inc(q["err_ready"], 1)
                            dve.wait_ge(q["u_done"], g + 1)
                            if g:
                                dve.wait_ge(q["dz_ready"], g)
                            dve.scalar_tensor_tensor(out=W2[:, :], in0=Th[:, :], scalar=2.0, in1=U[:, :],
                                                     op0=ALU.mult, op1=ALU.subtract).then_inc(q["w_done"], 1)
                        if t < T0:
                            dve.wait_ge(q["osb_ready"], t + 1)
                            dve.tensor_tensor(OT[:, P * t:P * (t + 1)], Osb[:, :], ps[:, OB, P:2 * P], ALU.mult).then_inc(q["ot_ready"], 1)
                        if 0 <= g < T0:
                            dve.wait_ge(q["dh_ready"], g + 1)
                            dve.wait_ge(q["w_done"], g + 1)
                            if g:
                                dve.wait_ge(q["g1_done"], g)
                                dve.wait_ge(q["sums_done"], 2 * g)
                            dve.scalar_tensor_tensor(out=dz[:, :], in0=W2[:, :], scalar=2.0, in1=ps[:, ZB, :],
                                                     op0=ALU.add, op1=ALU.mult).then_inc(q["dz_ready"], 1)

                @block.gpsimd
                def _(pool):
                    for g in range(T0):
                        if g:
                            pool.wait_ge(q["sums_done"], 2 * g)
                        pool.wait_ge(q["err_ready"], g + 1)
                        pool.tensor_tensor(errsum[:, :], errsum[:, :], err[:, :], ALU.add).then_inc(q["sums_done"], 1)
                        pool.wait_ge(q["dz_ready"], g + 1)
                        pool.tensor_tensor(dzsum[:, :], dzsum[:, :], dz[:, :], ALU.add).then_inc(q["sums_done"], 1)

        updated_mlp(nc, sem, w, ident, ps, XT, OT, dzsum, errsum, G1, G2, Y, n0, loaded_b)


def updated_mlp(nc, sem, w, ident, ps, XT, OT, dzsum, errsum, G1, G2, Y, n0, loaded_b):
    y_stat = n0.y_stat
    with ExitStack() as c:
        def sb(name, shape, dt=F32):
            return c.enter_context(nc.sbuf_tensor("um_" + name, shape, dt))

        keep, nth = sb("keep", [P, 1]), sb("nth", [P, 3])
        w1n, w2n = sb("w1n", [P, HID]), sb("w2n", [P, HID])
        w1k, w2k = sb("w1k", [P, HID]), sb("w2k", [P, HID])
        g2s = sb("g2s", [P, HID])
        b1k, b1n, b2k, b2n = sb("b1k", [P, HC]), sb("b1n", [P, HC]), sb("b2k", [P, 1]), sb("b2n", [P, 1])
        hT = sb("hT", [P, HC, NB])
        swaT, memT = sb("swaT", [P, NB]), sb("memT", [P, NB])
        t1, t2 = sb("t1", [P, NB]), sb("t2", [P, NB])
        a1, a2, mg = sb("a1", [P, NB]), sb("a2", [P, NB]), sb("mg", [P, NB])
        dve_done, bsum_ready, g2t_ready, g2s_ready, new_ready = (sem("um_dve_done"), sem("um_bsum_ready"),
                                                                 sem("um_g2t_ready"), sem("um_g2s_ready"), sem("um_new_ready"))
        z_ready, h_ready, swa_psum, swa_ready, mem_psum, mem_ready = (sem("um_z_ready"), sem("um_h_ready"), sem("um_swa_psum"),
                                                                      sem("um_swa_ready"), sem("um_mem_psum"), sem("um_mem_ready"))
        g_psum, tanh_ready, mg_ready, turned, y_ready = (sem("um_g_psum"), sem("um_tanh_ready"), sem("um_mg_ready"),
                                                         sem("um_turned"), sem("um_y_ready"))
        a_done = sem("um_a_done")
        NJ = TOK // NB
        cols = [SM * (j // 2) + NPM + NB * (j % 2) for j in range(NJ)]

        with nc.Block() as block:
            @block.vector
            def _(dve):
                chain = Count(dve_done)
                chain.add(dve.tensor_scalar(keep[:, :], w("alpha"), -1.0, 1.0, ALU.mult, ALU.add))
                for n in range(3):
                    chain.add(dve.tensor_scalar(nth[:, n:n + 1], w("theta"), -0.5 ** n, None, ALU.mult))
                dve.tensor_copy(g2s[:, :], G2).then_inc(g2s_ready, 1)
                dve.wait_ge(dve_done, chain.n)
                chain.add(dve.tensor_scalar(w1k[:, :], w("w1T"), keep[:, :], None, ALU.mult))
                chain.add(dve.tensor_scalar(w2k[:, :], w("w2T"), keep[:, :], None, ALU.mult))
                chain.add(dve.tensor_scalar(b1k[:, :], w("b1col"), keep[:, :], None, ALU.mult))
                chain.add(dve.tensor_scalar(b2k[:, :], w("b2col"), keep[:, :], None, ALU.mult))
                dve.wait_ge(dve_done, chain.n)
                dve.scalar_tensor_tensor(out=w1n[:, :], in0=G1, scalar=nth[:, 2:3], in1=w1k[:, :],
                                         op0=ALU.mult, op1=ALU.add).then_inc(new_ready, 1)
                dve.wait_ge(bsum_ready, 1)
                dve.scalar_tensor_tensor(out=b1n[:, :], in0=ps[:, 0, 0:HC], scalar=nth[:, 2:3], in1=b1k[:, :],
                                         op0=ALU.mult, op1=ALU.add).then_inc(new_ready, 1)
                dve.scalar_tensor_tensor(out=b2n[:, :], in0=ps[:, 0, HC:HC + 1], scalar=nth[:, 0:1], in1=b2k[:, :],
                                         op0=ALU.mult, op1=ALU.add).then_inc(new_ready, 1)
                dve.wait_ge(g2t_ready, 1)
                dve.scalar_tensor_tensor(out=w2n[:, :], in0=ps[:, 1, :], scalar=nth[:, 1:2], in1=w2k[:, :],
                                         op0=ALU.mult, op1=ALU.add).then_inc(new_ready, 1)
                for j in range(NJ):
                    dve.wait_ge(swa_psum, j + 1)
                    if j:
                        dve.wait_ge(mg_ready, j)
                        dve.wait_ge(g_psum, 2 * j)
                    dve.tensor_copy(swaT[:, :], ps[:, 5, :]).then_inc(swa_ready, 1)
                    dve.wait_ge(swa_ready, j + 1)
                    dve.wait_ge(tanh_ready, 2 * j + 1)
                    dve.scalar_tensor_tensor(out=a1[:, :], in0=t1[:, :], scalar=1.0, in1=swaT[:, :],
                                             op0=ALU.add, op1=ALU.mult).then_inc(a_done, 1)
                    dve.wait_ge(tanh_ready, 2 * j + 2)
                    dve.wait_ge(mem_ready, j + 1)
                    dve.scalar_tensor_tensor(out=a2[:, :], in0=t2[:, :], scalar=1.0, in1=memT[:, :],
                                             op0=ALU.add, op1=ALU.mult).then_inc(a_done, 1)
                    dve.wait_ge(a_done, 2 * j + 2)
                    if j:
                        dve.wait_ge(turned, j)
                    dve.tensor_tensor(mg[:, :], a1[:, :], a2[:, :], ALU.add).then_inc(mg_ready, 1)
                    if j:
                        dve.wait_ge(y_ready, j)
                        y_stat.block(dve, Y, j - 1)
                for j in range(NJ - 1):
                    n0.factors_y(dve, j)
                n0.sum_x(dve, 0)
                dve.wait_ge(y_ready, NJ)
                y_stat.block(dve, Y, NJ - 1)
                n0.factors_x(dve, 0)
                n0.factors_y(dve, NJ - 1)
                n0.at_least(dve, "factors", 2 * NJ)
                n0.at_least(dve, "factors2", 2)

            @block.tensor
            def _(pe):
                pe.wait_ge(loaded_b, 16)
                for k in range(HC):
                    pe.matmul(ps[:, 0, k:k + 1], dzsum[:, P * k:P * (k + 1)], w("ones"), start=True, stop=True)
                pe.matmul(ps[:, 0, HC:HC + 1], errsum[:, :], w("ones"), start=True, stop=True).then_inc(bsum_ready, 1)
                pe.wait_ge(g2s_ready, 1)
                for k in range(HC):
                    ins = pe.transpose(ps[:, 1, P * k:P * (k + 1)], g2s[:, P * k:P * (k + 1)], ident)
                ins.then_inc(g2t_ready, 1)

                def z_of(j):
                    for k in range(HC):
                        if j:
                            pe.wait_ge(h_ready, HC * (j - 1) + k + 1)
                        pe.matmul(ps[:, k, :], w1n[:, P * k:P * (k + 1)], XT[:, NPM + cols[j]:NPM + cols[j] + NB],
                                  start=True, stop=True).then_inc(z_ready, 1)

                def swa_of(j):
                    if j:
                        pe.wait_ge(swa_ready, j)
                    pe.matmul(ps[:, 5, :], w("woT"), OT[:, cols[j]:cols[j] + NB], start=True, stop=True).then_inc(swa_psum, 1)

                pe.wait_ge(new_ready, 4)
                z_of(0)
                swa_of(0)
                for j in range(NJ):
                    if j:
                        pe.wait_ge(mem_ready, j)
                    for k in range(HC):
                        pe.wait_ge(h_ready, HC * j + k + 1)
                        ins = pe.matmul(ps[:, 4, :], w2n[:, P * k:P * (k + 1)], hT[:, k, :], start=(k == 0), stop=(k == HC - 1))
                    ins.then_inc(mem_psum, 1)
                    pe.wait_ge(swa_ready, j + 1)
                    if j:
                        pe.wait_ge(y_ready, j)
                    pe.matmul(ps[:, 6, :], w("lin1T"), swaT[:, :], start=True, stop=True).then_inc(g_psum, 1)
                    pe.wait_ge(mem_ready, j + 1)
                    if j:
                        pe.wait_ge(tanh_ready, 2 * j)
                    pe.matmul(ps[:, 7, :], w("lin2T"), memT[:, :], start=True, stop=True).then_inc(g_psum, 1)
                    if j + 1 < NJ:
                        z_of(j + 1)
                    pe.wait_ge(mg_ready, j + 1)
                    pe.wait_ge(tanh_ready, 2 * j + 1)
                    for n in range(4):
                        ins = pe.transpose(ps[:, 6, P * n:P * (n + 1)], mg[:, P * n:P * (n + 1)], ident)
                    ins.then_inc(turned, 1)
                    if j + 1 < NJ:
                        swa_of(j + 1)

            @block.scalar
            def _(act):
                def y_of(j):
                    act.wait_ge(turned, j + 1)
                    act.activation(Y[:, 4 * j:4 * j + 4, :], ps[:, 6, :].rearrange("p (t d) -> p t d", d=D), ACT.Copy,
                                   scale=0.5).then_inc(y_ready, 1)

                act.wait_ge(new_ready, 4)
                for j in range(NJ):
                    for k in range(HC):
                        act.wait_ge(z_ready, HC * j + k + 1)
                        if j and k == 0:
                            act.wait_ge(mem_psum, j)
                        act.activation(hT[:, k, :], ps[:, k, :], ACT.Silu, bias=b1n[:, k:k + 1]).then_inc(h_ready, 1)
                    if j:
                        y_of(j - 1)
                    act.wait_ge(mem_psum, j + 1)
                    if j:
                        act.wait_ge(a_done, 2 * j)
                        act.wait_ge(g_psum, 2 * j)
                    act.activation(memT[:, :], ps[:, 4, :], ACT.Identity, bias=b2n[:, :]).then_inc(mem_ready, 1)
                    act.wait_ge(g_psum, 2 * j + 1)
                    act.activation(t1[:, :], ps[:, 6, :], ACT.Tanh, scale=0.5).then_inc(tanh_ready, 1)
                    act.wait_ge(g_psum, 2 * j + 2)
                    act.activation(t2[:, :], ps[:, 7, :], ACT.Tanh, scale=0.5).then_inc(tanh_ready, 1)
                for j in range(NJ - 1):
                    n0.deviation_y(act, j)
                y_of(NJ - 1)
                n0.deviation_x(act, 0)
                n0.deviation_y(act, NJ - 1)
                act.wait_ge(y_ready, NJ)


def wait(eng, sem, value):
    if isinstance(value, int) and value <= 0:
        return
    eng.wait_ge(sem, value)


def experts(nc, sem, w, ident, ps, XNT, Y, n0, n1, y_stat, loaded_b, WC, packC, loaded_c):
    with ExitStack() as c:
        def sb(name, shape, dt=F32):
            return c.enter_context(nc.sbuf_tensor("ex_" + name, shape, dt))

        comb_ready, lt_ready, lt_out = sem("ex_comb_ready"), sem("ex_lt_ready"), sem("ex_lt_out")
        LT = sb("LT", [E, TOK])
        L, M8, I8 = sb("L", [P, TT, E]), sb("M8", [P, TT, 8]), sb("I8", [P, TT, 8], U32)
        IF = sb("IF", [P, TT, 2])
        dd, ee, dn, w1, w2 = (sb(n, [P, TT, 1]) for n in ("dd", "ee", "dn", "w1", "w2"))
        c1, c2, C1, C2, COMB = (sb(n, [P, TT, E]) for n in ("c1", "c2", "C1", "C2", "COMB"))
        dve_done, logits_ready, d_ready, e_ready = sem("ex_dve_done"), sem("ex_logits_ready"), sem("ex_d_ready"), sem("ex_e_ready")

        NJ, NC = TOK // NB, E * I // P
        combT = sb("combT", [P, P])
        CB = sb("CB", [P, E, NB])
        comb = nc.dram_tensor("comb", [NJ, E, 4, P], F32, kind="Internal").ap()
        sg, cw, h = sb("sg", [P, 2, NB]), sb("cw", [P, 2, NB]), sb("h", [P, 2, NB])
        yT = sb("yT", [P, NB])
        ct_psum, ct_out, comb_out, cb_ready, gu_ready, silu_ready, cw_ready, mixed, h_ready, down_done, yt_out, turned, y_out = (
            sem("ex_" + n) for n in ("ct_psum ct_out comb_out cb_ready gu_ready silu_ready cw_ready mixed h_ready down_done yt_out "
                                     "turned y_out").split())
        GB, UB, YB, TB = 0, 2, 6, 7
        wg, wu, wd = w("WgT"), w("WuT"), w("WdT")
        MIXED = [I * e // P for e in range(1, E) if I * e % P]

        def owners(ch):
            if ch not in MIXED:
                return P * ch // I, None
            low = P * ch // I
            cut = I * (low + 1) - P * ch
            return (low, (low + 1, cut, P)) if cut >= P // 2 else (low + 1, (low, 0, cut))

        def last_chunk(e):
            return (I * (e + 1) - 1) // P

        def mixed_count(i, ch):
            return len(MIXED) * i + sum(m <= ch for m in MIXED)

        def u_reader(i, ch):
            return NC * i + (ch - 4 if ch >= 4 else ch - 2 if ch < 2 else ch - 4) + 1

        with nc.Block() as block:
            @block.tensor
            def _(pe):
                def logits(j):
                    n0.at_least(pe, "evac", j + 1)
                    wait(pe, lt_out, j)
                    pe.matmul(ps[0:E, TB, :], w("routerT"), XNT[:, NB * j:NB * (j + 1)], start=True, stop=True).then_inc(lt_ready, 1)

                def turn_logits(j):
                    pe.wait_ge(lt_out, j + 1)
                    for t in range(4 * j, 4 * j + 4):
                        ins = pe.transpose(ps[:, YB, E * t:E * (t + 1)], LT[:, P * t:P * (t + 1)], ident[0:E, 0:E])
                    if j == NJT - 1:
                        ins.then_inc(logits_ready, 1)

                pe.wait_ge(loaded_b, 16)
                for j in range(NJT):
                    n0.turn(pe, j)
                    if j:
                        logits(j - 1)
                    if j > 1:
                        turn_logits(j - 2)
                turn_logits(NJT - 2)
                logits(NJT - 1)
                turn_logits(NJT - 1)

                def gate_up(i, ch):
                    n = NC * i + ch
                    x = XNT[:, bass.ds(NB * i, NB)]
                    wait(pe, silu_ready, n - 1)
                    wait(pe, h_ready, u_reader(i, ch))
                    pe.matmul(ps[:, GB + ch % 2, :], wg[:, P * ch:P * (ch + 1)], x, start=True, stop=True)
                    pe.matmul(ps[:, UB + ch % 4, :], wu[:, P * ch:P * (ch + 1)], x, start=True, stop=True).then_inc(gu_ready, 1)

                def down(i, ch):
                    wait(pe, h_ready, NC * i + ch + 1)
                    if ch == 0:
                        wait(pe, yt_out, i)
                    pe.matmul(ps[:, YB, :], wd[:, D * ch:D * (ch + 1)], h[:, ch % 2, :], start=(ch == 0),
                              stop=(ch == NC - 1)).then_inc(down_done, 1)

                def turn(i):
                    wait(pe, yt_out, i + 1)
                    if isinstance(i, int) and i == 0:
                        pe.wait_ge(ct_out, 1)
                    wait(pe, y_out, i)
                    for n in range(4):
                        ins = pe.transpose(ps[:, TB, P * n:P * (n + 1)], yT[:, P * n:P * (n + 1)], ident)
                    ins.then_inc(turned, 1)

                def body(i, first):
                    for ch in range(NC):
                        gate_up(i, ch)
                        if ch == 1 and first:
                            pe.wait_ge(comb_ready, 1)
                            pe.transpose(ps[:, TB, 0:P], COMB[:, :, :].rearrange("p t e -> p (t e)"), ident).then_inc(ct_psum, 1)
                        if ch >= 2:
                            down(i, ch - 2)
                        elif not first:
                            down(i - 1, NC + ch - 2)
                        if ch == 3 and not first:
                            turn(i - 1)

                body(0, True)
                with pe.Fori(1, NJ - 1) as i:
                    body(i, False)
                body(NJ - 1, False)
                for ch in (NC - 2, NC - 1):
                    down(NJ - 1, ch)
                turn(NJ - 1)

            @block.scalar
            def _(act):
                def logits_out(j):
                    act.wait_ge(lt_ready, j + 1)
                    act.activation(LT[:, NB * j:NB * (j + 1)], ps[0:E, TB, :], ACT.Copy).then_inc(lt_out, 1)

                n0.scalar(act, XNT, lambda j: logits_out(j - 1) if j else None, begun=True)
                logits_out(NJT - 1)
                act.wait_ge(d_ready, 1)
                act.activation(ee[:, :, :], dd[:, :, :], ACT.Exp).then_inc(e_ready, 1)
                act.wait_ge(ct_psum, 1)
                act.activation(combT[:, :], ps[:, TB, 0:P], ACT.Copy).then_inc(ct_out, 1)

                def sum_out(i):
                    wait(act, down_done, NC * (i + 1))
                    wait(act, turned, i)
                    act.activation(yT[:, :], ps[:, YB, :], ACT.Copy).then_inc(yt_out, 1)

                def y_of(i):
                    wait(act, turned, i + 1)
                    act.activation(Y[:, bass.ds(4 * i, 4), :], ps[:, TB, :].rearrange("p (t d) -> p t d", d=D),
                                   ACT.Copy).then_inc(y_out, 1)

                def body(i, first, last):
                    for ch in range(NC):
                        n = NC * i + ch
                        wait(act, gu_ready, n + 1)
                        wait(act, h_ready, n - 1)
                        act.activation(sg[:, ch % 2, :], ps[:, GB + ch % 2, :], ACT.Silu).then_inc(silu_ready, 1)
                        if ch == 2 and not first:
                            sum_out(i - 1)
                        if ch == 4 and not first:
                            y_of(i - 1)
                        if last and ch == 8:
                            for j in range(NJ - 1):
                                n1.deviation_y(act, j)
                        if last and ch == 18:
                            for j in range(NJ - 1):
                                n1.deviation_x(act, j)
                        if last and ch == NC - 1:
                            n1.at_least(act, "factors2", 2)
                            n1.scaled(act, 0, n1.XN, n1.XP, n1.rstd2, n1.shift2, "xn_scalar")

                body(0, True, False)
                with act.Fori(1, NJ - 1) as i:
                    body(i, False, False)
                body(NJ - 1, False, True)
                sum_out(NJ - 1)
                y_of(NJ - 1)

            @block.gpsimd
            def _(pool):
                n0.gpsimd(pool)

                def body(i):
                    for ch in range(NC):
                        n = NC * i + ch
                        e, _ = owners(ch)
                        wait(pool, silu_ready, n + 1)
                        wait(pool, cb_ready, 16 * (E * i + e + 1))
                        wait(pool, h_ready, n - 1)
                        pool.tensor_tensor(cw[:, ch % 2, :], sg[:, ch % 2, :], CB[:, e, :], ALU.mult).then_inc(cw_ready, 1)

                body(0)
                with pool.Fori(1, NJ) as i:
                    body(i)

            @block.vector
            def _(dve):
                n0.vector(dve, begun=True)
                chain = Count(dve_done)

                def then(ins):
                    dve.wait_ge(dve_done, chain.add(ins))

                dve.wait_ge(logits_ready, 1)
                then(dve.tensor_copy(L[:, :, :], ps[:, YB, 0:TT * E].rearrange("p (t e) -> p t e", e=E)))
                for t in range(TT):
                    n = chain.add(dve.max(M8[:, t, :], L[:, t, :]))
                dve.wait_ge(dve_done, n)
                for t in range(TT):
                    n = chain.add(dve.max_index(I8[:, t, :], M8[:, t, :], L[:, t, :]))
                then(dve.tensor_tensor(dd[:, :, :], M8[:, :, 1:2], M8[:, :, 0:1], ALU.subtract))
                dve.nop().then_inc(d_ready, 1)
                dve.wait_ge(e_ready, 1)
                then(dve.tensor_scalar(dn[:, :, :], ee[:, :, :], 1.0, None, ALU.add))
                then(dve.reciprocal(w1[:, :, :], dn[:, :, :]))
                then(dve.tensor_tensor(w2[:, :, :], ee[:, :, :], w1[:, :, :], ALU.mult))
                then(dve.tensor_copy(IF[:, :, :], I8[:, :, 0:2]))
                no = w("expert_no").unsqueeze(1).to_broadcast([P, TT, E])
                for k, (cc, CC, ww) in enumerate(((c1, C1, w1), (c2, C2, w2))):
                    then(dve.tensor_tensor(cc[:, :, :], IF[:, :, k:k + 1].to_broadcast([P, TT, E]), no, ALU.is_equal))
                    then(dve.tensor_tensor(CC[:, :, :], cc[:, :, :], ww[:, :, :].to_broadcast([P, TT, E]), ALU.mult))
                then(dve.tensor_tensor(COMB[:, :, :], C1[:, :, :], C2[:, :, :], ALU.add))
                dve.nop().then_inc(comb_ready, 1)

                def body(i, first, last):
                    for ch in range(NC):
                        n = NC * i + ch
                        _, rest = owners(ch)
                        wait(dve, cw_ready, n + 1)
                        if rest:
                            e, a, b = rest
                            wait(dve, silu_ready, n + 1)
                            wait(dve, cb_ready, 16 * (E * i + e + 1))
                            dve.tensor_tensor(cw[a:b, ch % 2, :], sg[a:b, ch % 2, :], CB[a:b, e, :], ALU.mult).then_inc(mixed, 1)
                            wait(dve, mixed, mixed_count(i, ch))
                        wait(dve, gu_ready, n + 1)
                        wait(dve, down_done, n - 1)
                        dve.tensor_tensor(h[:, ch % 2, :], cw[:, ch % 2, :], ps[:, UB + ch % 4, :], ALU.mult).then_inc(h_ready, 1)
                        if ch == 7 and not first:
                            wait(dve, y_out, i)
                            y_stat.sums(dve, Y, i - 1)
                            if last:
                                for j in range(NJ - 1):
                                    y_stat.results(dve, j)
                        if last and ch == 10:
                            for j in range(NJ - 1):
                                n1.factors_y(dve, j)
                        if last and 11 <= ch < 11 + 2 * (NJ - 1):
                            n1.sum_tile(dve, 2 * (ch - 11))
                            n1.sum_tile(dve, 2 * (ch - 11) + 1)
                        if last and ch == 17:
                            for j in range(NJ - 1):
                                n1.own.results(dve, j)
                        if last and ch == 19:
                            for j in range(NJ - 1):
                                n1.factors_x(dve, j)

                body(0, True, False)
                with dve.Fori(1, NJ - 1) as i:
                    body(i, False, False)
                body(NJ - 1, False, True)
                n1.xn_by_vector(dve, 1)
                n1.xn_by_vector(dve, 2)
                dve.wait_ge(y_out, NJ)
                y_stat.block(dve, Y, NJ - 1)
                y_stat.wait_all(dve)

            @block.sync
            def _(sp):
                sp.dma_start(WC[:, :], packC).then_inc(loaded_c, 16)
                sp.wait_ge(ct_out, 1)

                def comb_of(j):
                    sp.dma_start(comb[j, :, :, :].rearrange("e t p -> t e p"), combT[4 * E * j:4 * E * (j + 1), :]).then_inc(comb_out, 16)

                comb_of(0)
                sp.wait_ge(comb_out, 16)

                def body(i):
                    for e in range(E):
                        wait(sp, cb_ready, 16 * (E * i + e))
                        wait(sp, h_ready, NC * (i - 1) + last_chunk(e) + 1)
                        src = comb[bass.ds(i, 1), e, :, :].rearrange("o t p -> (o t p)")
                        sp.dma_start(CB[:, e, :], src.partition_broadcast(P)).then_inc(cb_ready, 16)

                for i in range(NJ):
                    body(i)
                    if i == 0:
                        for j in range(1, NJ):
                            comb_of(j)
                        sp.wait_ge(comb_out, 16 * NJ)
                sp.wait_ge(cb_ready, 16 * E * NJ)


def second_attention(nc, sem, w, ident, idb, ps, XNT, Y, ATT, n1, n2, loaded_c):
    NG = B * NH1 // 4
    KC = S // P
    SCALE = 1.0 / float(np.sqrt(np.float32(NH1 + DC + DC)))
    NR, MR = 9 * DH1, 96
    KR = MR + 3
    NQ = 3
    with ExitStack() as c0:
        def sb(name, shape, dt=F32):
            return c0.enter_context(nc.sbuf_tensor("sa_" + name, shape, dt))

        VA = sb("VA", [P, NG, KC, 4, DH1 + 1])
        ATT = ATT[:, :, :].rearrange("p (b q) (g f) -> p b q g f", b=B, g=4)
        parts_q = nc.dram_tensor("parts_q", [3, NG * DH1, 4 * S], BF16, kind="Internal").ap()
        parts_k = nc.dram_tensor("parts_k", [3, NG * DH1, 4 * S], BF16, kind="Internal").ap()
        QS, KS = sb("QS", [P, NQ, 4, S], BF16), sb("KS", [P, NQ, 4, S], BF16)
        SPL = sb("SPL", [P, 2, 2, 3, NB], BF16)
        rows_set, parts_out = sem("sa_rows_set"), (sem("sa_parts_out0"), sem("sa_parts_out1"))

        VG = sb("VG", [P, KC, 4, 32])
        MS = sb("MS", [P, 2, KC, KR], BF16)
        stacked, st_ready, zeroed = sem("sa_stacked"), sem("sm_st_ready"), sem("sm_zeroed")
        NSTACK = 2 * 3
        IT = 4 * KC + 4

        def stack_rows(pool, n):
            for k, (dst, a, b, value) in enumerate(((QS, 64, MR, 0.0), (KS, 64, MR, 0.0), (KS, MR, KR, 1.0))):
                pool.wait_ge(rows_set, 1 + 3 * n + k)
                pool.memset(dst[a:b, n, :, :], value).then_inc(rows_set, 1)

        def stack(sp, g):
            wait(sp, stacked, 16 * NSTACK * g)
            if not (isinstance(g, int) and g < NQ):
                sp.wait_ge(st_ready, 2 * (IT * (g - NQ + 1) + 3))
            for i in range(3):
                rows = slice(3 * DH1 * i, 3 * DH1 * (i + 1))
                q_i = parts_q[i, bass.ds(DH1 * g, DH1), :].unsqueeze(0).to_broadcast([3, DH1, 4 * S])
                for dst, src in ((QS, q_i), (KS, parts_k[:, bass.ds(DH1 * g, DH1), :])):
                    sp.dma_start(dst[rows, bass.ds(g % NQ, 1), :, :].rearrange("r o h n -> r (o h n)"), src).then_inc(stacked, 16)

        with ExitStack() as c:
            def sbi(name, shape, dt=F32):
                return c.enter_context(nc.sbuf_tensor("sp_" + name, shape, dt))

            CT = sbi("CT", [P, 2, NB])
            r1, r2, r3 = (sbi(n, [P, NB]) for n in ("r1", "r2", "r3"))
            qk, rest = sbi("qk", [P, 2, NB]), sbi("rest", [P, 2, NB])
            ct_psum, ct_ready, q_psum, k_psum, v_psum, q_read, k_read, v_read, dve_done = (
                sem("sp_" + n) for n in "ct_psum ct_ready q_psum k_psum v_psum q_read k_read v_read dve_done".split())
            qk_ready, first_part, rest_ready, second_part, split = (
                sem("sp_" + n) for n in "qk_ready first_part rest_ready second_part split".split())
            NJ = TOK // NB

            with nc.Block() as block:
                @block.gpsimd
                def _(pool):
                    n1.gpsimd(pool)
                    pool.memset(VA[:, :, :, :, DH1:DH1 + 1], 1.0).then_inc(rows_set, 1)
                    stack_rows(pool, 0)
                    pool.wait_ge(rows_set, 4)
                    pool.memset(VG[:, :, :, :], 0.0).then_inc(zeroed, 1)
                    pool.memset(MS[:, :, :, :], 0.0).then_inc(zeroed, 1)

                    def third_part(u):
                        pool.wait_ge(second_part, u + 1)
                        pool.tensor_tensor(SPL[:, (u // 2) % 2, u % 2, 2, :], rest[:, u % 2, :], SPL[:, (u // 2) % 2, u % 2, 1, :],
                                           ALU.subtract).then_inc(split, 1)

                    for u in range(2 * NJ):
                        pool.wait_ge(first_part, u + 1)
                        wait(pool, split, u - 1)
                        pool.tensor_tensor(rest[:, u % 2, :], qk[:, u % 2, :], SPL[:, (u // 2) % 2, u % 2, 0, :],
                                           ALU.subtract).then_inc(rest_ready, 1)
                        if u:
                            third_part(u - 1)
                    third_part(2 * NJ - 1)
                    pool.wait_ge(zeroed, 2)
                    pool.wait_ge(split, 2 * NJ)

                @block.tensor
                def _(pe):
                    def down(j):
                        wait(pe, ct_ready, j)
                        pe.matmul(ps[:, 0, :], w("Wdown"), XNT[:, NB * j:NB * (j + 1)], start=True, stop=True).then_inc(ct_psum, 1)

                    pe.wait_ge(loaded_c, 16)
                    for j in range(NJT - 1):
                        n1.turn(pe, j)
                    n1.at_least(pe, "evac", 1)
                    down(0)
                    n1.at_least(pe, "evac", 2)
                    for j in range(NJ):
                        x, ct = XNT[:, NB * j:NB * (j + 1)], CT[:, j % 2, :]
                        if j + 1 < NJ:
                            down(j + 1)
                        pe.wait_ge(ct_ready, j + 1)
                        wait(pe, q_read, j)
                        for n, name in ((2, "Wqr"), (3, "Wqr_sw"), (1, "Wuq")):
                            ins = pe.matmul(ps[:, n, :], w(name), ct, start=True, stop=True)
                        ins.then_inc(q_psum, 1)
                        if j == 0:
                            n1.turn(pe, 3)
                            n1.at_least(pe, "evac", 3)
                        wait(pe, k_read, j)
                        pe.matmul(ps[:, 5, :], w("Wkr"), x, start=True, stop=True)
                        pe.matmul(ps[:, 6, :], w("Wkr_sw"), x, start=True, stop=True)
                        if j == 0:
                            n1.at_least(pe, "evac", 4)
                        pe.matmul(ps[:, 4, :], w("Wuk"), ct, start=True, stop=True).then_inc(k_psum, 1)
                        wait(pe, v_read, 4 * j)
                        for n in range(4):
                            pe.matmul(ps[:, 7, P * n:P * (n + 1)], CT[:, j % 2, P * n:P * (n + 1)], w("Wuv"), start=True, stop=False)
                            ins = pe.matmul(ps[:, 7, P * n:P * (n + 1)], ident, w("b_uv_row"), start=False, stop=True)
                        ins.then_inc(v_psum, 1)

                @block.scalar
                def _(act):
                    def compressed(j):
                        act.wait_ge(ct_psum, j + 1)
                        wait(act, v_psum, j - 1)
                        act.activation(CT[:, j % 2, :], ps[:, 0, :], ACT.Identity, bias=w("b_down")).then_inc(ct_ready, 1)

                    n1.deviation_y(act, NJT - 1)
                    for j in range(NJT - 1):
                        n1.xnt_of(act, j, XNT)
                    compressed(0)
                    n1.deviation_x(act, NJT - 1)
                    compressed(1)
                    n1.xnt_of(act, NJT - 1, XNT)
                    for j in range(NJ):
                        if 0 < j < NJ - 1:
                            compressed(j + 1)
                        for k in range(2):
                            u = 2 * j + k
                            act.wait_ge(qk_ready, u + 1)
                            wait(act, parts_out[j % 2], 16 * 2 * (j // 2))
                            act.activation(SPL[:, j % 2, k, 0, :], qk[:, u % 2, :], ACT.Copy).then_inc(first_part, 1)
                            act.wait_ge(rest_ready, u + 1)
                            act.activation(SPL[:, j % 2, k, 1, :], rest[:, u % 2, :], ACT.Copy).then_inc(second_part, 1)
                        act.wait_ge(v_psum, j + 1)
                        act.wait_ge(rows_set, 1)
                        b, kc = j // 2, 4 * (j % 2)
                        for n in range(4):
                            ins = act.activation(VA[:, 4 * b:4 * b + 4, kc + n, :, 0:DH1],
                                                 ps[:, 7, P * n:P * (n + 1)].rearrange("p (g h d) -> p g h d", h=4, d=DH1), ACT.Copy)
                            ins.then_inc(v_read, 1)
                    act.wait_ge(v_read, 4 * NJ)

                @block.vector
                def _(dve):
                    chain = Count(dve_done)

                    n1.factors_y(dve, NJT - 1)
                    n1.sum_x(dve, NJT - 1)
                    n1.factors_x(dve, NJT - 1)
                    n1.xn_by_vector(dve, NJT - 1)
                    for j in range(NJ):
                        pos = slice(NB * (j % 2), NB * (j % 2 + 1))
                        cos, sin = w("cos")[:, pos], w("sin")[:, pos]
                        for k, (bank, psum, read, bs) in enumerate((((1, 2, 3), q_psum, q_read, ("b_uq", "b_qr", "b_qr_sw")),
                                                                    ((4, 5, 6), k_psum, k_read, ("b_uk", "b_kr", "b_kr_sw")))):
                            u = 2 * j + k
                            dve.wait_ge(psum, j + 1)
                            wait(dve, qk_ready, u)
                            chain.add(dve.scalar_tensor_tensor(out=r1[:, :], in0=ps[:, bank[1], :], scalar=w(bs[1]), in1=cos,
                                                               op0=ALU.add, op1=ALU.mult))
                            n = chain.add(dve.scalar_tensor_tensor(out=r2[:, :], in0=ps[:, bank[2], :], scalar=w(bs[2]), in1=sin,
                                                                   op0=ALU.add, op1=ALU.mult))
                            dve.wait_ge(dve_done, n - 1)
                            dve.scalar_tensor_tensor(out=r3[:, :], in0=ps[:, bank[0], :], scalar=w(bs[0]), in1=r1[:, :],
                                                     op0=ALU.add, op1=ALU.add).then_inc(read, 1)
                            dve.wait_ge(read, j + 1)
                            wait(dve, first_part, u - 1)
                            wait(dve, rest_ready, u - 1)
                            dve.tensor_tensor(qk[:, u % 2, :], r3[:, :], r2[:, :], ALU.add).then_inc(qk_ready, 1)
                    dve.wait_ge(qk_ready, 2 * NJ)

                @block.sync
                def _(sp):
                    for j in range(NJ):
                        b, pos = j // 2, slice(NB * (j % 2), NB * (j % 2 + 1))
                        for k, parts in enumerate((parts_q, parts_k)):
                            sp.wait_ge(split, 2 * j + k + 1)
                            dst = parts[:, D // 4 * b:D // 4 * (b + 1), :].rearrange("i r (h n) -> (r h) i n", h=4)
                            sp.dma_start(dst[:, :, pos], SPL[:, j % 2, k, :, :]).then_inc(parts_out[j % 2], 16)
                        if j == 1:
                            sp.wait_ge(parts_out[0], 16 * 2)
                            sp.wait_ge(parts_out[1], 16 * 2)
                            sp.wait_ge(rows_set, 1 + 3)
                            stack(sp, 0)

        PR = sb("PR", [P, 2, 4, S])
        OU = XNT[:, 0:S]
        MX = sb("MX", [P, 4, KC, 2])
        NM, R1, R2 = sb("NM", [P, KC]), sb("R1", [P, KC]), sb("R2", [P, KC])
        RD = sb("RD", [P, KC, 4])
        (st_used, pv_done, s_ready, smax_done, ms_ready, vg_ready, ou_ready, turned, small_done,
         rd_ready) = (sem("sm_" + n) for n in
                              "st_used pv_done s_ready smax_done ms_ready vg_ready ou_ready turned small_done rd_ready".split())
        SLOTS = 4 * KC
        ST, PV = 4, 6
        NQR = S // 4

        def items(last):
            out = []
            for s in range(SLOTS):
                out.append(("scores", s // 4, s % 4))
                if s == 1:
                    out.append(("maxima", 0, 3))
                if s in (10, 18, 26) and not last:
                    out.append(("maxima", 1, s // 8 - 1))
            return out

        def item_count(g, k, half=1):
            return 2 * (IT * g + 3 + k) + half + 1

        def slot_count(g, s, half=1, last=False):
            return item_count(g, items(last).index(("scores", s // 4, s % 4)), half)

        def maxima_item(g, h):
            if h == 3:
                return item_count(g, 2)
            if isinstance(g, int) and g == 0:
                return 2 * (h + 1)
            return item_count(g - 1, items(False).index(("maxima", 1, h)))

        def first_bank(k, last):
            return (ST, 0, 2)[k % 3] if last else ST

        def wait_for_bank(pe, k, n, at, last):
            if not last:
                wait(pe, st_used, at + n - 2)
            elif k == 0:
                pe.wait_ge(st_used, at + n - 2)
            elif k < 3:
                pe.wait_ge(smax_done, SLOTS * NG + k - 2)
            else:
                pe.wait_ge(st_used, at + n - 6)

        def sums_in_slot(s):
            if s == 0:
                return [(1, KC - 2, 3)]
            if s in (1, 2):
                return [(1, KC - 1, 2 * s - 2), (1, KC - 1, 2 * s - 1)]
            if s in (6, 7, 8):
                return [(0, 0, s - 6)]
            if s == 9:
                return [(0, 0, 3), (0, 1, 0)]
            return [(0, (s - 5) // 4, (s - 5) % 4)] if s > 9 else []

        with nc.Block() as block:
            @block.sync
            def _(sp):
                for k in range(2):
                    sp.wait_ge(parts_out[k], 16 * TOK // NB)
                for g in range(1, NQ):
                    sp.wait_ge(rows_set, 1 + 3 * (g + 1))
                    stack(sp, g)
                with sp.Fori(NQ, NG) as g:
                    stack(sp, g)

            @block.gpsimd
            def _(pool):
                def values(g):
                    wait(pool, pv_done, SLOTS * g)
                    pool.tensor_copy(VG[:, :, :, 0:DH1 + 1],
                                     VA[:, bass.ds(g, 1), :, :, :].rearrange("p o k h d -> p (o k) h d")).then_inc(vg_ready, 1)

                values(0)
                pool.wait_ge(vg_ready, 1)
                for n in range(1, NQ):
                    stack_rows(pool, n)
                pool.wait_ge(rows_set, 1 + 3 * NQ)
                with pool.Fori(1, NG) as g:
                    values(g)

            @block.tensor
            def _(pe):
                def row_scores(g, x):
                    h, qt, par = x // KC, x % KC, g % NQ
                    if x == 0:
                        wait(pe, stacked, 16 * NSTACK * (g + 1))
                    wait(pe, smax_done, SLOTS * g + x - 1)
                    for n in range(2):
                        ins = pe.matmul(ps[:, 2 * (x % 2) + n, :], QS[0:MR, bass.ds(par, 1), h, P * qt:P * (qt + 1)].rearrange("p o n -> p (o n)"),
                                        KS[0:MR, bass.ds(par, 1), h, NB * n:NB * (n + 1)].rearrange("p o n -> p (o n)"),
                                        start=True, stop=True)
                    ins.then_inc(s_ready, 1)

                def maxima_rows(g, h, at, k=0, last=False):
                    wait(pe, ms_ready, 4 * g + h + 1)
                    for n in range(2):
                        wait_for_bank(pe, k, n, at, last)
                        for qt in range(4 * n, 4 * n + 4):
                            ins = pe.matmul(ps[0:KR, first_bank(k, last) + n, P * (qt % 4):P * (qt % 4 + 1)], MS[:, h % 2, qt, :], idb[:, :],
                                            start=True, stop=True)
                        ins.then_inc(st_ready, 1)

                def key_scores(g, kc, h, at, k, last):
                    par = g % NQ
                    if kc == 0:
                        wait(pe, st_used, maxima_item(g, h))
                    for n in range(2):
                        wait_for_bank(pe, k, n, at, last)
                        pe.matmul(ps[:, first_bank(k, last) + n, :], KS[0:KR, bass.ds(par, 1), h, P * kc:P * (kc + 1)].rearrange("p o n -> p (o n)"),
                                  QS[0:KR, bass.ds(par, 1), h, NB * n:NB * (n + 1)].rearrange("p o n -> p (o n)"),
                                  start=True, stop=True).then_inc(st_ready, 1)

                def values(g, kc, q, last=False):
                    if q == 0:
                        wait(pe, st_used, slot_count(g, 4 * kc + 3, 1, last))
                    if kc == 0:
                        wait(pe, vg_ready, g + 1)
                        wait(pe, rd_ready, 4 * (g - 1) + (4 if q > 1 else 2))
                    for h in range(4):
                        ins = pe.matmul(ps[32 * h:32 * (h + 1), PV + q // 2, NQR * (q % 2):NQR * (q % 2 + 1)], VG[:, kc, h, :],
                                        PR[:, kc % 2, h, NQR * q:NQR * (q + 1)], start=(kc == 0 and q % 2 == 0),
                                        stop=(kc == KC - 1), tile_position=(0, 32 * h), skip_group_check=True)
                    ins.then_inc(pv_done, 1)

                def turn(g, n):
                    wait(pe, ou_ready, 2 * g + n + 1)
                    for qt in range(4):
                        ins = pe.transpose(ps[:, PV + n, P * qt:P * (qt + 1)], OU[:, NB * n + P * qt:NB * n + P * (qt + 1)], ident)
                    ins.then_inc(turned, 1)

                def body(g, first, last):
                    s = 0
                    for k, (kind, kc, h) in enumerate(items(last)):
                        at = item_count(g, k, 0)
                        if kind == "maxima":
                            maxima_rows(g + kc, h, at, k, last)
                            continue
                        if s in (4, 6) and not first:
                            turn(g - 1, s // 2 - 2)
                        for back, chunk, q in sums_in_slot(s):
                            if not (first and back):
                                values(g - back, chunk, q, last and not back)
                        key_scores(g, kc, h, at, k, last)
                        if not last:
                            row_scores(g + 1, s)
                        s += 1

                for h in range(4):
                    for qt in range(KC):
                        row_scores(0, KC * h + qt)
                    if h:
                        maxima_rows(0, h - 1, 2 * h - 1)
                body(0, True, False)
                with pe.Fori(1, NG - 1) as g:
                    body(g, False, False)
                body(NG - 1, False, True)
                values(NG - 1, KC - 2, 3, True)
                for q in range(4):
                    values(NG - 1, KC - 1, q, True)
                for n in range(2):
                    turn(NG - 1, n)

            @block.scalar
            def _(act):
                def rows_out(g, h, at, bank=ST):
                    for n in range(2):
                        act.wait_ge(st_ready, at + n)
                        act.activation(QS[MR:KR, bass.ds(g % NQ, 1), h, NB * n:NB * (n + 1)], ps[MR:KR, bank + n, :].unsqueeze(1),
                                       ACT.Copy).then_inc(st_used, 1)

                def sums_out(g, n):
                    wait(act, pv_done, SLOTS * g + 4 * (KC - 1) + 2 * (n + 1))
                    act.activation(OU[:, NB * n:NB * (n + 1)], ps[:, PV + n, :], ACT.Copy).then_inc(ou_ready, 1)

                def body(g, first, last):
                    s = 0
                    for k, (kind, kc, h) in enumerate(items(last)):
                        at = item_count(g, k, 0)
                        if kind == "maxima":
                            rows_out(g + kc, h, at, first_bank(k, last))
                            continue
                        for n in range(2):
                            act.wait_ge(st_ready, at + n)
                            wait(act, pv_done, SLOTS * g + 4 * (kc - 2) + 2 * (n + 1))
                            act.activation(PR[:, kc % 2, h, NB * n:NB * (n + 1)], ps[:, first_bank(k, last) + n, :], ACT.Exp,
                                           scale=SCALE).then_inc(st_used, 1)
                        if s in (2, 3) and not first:
                            sums_out(g - 1, s - 2)
                        s += 1

                for h in range(3):
                    rows_out(0, h, 2 * h + 1)
                body(0, True, False)
                with act.Fori(1, NG - 1) as g:
                    body(g, False, False)
                body(NG - 1, False, True)
                for n in range(2):
                    sums_out(NG - 1, n)

            @block.vector
            def _(dve):
                def row_maxima(g, x):
                    h, qt = x // KC, x % KC
                    wait(dve, s_ready, SLOTS * g + x + 1)
                    if qt == 0:
                        wait(dve, small_done, 4 * (4 * g + h) - 12)
                    dve.tensor_reduce(MX[:, h, qt, :], ps[:, 2 * (x % 2):2 * (x % 2) + 2, :], AX.X, ALU.max).then_inc(smax_done, 1)

                def split_maxima(g, h):
                    par, base = h % 2, 4 * (4 * g + h)
                    wait(dve, smax_done, SLOTS * g + KC * (h + 1))
                    if not (isinstance(g, int) and g == 0 and h < 2):
                        wait(dve, st_ready, maxima_item(g, h - 2) if h >= 2 else maxima_item(g - 1, h + 2))
                    dve.tensor_reduce(NM[:, :], MX[:, h, :, :], AX.X, ALU.max, negate=True).then_inc(small_done, 1)
                    dve.wait_ge(small_done, base + 1)
                    dve.tensor_copy(MS[:, par, :, MR:MR + 1], NM[:, :].unsqueeze(2)).then_inc(small_done, 1)
                    dve.wait_ge(small_done, base + 2)
                    dve.tensor_tensor(R1[:, :].unsqueeze(2), NM[:, :].unsqueeze(2), MS[:, par, :, MR:MR + 1], ALU.subtract).then_inc(small_done, 1)
                    dve.wait_ge(small_done, base + 3)
                    dve.tensor_copy(MS[:, par, :, MR + 1:MR + 2], R1[:, :].unsqueeze(2)).then_inc(small_done, 1)
                    dve.wait_ge(small_done, base + 4)
                    dve.tensor_tensor(MS[:, par, :, MR + 2:MR + 3], R1[:, :].unsqueeze(2), MS[:, par, :, MR + 1:MR + 2],
                                      ALU.subtract).then_inc(ms_ready, 1)

                def divide(g, n):
                    wait(dve, turned, 2 * g + n + 1)
                    sums = ps[:, PV + n, :].rearrange("p (q h d) -> p q h d", h=4, d=32)
                    rd = RD[:, 4 * n:4 * n + 4, :].unsqueeze(3)
                    dve.reciprocal(rd, sums[:, :, :, DH1:DH1 + 1]).then_inc(rd_ready, 1)
                    dve.wait_ge(rd_ready, 4 * g + 2 * n + 1)
                    dve.tensor_tensor(ATT[:, bass.ds(g // 4, 1), 4 * n:4 * n + 4, bass.ds(g % 4, 1), :].rearrange("p o q r (h d) -> p (o q r) h d", h=4),
                                      sums[:, :, :, 0:DH1], rd.to_broadcast([P, 4, 4, DH1]), ALU.mult).then_inc(rd_ready, 1)

                def body(g, first, last):
                    for x in range(SLOTS):
                        if not last:
                            row_maxima(g + 1, x)
                            if x % KC == KC - 1:
                                split_maxima(g + 1, x // KC)
                        if x in (4, 5) and not first:
                            divide(g - 1, x - 4)

                for x in range(SLOTS):
                    row_maxima(0, x)
                    if x % KC == KC - 1:
                        split_maxima(0, x // KC)
                body(0, True, False)
                with dve.Fori(1, NG - 1) as g:
                    body(g, False, False)
                body(NG - 1, False, True)
                for n in range(2):
                    divide(NG - 1, n)
                dve.wait_ge(rd_ready, 4 * NG)

        attT = XNT[:, S:2 * S].rearrange("p (j t d) -> p j t d", j=2, d=P)
        t_ready, t_out, o_ready, y_ready = sem("so_t_ready"), sem("so_t_out"), sem("so_o_ready"), sem("so_y_ready")
        with nc.Block() as block:
            @block.tensor
            def _(pe):
                def turn(j):
                    wait(pe, t_out, j - 1)
                    for n in range(4):
                        b, qt = (4 * j + n) // KC, (4 * j + n) % KC
                        ins = pe.transpose(ps[:, j % 2, P * n:P * (n + 1)], ATT[:, b, qt, :, :].rearrange("p g f -> p (g f)"), ident)
                    ins.then_inc(t_ready, 1)

                turn(0)
                for j in range(TT // 4):
                    if j + 1 < TT // 4:
                        turn(j + 1)
                    pe.wait_ge(t_out, j + 1)
                    wait(pe, y_ready, j - 1)
                    for n in range(4):
                        ins = pe.matmul(ps[:, 2 + j % 2, P * n:P * (n + 1)], attT[:, j % 2, n, :], w("WoL1"), start=True, stop=True)
                    ins.then_inc(o_ready, 1)

            @block.scalar
            def _(act):
                for j in range(TT // 4):
                    act.wait_ge(t_ready, j + 1)
                    wait(act, o_ready, j - 1)
                    act.activation(attT[:, j % 2, :, :], ps[:, j % 2, :].rearrange("p (t d) -> p t d", d=P), ACT.Copy).then_inc(t_out, 1)
                for j in range(NJT):
                    n2.deviation_y(act, j)
                n2.deviation_x(act, 0)

            @block.vector
            def _(dve):
                for j in range(TT // 4):
                    dve.wait_ge(o_ready, j + 1)
                    dve.tensor_tensor(Y[:, 4 * j:4 * j + 4, :], ps[:, 2 + j % 2, :].rearrange("p (t d) -> p t d", d=D),
                                      w("b_o_row").unsqueeze(1).to_broadcast([P, 4, D]), ALU.add).then_inc(y_ready, 1)
                    dve.wait_ge(y_ready, j + 1)
                    n2.y_stat.block(dve, Y, j)
                for j in range(NJT):
                    n2.factors_y(dve, j)
                n2.sum_x(dve, 0)
                n2.factors_x(dve, 0)
                n2.at_least(dve, "factors2", 2)


def channel_mix(nc, sem, w, ident, ps, XNT, Y, n2, norm, y_stat, out):
    NJ = TOK // NB
    with ExitStack() as c:
        def sb(name, shape, dt=F32):
            return c.enter_context(nc.sbuf_tensor("cm_" + name, shape, dt))

        n3 = norm(3, c, None, out)
        om = sb("om", [P, 2])
        pr, pk = sb("pr", [P, TOK]), sb("pk", [P, TOK])
        xr, xk = sb("xr", [P, TOK]), sb("xk", [P, TOK])
        r, kr, ka, o = sb("r", [P, 2, NB]), sb("kr", [P, 2, NB]), sb("ka", [P, 2, NB]), sb("o", [P, 2, NB])
        one_minus, shifted, zero, mixed = sem("cm_one_minus"), sem("cm_shifted"), sem("cm_zero"), sem("cm_mixed")
        rk_ready, r_out, k_out, ka_ready, v_ready, o_ready, turned, y_ready = (
            sem("cm_" + n) for n in "rk_ready r_out k_out ka_ready v_ready o_ready turned y_ready".split())

        with nc.Block() as block:
            @block.vector
            def _(dve):
                dve.tensor_scalar(om[:, 0:1], w("mu_r"), -1.0, 1.0, ALU.mult, ALU.add).then_inc(one_minus, 1)
                dve.tensor_scalar(om[:, 1:2], w("mu_k"), -1.0, 1.0, ALU.mult, ALU.add).then_inc(one_minus, 1)
                dve.wait_ge(zero, 4)

                def mix(j):
                    cols = slice(NB * j, NB * (j + 1))
                    for n, (mu, p, x) in enumerate((("mu_r", pr, xr), ("mu_k", pk, xk))):
                        dve.wait_ge(shifted, 2 * j + n + 1)
                        dve.scalar_tensor_tensor(out=x[:, cols], in0=XNT[:, cols], scalar=w(mu), in1=p[:, cols],
                                                 op0=ALU.mult, op1=ALU.add).then_inc(mixed, 1)

                n2.vector(dve, begun=True)
                for j in range(NJ - 1):
                    mix(j)
                for j in range(NJ):
                    dve.wait_ge(k_out, j + 1)
                    wait(dve, v_ready, j - 1)
                    dve.tensor_tensor(ka[:, j % 2, :], kr[:, j % 2, :], kr[:, j % 2, :], ALU.mult).then_inc(ka_ready, 1)
                    if j == 0:
                        mix(NJ - 1)
                    dve.wait_ge(v_ready, j + 1)
                    dve.wait_ge(r_out, j + 1)
                    wait(dve, turned, j - 1)
                    dve.tensor_tensor(o[:, j % 2, :], r[:, j % 2, :], ps[:, 4 + j % 2, :], ALU.mult).then_inc(o_ready, 1)
                    if j >= 2:
                        dve.wait_ge(y_ready, j - 1)
                        y_stat.block(dve, Y, j - 2)
                n3.at_least(dve, "x_ready", 0)
                dve.wait_ge(y_ready, 3)
                y_stat.block(dve, Y, 2)
                n3.factors_y(dve, 0)
                n3.factors_y(dve, 1)
                dve.wait_ge(y_ready, 4)
                y_stat.block(dve, Y, 3)
                n3.factors_y(dve, 2)
                n3.last_by_vector(dve, 2)
                n3.last_sum(dve, 0)
                n3.factors_y(dve, 3)
                n3.last_by_vector(dve, 3)
                for j in range(1, NJ):
                    n3.last_sum(dve, j)

            @block.gpsimd
            def _(pool):
                for b in range(B):
                    for dst in (pr, pk):
                        pool.memset(dst[:, S * b:S * b + 1], 0.0).then_inc(zero, 1)
                n2.gpsimd(pool)

            @block.tensor
            def _(pe):
                def rk(j):
                    pe.wait_ge(mixed, 2 * (j + 1))
                    wait(pe, r_out, j - 1)
                    wait(pe, k_out, j - 1)
                    pe.matmul(ps[:, j % 2, :], w("W_rT"), xr[:, NB * j:NB * (j + 1)], start=True, stop=True)
                    pe.matmul(ps[:, 2 + j % 2, :], w("W_kT"), xk[:, NB * j:NB * (j + 1)], start=True, stop=True).then_inc(rk_ready, 1)

                for j in range(NJT):
                    n2.turn(pe, j)
                rk(0)
                def turn(j):
                    pe.wait_ge(o_ready, j + 1)
                    wait(pe, y_ready, j - 1)
                    for n in range(4):
                        ins = pe.transpose(ps[:, 6 + j % 2, P * n:P * (n + 1)], o[:, j % 2, P * n:P * (n + 1)], ident)
                    ins.then_inc(turned, 1)

                for j in range(NJ):
                    if j + 1 < NJ:
                        rk(j + 1)
                    pe.wait_ge(ka_ready, j + 1)
                    wait(pe, o_ready, j - 1)
                    pe.matmul(ps[:, 4 + j % 2, :], w("W_vT"), ka[:, j % 2, :], start=True, stop=True).then_inc(v_ready, 1)
                    if j:
                        turn(j - 1)
                turn(NJ - 1)

            @block.scalar
            def _(act):
                def shift(j):
                    first = 1 if j % (S // NB) == 0 else 0
                    n2.at_least(act, "evac", j + 1)
                    for n, dst in enumerate((pr, pk)):
                        act.activation(dst[:, NB * j + first:NB * (j + 1)], XNT[:, NB * j + first - 1:NB * (j + 1) - 1], ACT.Copy,
                                       scale=om[:, n:n + 1]).then_inc(shifted, 1)

                def y_of(j):
                    act.wait_ge(turned, j + 1)
                    n2.at_least(act, "x_ready", j + 1)
                    act.activation(Y[:, 4 * j:4 * j + 4, :], ps[:, 6 + j % 2, :].rearrange("p (t d) -> p t d", d=D),
                                   ACT.Copy).then_inc(y_ready, 1)

                act.wait_ge(one_minus, 2)
                n2.scalar(act, XNT, shift, begun=True)
                for j in range(NJ):
                    act.wait_ge(rk_ready, j + 1)
                    wait(act, ka_ready, j - 1)
                    act.activation(kr[:, j % 2, :], ps[:, 2 + j % 2, :], ACT.Relu).then_inc(k_out, 1)
                    wait(act, o_ready, j - 1)
                    act.activation(r[:, j % 2, :], ps[:, j % 2, :], ACT.Sigmoid).then_inc(r_out, 1)
                    if j:
                        y_of(j - 1)
                n3.deviation_y(act, 0)
                n3.deviation_y(act, 1)
                y_of(NJ - 1)
                n3.deviation_y(act, 2)
                n3.last_by_scalar(act, 0)
                n3.deviation_y(act, 3)
                n3.last_by_scalar(act, 1)

            @block.sync
            def _(sp):
                n3.store(sp)


def _packed(pack, parts):
    cols = []
    for name, n in pack:
        a = np.asarray(parts[name])
        full = np.zeros((P, n), np.float32)
        full[:a.shape[0], :] = a.reshape(a.shape[0], n)
        cols.append(full)
    return np.ascontiguousarray(np.concatenate(cols, axis=1))


def _layout(x):
    def col(v):
        return np.asarray(v).reshape(-1, 1)

    def rows(v, n=P):
        return np.broadcast_to(np.asarray(v).reshape(1, -1), (n, np.asarray(v).size))

    def low(a):
        return np.concatenate([a, np.zeros((P - a.shape[0], a.shape[1]), a.dtype)], 0)

    def high(a):
        return np.concatenate([np.zeros((P - a.shape[0], a.shape[1]), a.dtype), a], 0)

    g = {k: np.asarray(v) for k, v in x.items()}
    pair = np.arange(D) ^ 1
    b1row = np.zeros((P, HID), np.float32)
    b1row[[0, 32, 64]] = g["L0_attn_b1"]
    masks, ones3 = _constants()
    a = {
        "masks": masks, "ones3": ones3,
        "woT": g["L0_attn_wo"].T, "wqT": g["L0_attn_wq"].T, "wkT": g["L0_attn_wk"].T, "wvT": g["L0_attn_wv"].T,
        "ident": np.eye(P, dtype=np.float32),
        "headmask": (np.arange(P)[:, None] // DH0 == np.arange(NH0)).astype(np.float32),
        "b1row": b1row, "b2row": rows(g["L0_attn_b2"]), "alpha": rows(g["L0_attn_alpha"]), "theta": rows(g["L0_attn_theta"]),
        "b1col": g["L0_attn_b1"].reshape(HC, P).T, "b2col": col(g["L0_attn_b2"]), "ones": np.ones((P, 1), np.float32),
        "w1T": g["L0_attn_w1"].T, "w2": g["L0_attn_w2"],
        "w2T": g["L0_attn_w2"].T.reshape(HC, P, D).transpose(1, 0, 2).reshape(P, HID),
    }
    b = {
        "lin1T": g["L0_attn_lin1"].T, "lin2T": g["L0_attn_lin2"].T, "routerT": g["L0_ffn_router_w"].T,
        "expert_no": rows(np.arange(E, dtype=np.float32)),
        "WgT": g["L0_ffn_Wg"].transpose(2, 0, 1).reshape(D, E * I), "WuT": g["L0_ffn_Wu"].transpose(2, 0, 1).reshape(D, E * I),
        "WdT": g["L0_ffn_Wd"].transpose(0, 2, 1).reshape(E * I // P, P, D).transpose(1, 0, 2).reshape(P, E * I // P * D),
    }
    theta = np.float32(10000.0) ** (np.float32(-2.0) * np.arange(D // 2, dtype=np.float32)) / np.float32(D // 2)
    angle = (np.arange(S, dtype=np.float32)[:, None] * theta[None, :]).astype(np.float64)
    cos, sin = np.cos(angle).astype(np.float32), np.sin(angle).astype(np.float32)
    sin_signed = np.repeat(sin.T, 2, axis=0)
    sin_signed[0::2] = -sin_signed[0::2]
    q = {k[8:]: v for k, v in g.items() if k.startswith("L1_attn_")}
    order = np.arange(D).reshape(NH1 // 4, 4, DH1).transpose(0, 2, 1).reshape(D)
    pair = pair[order]
    cc = {
        "Wdown": np.concatenate([q["Wd_q_w"], q["Wd_kv_w"]], 1),
        "Wuq": low(q["Wu_q_w"][:, order]), "Wqr": low(q["Wq_r_w"][:, order]), "Wqr_sw": low(q["Wq_r_w"][:, pair]),
        "Wuk": high(q["Wu_k_w"][:, order]), "Wkr": q["Wk_r_w"][:, order], "Wkr_sw": q["Wk_r_w"][:, pair], "Wuv": high(q["Wu_v_w"]),
        "b_down": col(np.concatenate([q["Wd_q_b"], q["Wd_kv_b"]])), "b_uq": col(q["Wu_q_b"][order]), "b_qr": col(q["Wq_r_b"][order]),
        "b_qr_sw": col(q["Wq_r_b"][pair]), "b_uk": col(q["Wu_k_b"][order]), "b_kr": col(q["Wk_r_b"][order]), "b_kr_sw": col(q["Wk_r_b"][pair]),
        "b_uv_row": rows(q["Wu_v_b"]), "WoL1": q["Wo_w"], "b_o_row": rows(q["Wo_b"]),
        "cos": np.repeat(cos.T, 2, axis=0)[order], "sin": sin_signed[order],
        "W_rT": g["L1_ffn_W_r"].T, "W_kT": g["L1_ffn_W_k"].T, "W_vT": g["L1_ffn_W_v"].T,
        "mu_r": col(g["L1_ffn_mu_r"]), "mu_k": col(g["L1_ffn_mu_k"]),
    }
    return _packed(PACK_A, a), _packed(PACK_B, b), _packed(PACK_C, cc)


def _constants():
    r, k = np.arange(P)[:, None], np.arange(KW)[None, :]
    seen = (k > r) & (k <= r + WIN)
    tiles = [seen, seen & (k >= NPM), seen & ((r < NPM) | (k >= P))]
    ones3 = np.zeros((P, P), np.float32)
    ones3[[0, 32, 64]] = 1
    return np.concatenate([np.where(m, 0.0, -2.0 ** 100) for m in tiles], 1).astype(np.float32), ones3


def kernel(**inputs):
    import concourse.bacc as bacc
    from concourse.bass_utils import run_bass_kernel_spmd

    pack_a, pack_b, pack_c = _layout({k: v for k, v in inputs.items() if k not in ("L0_attn_x", "L0_attn_mem")})
    arrays = {"pack_a": pack_a, "pack_b": pack_b, "pack_c": pack_c,
              "x_in": np.ascontiguousarray(np.asarray(inputs["L0_attn_x"]).reshape(TOK, D)),
              "mem": np.ascontiguousarray(np.asarray(inputs["L0_attn_mem"]))}
    nc = bacc.Bacc("TRN2", target_bir_lowering=False, num_devices=1)
    aps = [nc.dram_tensor(n, a.shape, mybir.dt.from_np(a.dtype), kind="ExternalInput").ap() for n, a in arrays.items()]
    out = nc.dram_tensor("out", [TOK, D], F32, kind="ExternalOutput").ap()
    build(nc, *aps, out)
    r = run_bass_kernel_spmd(nc, [arrays], core_ids=[0])
    return r.results[0]["out"].reshape(B, S, D)
```
